# Optimizing a Trainium2 kernel written in Bass

```python
import numpy as np
import jax
import jax.numpy as jnp

def _softmax(x, axis=-1):
    return jax.nn.softmax(x, axis=axis)

def _gelu(x):
    return jax.nn.gelu(x, approximate=True)

def _silu(x):
    return jax.nn.silu(x)

def _sigmoid(x):
    return jax.nn.sigmoid(x)

def _layernorm(x, axis=-1, eps=1e-05):
    m = jnp.mean(x, axis=axis, keepdims=True)
    v = jnp.var(x, axis=axis, keepdims=True)
    return (x - m) / jnp.sqrt(v + eps)

def _scatter_add(tgt, idx, src, axis=0):
    return tgt.at[idx].add(src)

def _segment_sum(src, seg, n):
    return jax.ops.segment_sum(src, seg, n)
kernel_name = 'mk_audio_tower_d4_tok_audfeat256_r4_a73a1d'

def setup_inputs(seed: int=0):
    np.random.seed(seed)
    _w = jnp.asarray

    def _rec_inputs():
        import jax
        import jax.numpy as jnp
        _rk = jax.random.key(seed)
        x = 7.22013e-05 + 1.00017 * jax.random.normal(jax.random.fold_in(_rk, 1), (16, 250, 64), jnp.float32)
        return x
    x = _rec_inputs()

    def _L0_tok_setup():
        import jax, jax.numpy as jnp
        import numpy as np
        WIN = 9
        key = jax.random.key(seed)
        ks = jax.random.split(key, 4)
        N, L, C, U = (8, 1024, 64, 64)
        x = jax.random.normal(ks[0], (N, L, C), dtype=jnp.float32)
        W_qry = jax.random.normal(ks[1], (C, U), dtype=jnp.float32) * 0.05
        W_key = jax.random.normal(ks[2], (C, U), dtype=jnp.float32) * 0.05
        v = jax.random.normal(ks[3], (U,), dtype=jnp.float32) * 0.05
        b = jnp.zeros((U,), dtype=jnp.float32)
        return {'x': x, 'W_qry': W_qry, 'W_key': W_key, 'v': v, 'b': b}
    _L0_tok_all = _L0_tok_setup()
    _L0_tok_in = {k: v for k, v in _L0_tok_all.items() if k in ('W_qry', 'W_key', 'v', 'b')}
    del _L0_tok_all

    def _L0_attn_setup():
        import jax, jax.numpy as jnp
        import numpy as np
        B_, L_, DM = (4, 512, 64)
        DI, DS, DR, DC = (128, 16, 16, 4)

        def _causal_dw_conv(x, w, b):
            k = w.shape[1]
            xp = jnp.pad(x, ((0, 0), (0, 0), (k - 1, 0)))
            L = x.shape[-1]
            y = b[None, :, None]
            for i in range(k):
                y = y + w[None, :, i:i + 1] * xp[:, :, i:i + L]
            return y

        def _selective_scan(u, delta, A, Bm, Cm, Dp, z):
            dA = jnp.exp(jnp.einsum('bdl,dn->lbdn', delta, A))
            dBu = jnp.einsum('bdl,bnl->lbdn', delta * u, Bm)
            Ct = jnp.transpose(Cm, (2, 0, 1))
            h0 = jnp.zeros((u.shape[0], u.shape[1], A.shape[1]), u.dtype)

            def step(h, inps):
                dA_t, dBu_t, C_t = inps
                h = dA_t * h + dBu_t
                return (h, jnp.einsum('bdn,bn->bd', h, C_t))
            _, ys = jax.lax.scan(step, h0, (dA, dBu, Ct))
            y = jnp.transpose(ys, (1, 2, 0))
            return (y + u * Dp[None, :, None]) * jax.nn.silu(z)

        def _mamba_dir(xz, cw, cb, xpw, dtw, dtb, A_log, Dp):
            x, z = jnp.split(xz, 2, axis=1)
            x = jax.nn.silu(_causal_dw_conv(x, cw, cb))
            xdbl = jnp.einsum('bdl,ed->bel', x, xpw)
            dt, Bm, Cm = (xdbl[:, :DR], xdbl[:, DR:DR + DS], xdbl[:, DR + DS:])
            delta = jax.nn.softplus(jnp.einsum('brl,dr->bdl', dt, dtw) + dtb[None, :, None])
            A = -jnp.exp(A_log)
            return _selective_scan(x, delta, A, Bm, Cm, Dp, z)
        key = jax.random.key(seed)
        ks = jax.random.split(key, 14)
        g = lambda i, shape, s: jax.random.normal(ks[i], shape, jnp.float32) * s
        A_log = jnp.log(jnp.tile(jnp.arange(1, DS + 1, dtype=jnp.float32)[None, :], (DI, 1)))
        return {'hidden_states': jax.random.normal(ks[0], (B_, L_, DM), jnp.float32), 'in_proj_w': g(1, (2 * DI, DM), 0.03), 'conv_w': g(2, (DI, DC), 0.3), 'conv_b': jnp.zeros((DI,), jnp.float32), 'x_proj_w': g(3, (DR + 2 * DS, DI), 0.03), 'dt_proj_w': g(4, (DI, DR), 0.25), 'dt_proj_b': jnp.full((DI,), -4.6, jnp.float32), 'A_log': A_log, 'D': jnp.ones((DI,), jnp.float32), 'conv_w_b': g(5, (DI, DC), 0.3), 'conv_b_b': jnp.zeros((DI,), jnp.float32), 'x_proj_w_b': g(6, (DR + 2 * DS, DI), 0.03), 'dt_proj_w_b': g(7, (DI, DR), 0.25), 'dt_proj_b_b': jnp.full((DI,), -4.6, jnp.float32), 'A_b_log': A_log, 'D_b': jnp.ones((DI,), jnp.float32), 'out_proj_w': g(8, (DM, DI), 0.03)}
    _L0_attn_all = _L0_attn_setup()
    _L0_attn_in = {k: v for k, v in _L0_attn_all.items() if k in ('in_proj_w', 'conv_w', 'conv_b', 'x_proj_w', 'dt_proj_w', 'dt_proj_b', 'A_log', 'D', 'conv_w_b', 'conv_b_b', 'x_proj_w_b', 'dt_proj_w_b', 'dt_proj_b_b', 'A_b_log', 'D_b', 'out_proj_w')}
    del _L0_attn_all

    def _L0_ffn_setup():
        import jax, jax.numpy as jnp
        import numpy as np
        B, N, D = (16, 1024, 64)
        NUM_EXPERTS, TOP_K, HEADS = (4, 2, 4)
        N_EDGES = 262144
        LN_EPS = 1e-05

        def _layernorm(x, g, b):
            mu = x.mean(-1, keepdims=True)
            var = ((x - mu) ** 2).mean(-1, keepdims=True)
            return (x - mu) * jax.lax.rsqrt(var + LN_EPS) * g + b

        def _forward(x, edge_index, W_gat, att_src, att_dst, b_gat, ln_gamma, ln_beta, W1, b1, W2, b2):
            Bc, Nc, Dc = x.shape
            M = Bc * Nc
            x_flat = x.reshape(M, Dc)
            h = (x_flat @ W_gat).reshape(M, HEADS, NUM_EXPERTS)
            loops = jnp.arange(M, dtype=edge_index.dtype)
            src = jnp.concatenate([edge_index[0], loops])
            dst = jnp.concatenate([edge_index[1], loops])
            a_src = (h * att_src).sum(-1)
            a_dst = (h * att_dst).sum(-1)
            e = jax.nn.leaky_relu(a_src[src] + a_dst[dst], negative_slope=0.2)
            e_max = jax.ops.segment_max(e, dst, num_segments=M)
            ee = jnp.exp(e - e_max[dst])
            denom = jax.ops.segment_sum(ee, dst, num_segments=M)
            alpha = ee / (denom[dst] + 1e-16)
            msg = h[src] * alpha[:, :, None]
            agg = jax.ops.segment_sum(msg, dst, num_segments=M).reshape(M, HEADS * NUM_EXPERTS) + b_gat
            scores = _layernorm(agg, ln_gamma, ln_beta).reshape(M, HEADS, NUM_EXPERTS).mean(1)
            scores = scores.reshape(Bc, Nc, NUM_EXPERTS)
            topk_s, topk_i = jax.lax.top_k(scores, TOP_K)
            w = jax.nn.softmax(topk_s, axis=-1)
            out = jnp.zeros_like(x)
            for ei in range(NUM_EXPERTS):
                g = jnp.where(topk_i == ei, w, 0.0).sum(-1)
                hh = jax.nn.gelu(x @ W1[ei] + b1[ei], approximate=False)
                out = out + g[..., None] * (hh @ W2[ei] + b2[ei])
            return out
        key = jax.random.key(seed)
        ks = jax.random.split(key, 8)
        s = 0.05
        return {'x': jax.random.normal(ks[0], (B, N, D), jnp.float32), 'W_gat': jax.random.normal(ks[1], (D, HEADS * NUM_EXPERTS), jnp.float32) * s, 'att_src': jax.random.normal(ks[2], (HEADS, NUM_EXPERTS), jnp.float32) * s, 'att_dst': jax.random.normal(ks[3], (HEADS, NUM_EXPERTS), jnp.float32) * s, 'b_gat': jnp.zeros((HEADS * NUM_EXPERTS,), jnp.float32), 'ln_gamma': jnp.ones((HEADS * NUM_EXPERTS,), jnp.float32), 'ln_beta': jnp.zeros((HEADS * NUM_EXPERTS,), jnp.float32), 'W1': jax.random.normal(ks[4], (NUM_EXPERTS, D, 2 * D), jnp.float32) * s, 'b1': jnp.zeros((NUM_EXPERTS, 2 * D), jnp.float32), 'W2': jax.random.normal(ks[5], (NUM_EXPERTS, 2 * D, D), jnp.float32) * s, 'b2': jnp.zeros((NUM_EXPERTS, D), jnp.float32), 'edge_index': jax.random.randint(ks[6], (2, N_EDGES), 0, B * N, jnp.int32)}
    _L0_ffn_all = _L0_ffn_setup()
    _L0_ffn_in = {k: v for k, v in _L0_ffn_all.items() if k in ('W_gat', 'att_src', 'att_dst', 'b_gat', 'ln_gamma', 'ln_beta', 'W1', 'b1', 'W2', 'b2', 'edge_index')}
    del _L0_ffn_all

    def _L1_attn_setup():
        import jax, jax.numpy as jnp
        import numpy as np
        B, T, C = (16, 512, 64)
        TT = T
        LAYER_ID, N_LAYER = (3, 6)
        key = jax.random.key(seed)
        ks = jax.random.split(key, 6)
        ratio_0_to_1 = LAYER_ID / (N_LAYER - 1)
        ratio_1_to_almost0 = 1.0 - LAYER_ID / N_LAYER
        h = np.arange(TT, dtype=np.float32)
        decay_speed = -5.0 + 8.0 * (h / (TT - 1)) ** (0.7 + 1.3 * ratio_0_to_1)
        curve = -(TT - 1 - h)
        time_w = jnp.asarray(np.exp(np.clip(curve * decay_speed, -30.0, 0.0)), dtype=jnp.float32)
        i = np.arange(C, dtype=np.float32) / C
        time_mix_k = jnp.asarray((i ** ratio_1_to_almost0).reshape(1, 1, C), dtype=jnp.float32)
        time_mix_v = jnp.asarray((i ** ratio_1_to_almost0 + 0.3 * ratio_0_to_1).reshape(1, 1, C), dtype=jnp.float32)
        time_mix_r = jnp.asarray((i ** (0.5 * ratio_1_to_almost0)).reshape(1, 1, C), dtype=jnp.float32)
        x = jax.random.normal(ks[0], (B, T, C), dtype=jnp.float32)
        scale = 0.02
        Wk = scale * jax.random.normal(ks[1], (C, C), dtype=jnp.float32)
        Wv = scale * jax.random.normal(ks[2], (C, C), dtype=jnp.float32)
        Wr = scale * jax.random.normal(ks[3], (C, C), dtype=jnp.float32)
        Wo = scale * jax.random.normal(ks[4], (C, C), dtype=jnp.float32)
        return {'x': x, 'time_w': time_w, 'time_mix_k': time_mix_k, 'time_mix_v': time_mix_v, 'time_mix_r': time_mix_r, 'Wk': Wk, 'Wv': Wv, 'Wr': Wr, 'Wo': Wo}
    _L1_attn_all = _L1_attn_setup()
    _L1_attn_in = {k: v for k, v in _L1_attn_all.items() if k in ('time_w', 'time_mix_k', 'time_mix_v', 'time_mix_r', 'Wk', 'Wv', 'Wr', 'Wo')}
    del _L1_attn_all

    def _L1_ffn_setup():
        import jax, jax.numpy as jnp
        import numpy as np
        DIM = 64
        HEADS = 8
        NUM_KEYS = 64
        NUM_KV = NUM_KEYS ** 2
        PK_TOPK = 16
        FINAL_TOPK = 16
        DIM_KEY = DIM // 2
        P = 2

        def _pk(x, Wq_pk, pk_keys):
            b, n, _ = x.shape
            q = (x @ Wq_pk).reshape(b, n, P, HEADS, DIM_KEY).transpose(2, 0, 1, 3, 4)
            sim = jnp.einsum('pbnhd,pkhd->pbnhk', q, pk_keys)
            scores, idx = jax.lax.top_k(sim, PK_TOPK)
            idx0 = idx[0]
            idx1 = idx[1] * NUM_KEYS
            index = (idx0[..., :, None] + idx1[..., None, :]).reshape(b, n, HEADS, PK_TOPK * PK_TOPK)
            score = (scores[0][..., :, None] + scores[1][..., None, :]).reshape(b, n, HEADS, PK_TOPK * PK_TOPK)
            final_scores, pk_idx = jax.lax.top_k(score, FINAL_TOPK)
            final_indices = jnp.take_along_axis(index, pk_idx, axis=-1)
            final_scores = jax.nn.softmax(final_scores, axis=-1)
            return (final_scores, final_indices)
        key = jax.random.key(seed)
        ks = jax.random.split(key, 7)
        b, n = (2, 256)
        std = 0.02
        x = jax.random.normal(ks[0], (b, n, DIM), dtype=jnp.float32)
        Wq_pk = jax.random.normal(ks[1], (DIM, P * HEADS * DIM_KEY), dtype=jnp.float32) * std
        pk_keys = jax.random.normal(ks[2], (P, NUM_KEYS, HEADS, DIM_KEY), dtype=jnp.float32) * std
        Wq = jax.random.normal(ks[3], (DIM, HEADS * DIM), dtype=jnp.float32) * std
        keys_table = jax.random.normal(ks[4], (NUM_KV * HEADS, DIM), dtype=jnp.float32) * std
        values_table = jax.random.normal(ks[5], (NUM_KV * HEADS, DIM), dtype=jnp.float32) * std
        Wo = jax.random.normal(ks[6], (DIM * HEADS, DIM), dtype=jnp.float32) * std
        return {'x': x, 'Wq_pk': Wq_pk, 'pk_keys': pk_keys, 'Wq': Wq, 'keys_table': keys_table, 'values_table': values_table, 'Wo': Wo}
    _L1_ffn_all = _L1_ffn_setup()
    _L1_ffn_in = {k: v for k, v in _L1_ffn_all.items() if k in ('Wq_pk', 'pk_keys', 'Wq', 'keys_table', 'values_table', 'Wo')}
    del _L1_ffn_all

    def _L2_attn_setup():
        import jax, jax.numpy as jnp
        import numpy as np
        B, S, I, H, O = (64, 128, 64, 256, 64)

        def _rnn_layer(inp, W_ih, W_hh, b_ih, b_hh):
            pre = jnp.einsum('bsi,hi->bsh', inp, W_ih) + (b_ih + b_hh)
            h0 = jnp.zeros((inp.shape[0], W_hh.shape[0]), dtype=inp.dtype)

            def step(h, p_t):
                h = jnp.tanh(p_t + h @ W_hh.T)
                return (h, h)
            _, hs = jax.lax.scan(step, h0, jnp.swapaxes(pre, 0, 1))
            return jnp.swapaxes(hs, 0, 1)
        key = jax.random.key(seed)
        ks = jax.random.split(key, 12)
        s_in = 1.0 / np.sqrt(H)
        inp = {'x': jax.random.normal(ks[0], (B, S, I), dtype=jnp.float32), 'W_ih_0': jax.random.uniform(ks[1], (H, I), jnp.float32, -s_in, s_in), 'W_hh_0': jax.random.uniform(ks[2], (H, H), jnp.float32, -s_in, s_in), 'b_ih_0': jax.random.uniform(ks[3], (H,), jnp.float32, -s_in, s_in), 'b_hh_0': jax.random.uniform(ks[4], (H,), jnp.float32, -s_in, s_in), 'W_ih_1': jax.random.uniform(ks[5], (H, H), jnp.float32, -s_in, s_in), 'W_hh_1': jax.random.uniform(ks[6], (H, H), jnp.float32, -s_in, s_in), 'b_ih_1': jax.random.uniform(ks[7], (H,), jnp.float32, -s_in, s_in), 'b_hh_1': jax.random.uniform(ks[8], (H,), jnp.float32, -s_in, s_in), 'fc_w': jax.random.uniform(ks[9], (O, H), jnp.float32, -s_in, s_in), 'fc_b': jax.random.uniform(ks[10], (O,), jnp.float32, -s_in, s_in)}
        return inp
    _L2_attn_all = _L2_attn_setup()
    _L2_attn_in = {k: v for k, v in _L2_attn_all.items() if k in ('W_ih_0', 'W_hh_0', 'b_ih_0', 'b_hh_0', 'W_ih_1', 'W_hh_1', 'b_ih_1', 'b_hh_1', 'fc_w', 'fc_b')}
    del _L2_attn_all

    def _L2_ffn_setup():
        import jax, jax.numpy as jnp
        import numpy as np
        D_MODEL = 64
        EXPERT_DIM = 128
        NUM_EXPERTS = 8
        TOP_K = 2
        SEQ_LEN = 512
        BATCH = 2
        key = jax.random.key(seed)
        ks = jax.random.split(key, 8)
        s = 0.02
        x = jax.random.normal(ks[0], (SEQ_LEN, BATCH, D_MODEL), dtype=jnp.float32)
        Wg = jax.random.normal(ks[1], (D_MODEL, NUM_EXPERTS), dtype=jnp.float32) * s
        bg = jax.random.normal(ks[2], (NUM_EXPERTS,), dtype=jnp.float32) * s
        bias = jnp.zeros((NUM_EXPERTS,), dtype=jnp.float32)
        W1 = jax.random.normal(ks[3], (NUM_EXPERTS, D_MODEL, EXPERT_DIM), dtype=jnp.float32) * s
        b1 = jax.random.normal(ks[4], (NUM_EXPERTS, EXPERT_DIM), dtype=jnp.float32) * s
        W2 = jax.random.normal(ks[5], (NUM_EXPERTS, EXPERT_DIM, D_MODEL), dtype=jnp.float32) * s
        b2 = jax.random.normal(ks[6], (NUM_EXPERTS, D_MODEL), dtype=jnp.float32) * s
        return {'x': x, 'Wg': Wg, 'bg': bg, 'bias': bias, 'W1': W1, 'b1': b1, 'W2': W2, 'b2': b2}
    _L2_ffn_all = _L2_ffn_setup()
    _L2_ffn_in = {k: v for k, v in _L2_ffn_all.items() if k in ('Wg', 'bg', 'bias', 'W1', 'b1', 'W2', 'b2')}
    del _L2_ffn_all

    def _L3_attn_setup():
        import jax, jax.numpy as jnp
        import numpy as np
        B, S, F, H = (4, 256, 64, 8)
        SCALE = float(F) ** 0.5
        key = jax.random.key(seed)
        ks = jax.random.split(key, 5)
        return {'q_input': jax.random.normal(ks[0], (B, S, F), dtype=jnp.float32), 'Wq': jax.random.normal(ks[1], (F, F * H), dtype=jnp.float32) * 0.02, 'Wk': jax.random.normal(ks[2], (F, F * H), dtype=jnp.float32) * 0.02, 'Wv': jax.random.normal(ks[3], (F, F * H), dtype=jnp.float32) * 0.02, 'Wo': jax.random.normal(ks[4], (F * H, F), dtype=jnp.float32) * 0.02}
    _L3_attn_all = _L3_attn_setup()
    _L3_attn_in = {k: v for k, v in _L3_attn_all.items() if k in ('Wq', 'Wk', 'Wv', 'Wo')}
    del _L3_attn_all

    def _L3_ffn_setup():
        import jax, jax.numpy as jnp
        import numpy as np
        TOP_K = 2
        LN_EPS = 1e-05
        key = jax.random.key(seed)
        ks = jax.random.split(key, 8)
        B, S, D, E, H = (16, 256, 64, 8, 256)
        x = jax.random.normal(ks[0], (B, S, D), dtype=jnp.float32)
        Wr = jax.random.normal(ks[1], (D, E), dtype=jnp.float32) * 0.1
        br = jnp.zeros((E,), dtype=jnp.float32)
        ln_g = jnp.ones((E, D), dtype=jnp.float32)
        ln_b = jnp.zeros((E, D), dtype=jnp.float32)
        W1 = jax.random.normal(ks[2], (E, D, H), dtype=jnp.float32) * (1.0 / np.sqrt(D))
        b1 = jnp.zeros((E, H), dtype=jnp.float32)
        W2 = jax.random.normal(ks[3], (E, H, D), dtype=jnp.float32) * (1.0 / np.sqrt(H))
        b2 = jnp.zeros((E, D), dtype=jnp.float32)
        return {'x': x, 'Wr': Wr, 'br': br, 'ln_g': ln_g, 'ln_b': ln_b, 'W1': W1, 'b1': b1, 'W2': W2, 'b2': b2}
    _L3_ffn_all = _L3_ffn_setup()
    _L3_ffn_in = {k: v for k, v in _L3_ffn_all.items() if k in ('Wr', 'br', 'ln_g', 'ln_b', 'W1', 'b1', 'W2', 'b2')}
    del _L3_ffn_all
    return {'x': x, 'L0_tok_W_qry': _L0_tok_in['W_qry'], 'L0_tok_W_key': _L0_tok_in['W_key'], 'L0_tok_v': _L0_tok_in['v'], 'L0_tok_b': _L0_tok_in['b'], 'L0_attn_in_proj_w': _L0_attn_in['in_proj_w'], 'L0_attn_conv_w': _L0_attn_in['conv_w'], 'L0_attn_conv_b': _L0_attn_in['conv_b'], 'L0_attn_x_proj_w': _L0_attn_in['x_proj_w'], 'L0_attn_dt_proj_w': _L0_attn_in['dt_proj_w'], 'L0_attn_dt_proj_b': _L0_attn_in['dt_proj_b'], 'L0_attn_A_log': _L0_attn_in['A_log'], 'L0_attn_D': _L0_attn_in['D'], 'L0_attn_conv_w_b': _L0_attn_in['conv_w_b'], 'L0_attn_conv_b_b': _L0_attn_in['conv_b_b'], 'L0_attn_x_proj_w_b': _L0_attn_in['x_proj_w_b'], 'L0_attn_dt_proj_w_b': _L0_attn_in['dt_proj_w_b'], 'L0_attn_dt_proj_b_b': _L0_attn_in['dt_proj_b_b'], 'L0_attn_A_b_log': _L0_attn_in['A_b_log'], 'L0_attn_D_b': _L0_attn_in['D_b'], 'L0_attn_out_proj_w': _L0_attn_in['out_proj_w'], 'L0_ffn_W_gat': _L0_ffn_in['W_gat'], 'L0_ffn_att_src': _L0_ffn_in['att_src'], 'L0_ffn_att_dst': _L0_ffn_in['att_dst'], 'L0_ffn_b_gat': _L0_ffn_in['b_gat'], 'L0_ffn_ln_gamma': _L0_ffn_in['ln_gamma'], 'L0_ffn_ln_beta': _L0_ffn_in['ln_beta'], 'L0_ffn_W1': _L0_ffn_in['W1'], 'L0_ffn_b1': _L0_ffn_in['b1'], 'L0_ffn_W2': _L0_ffn_in['W2'], 'L0_ffn_b2': _L0_ffn_in['b2'], 'L0_ffn_edge_index': _L0_ffn_in['edge_index'], 'L1_attn_time_w': _L1_attn_in['time_w'], 'L1_attn_time_mix_k': _L1_attn_in['time_mix_k'], 'L1_attn_time_mix_v': _L1_attn_in['time_mix_v'], 'L1_attn_time_mix_r': _L1_attn_in['time_mix_r'], 'L1_attn_Wk': _L1_attn_in['Wk'], 'L1_attn_Wv': _L1_attn_in['Wv'], 'L1_attn_Wr': _L1_attn_in['Wr'], 'L1_attn_Wo': _L1_attn_in['Wo'], 'L1_ffn_Wq_pk': _L1_ffn_in['Wq_pk'], 'L1_ffn_pk_keys': _L1_ffn_in['pk_keys'], 'L1_ffn_Wq': _L1_ffn_in['Wq'], 'L1_ffn_keys_table': _L1_ffn_in['keys_table'], 'L1_ffn_values_table': _L1_ffn_in['values_table'], 'L1_ffn_Wo': _L1_ffn_in['Wo'], 'L2_attn_W_ih_0': _L2_attn_in['W_ih_0'], 'L2_attn_W_hh_0': _L2_attn_in['W_hh_0'], 'L2_attn_b_ih_0': _L2_attn_in['b_ih_0'], 'L2_attn_b_hh_0': _L2_attn_in['b_hh_0'], 'L2_attn_W_ih_1': _L2_attn_in['W_ih_1'], 'L2_attn_W_hh_1': _L2_attn_in['W_hh_1'], 'L2_attn_b_ih_1': _L2_attn_in['b_ih_1'], 'L2_attn_b_hh_1': _L2_attn_in['b_hh_1'], 'L2_attn_fc_w': _L2_attn_in['fc_w'], 'L2_attn_fc_b': _L2_attn_in['fc_b'], 'L2_ffn_Wg': _L2_ffn_in['Wg'], 'L2_ffn_bg': _L2_ffn_in['bg'], 'L2_ffn_bias': _L2_ffn_in['bias'], 'L2_ffn_W1': _L2_ffn_in['W1'], 'L2_ffn_b1': _L2_ffn_in['b1'], 'L2_ffn_W2': _L2_ffn_in['W2'], 'L2_ffn_b2': _L2_ffn_in['b2'], 'L3_attn_Wq': _L3_attn_in['Wq'], 'L3_attn_Wk': _L3_attn_in['Wk'], 'L3_attn_Wv': _L3_attn_in['Wv'], 'L3_attn_Wo': _L3_attn_in['Wo'], 'L3_ffn_Wr': _L3_ffn_in['Wr'], 'L3_ffn_br': _L3_ffn_in['br'], 'L3_ffn_ln_g': _L3_ffn_in['ln_g'], 'L3_ffn_ln_b': _L3_ffn_in['ln_b'], 'L3_ffn_W1': _L3_ffn_in['W1'], 'L3_ffn_b1': _L3_ffn_in['b1'], 'L3_ffn_W2': _L3_ffn_in['W2'], 'L3_ffn_b2': _L3_ffn_in['b2']}

def reference(x, L0_tok_W_qry, L0_tok_W_key, L0_tok_v, L0_tok_b, L0_attn_in_proj_w, L0_attn_conv_w, L0_attn_conv_b, L0_attn_x_proj_w, L0_attn_dt_proj_w, L0_attn_dt_proj_b, L0_attn_A_log, L0_attn_D, L0_attn_conv_w_b, L0_attn_conv_b_b, L0_attn_x_proj_w_b, L0_attn_dt_proj_w_b, L0_attn_dt_proj_b_b, L0_attn_A_b_log, L0_attn_D_b, L0_attn_out_proj_w, L0_ffn_W_gat, L0_ffn_att_src, L0_ffn_att_dst, L0_ffn_b_gat, L0_ffn_ln_gamma, L0_ffn_ln_beta, L0_ffn_W1, L0_ffn_b1, L0_ffn_W2, L0_ffn_b2, L0_ffn_edge_index, L1_attn_time_w, L1_attn_time_mix_k, L1_attn_time_mix_v, L1_attn_time_mix_r, L1_attn_Wk, L1_attn_Wv, L1_attn_Wr, L1_attn_Wo, L1_ffn_Wq_pk, L1_ffn_pk_keys, L1_ffn_Wq, L1_ffn_keys_table, L1_ffn_values_table, L1_ffn_Wo, L2_attn_W_ih_0, L2_attn_W_hh_0, L2_attn_b_ih_0, L2_attn_b_hh_0, L2_attn_W_ih_1, L2_attn_W_hh_1, L2_attn_b_ih_1, L2_attn_b_hh_1, L2_attn_fc_w, L2_attn_fc_b, L2_ffn_Wg, L2_ffn_bg, L2_ffn_bias, L2_ffn_W1, L2_ffn_b1, L2_ffn_W2, L2_ffn_b2, L3_attn_Wq, L3_attn_Wk, L3_attn_Wv, L3_attn_Wo, L3_ffn_Wr, L3_ffn_br, L3_ffn_ln_g, L3_ffn_ln_b, L3_ffn_W1, L3_ffn_b1, L3_ffn_W2, L3_ffn_b2):
    import jax
    import jax.numpy as jnp

    def _L0_tok_ref(x, W_qry, W_key, v, b):
        import jax, jax.numpy as jnp
        import numpy as np
        WIN = 9
        N, L, C = x.shape
        n_w = L - WIN + 1
        idx = jnp.arange(n_w)[:, None] + jnp.arange(WIN)[None, :]
        x_win = x[:, idx]
        x_ctr = x[:, WIN // 2:WIN // 2 + n_w]
        key = jnp.einsum('nwsc,cu->nwsu', x_win, W_key)
        qry = jnp.einsum('nwc,cu->nwu', x_ctr, W_qry)
        score = jnp.einsum('nwsu,u->nws', jnp.tanh(qry[:, :, None, :] + key + b), v)
        weight = jax.nn.softmax(score, axis=2)
        out = jnp.einsum('nwsc,nws->nwc', x_win, weight)
        return out

    def _L0_attn_ref(hidden_states, in_proj_w, conv_w, conv_b, x_proj_w, dt_proj_w, dt_proj_b, A_log, D, conv_w_b, conv_b_b, x_proj_w_b, dt_proj_w_b, dt_proj_b_b, A_b_log, D_b, out_proj_w):
        import jax, jax.numpy as jnp
        import numpy as np
        B_, L_, DM = (4, 512, 64)
        DI, DS, DR, DC = (128, 16, 16, 4)

        def _causal_dw_conv(x, w, b):
            k = w.shape[1]
            xp = jnp.pad(x, ((0, 0), (0, 0), (k - 1, 0)))
            L = x.shape[-1]
            y = b[None, :, None]
            for i in range(k):
                y = y + w[None, :, i:i + 1] * xp[:, :, i:i + L]
            return y

        def _selective_scan(u, delta, A, Bm, Cm, Dp, z):
            dA = jnp.exp(jnp.einsum('bdl,dn->lbdn', delta, A))
            dBu = jnp.einsum('bdl,bnl->lbdn', delta * u, Bm)
            Ct = jnp.transpose(Cm, (2, 0, 1))
            h0 = jnp.zeros((u.shape[0], u.shape[1], A.shape[1]), u.dtype)

            def step(h, inps):
                dA_t, dBu_t, C_t = inps
                h = dA_t * h + dBu_t
                return (h, jnp.einsum('bdn,bn->bd', h, C_t))
            _, ys = jax.lax.scan(step, h0, (dA, dBu, Ct))
            y = jnp.transpose(ys, (1, 2, 0))
            return (y + u * Dp[None, :, None]) * jax.nn.silu(z)

        def _mamba_dir(xz, cw, cb, xpw, dtw, dtb, A_log, Dp):
            x, z = jnp.split(xz, 2, axis=1)
            x = jax.nn.silu(_causal_dw_conv(x, cw, cb))
            xdbl = jnp.einsum('bdl,ed->bel', x, xpw)
            dt, Bm, Cm = (xdbl[:, :DR], xdbl[:, DR:DR + DS], xdbl[:, DR + DS:])
            delta = jax.nn.softplus(jnp.einsum('brl,dr->bdl', dt, dtw) + dtb[None, :, None])
            A = -jnp.exp(A_log)
            return _selective_scan(x, delta, A, Bm, Cm, Dp, z)
        xz = jnp.einsum('bld,ed->bel', hidden_states, in_proj_w)
        y_f = _mamba_dir(xz, conv_w, conv_b, x_proj_w, dt_proj_w, dt_proj_b, A_log, D)
        y_b = _mamba_dir(xz[..., ::-1], conv_w_b, conv_b_b, x_proj_w_b, dt_proj_w_b, dt_proj_b_b, A_b_log, D_b)[..., ::-1]
        y = y_f + y_b
        return jnp.einsum('bdl,od->blo', y, out_proj_w)

    def _L0_ffn_ref(x, W_gat, att_src, att_dst, b_gat, ln_gamma, ln_beta, W1, b1, W2, b2, edge_index):
        import jax, jax.numpy as jnp
        import numpy as np
        B, N, D = (16, 1024, 64)
        NUM_EXPERTS, TOP_K, HEADS = (4, 2, 4)
        N_EDGES = 262144
        LN_EPS = 1e-05

        def _layernorm(x, g, b):
            mu = x.mean(-1, keepdims=True)
            var = ((x - mu) ** 2).mean(-1, keepdims=True)
            return (x - mu) * jax.lax.rsqrt(var + LN_EPS) * g + b

        def _forward(x, edge_index, W_gat, att_src, att_dst, b_gat, ln_gamma, ln_beta, W1, b1, W2, b2):
            Bc, Nc, Dc = x.shape
            M = Bc * Nc
            x_flat = x.reshape(M, Dc)
            h = (x_flat @ W_gat).reshape(M, HEADS, NUM_EXPERTS)
            loops = jnp.arange(M, dtype=edge_index.dtype)
            src = jnp.concatenate([edge_index[0], loops])
            dst = jnp.concatenate([edge_index[1], loops])
            a_src = (h * att_src).sum(-1)
            a_dst = (h * att_dst).sum(-1)
            e = jax.nn.leaky_relu(a_src[src] + a_dst[dst], negative_slope=0.2)
            e_max = jax.ops.segment_max(e, dst, num_segments=M)
            ee = jnp.exp(e - e_max[dst])
            denom = jax.ops.segment_sum(ee, dst, num_segments=M)
            alpha = ee / (denom[dst] + 1e-16)
            msg = h[src] * alpha[:, :, None]
            agg = jax.ops.segment_sum(msg, dst, num_segments=M).reshape(M, HEADS * NUM_EXPERTS) + b_gat
            scores = _layernorm(agg, ln_gamma, ln_beta).reshape(M, HEADS, NUM_EXPERTS).mean(1)
            scores = scores.reshape(Bc, Nc, NUM_EXPERTS)
            topk_s, topk_i = jax.lax.top_k(scores, TOP_K)
            w = jax.nn.softmax(topk_s, axis=-1)
            out = jnp.zeros_like(x)
            for ei in range(NUM_EXPERTS):
                g = jnp.where(topk_i == ei, w, 0.0).sum(-1)
                hh = jax.nn.gelu(x @ W1[ei] + b1[ei], approximate=False)
                out = out + g[..., None] * (hh @ W2[ei] + b2[ei])
            return out
        return _forward(x, edge_index, W_gat, att_src, att_dst, b_gat, ln_gamma, ln_beta, W1, b1, W2, b2)

    def _L1_attn_ref(x, time_w, time_mix_k, time_mix_v, time_mix_r, Wk, Wv, Wr, Wo):
        import jax, jax.numpy as jnp
        import numpy as np
        B, T, C = (16, 512, 64)
        TT = T
        LAYER_ID, N_LAYER = (3, 6)
        Bx, Tx, Cx = x.shape
        maxlen = time_w.shape[0]
        xx = jnp.pad(x, ((0, 0), (1, 0), (0, 0)))[:, :-1]
        xk = x * time_mix_k + xx * (1.0 - time_mix_k)
        xv = x * time_mix_v + xx * (1.0 - time_mix_v)
        xr = x * time_mix_r + xx * (1.0 - time_mix_r)
        k = jnp.exp(jnp.clip(xk @ Wk, -60.0, 30.0))
        v = xv @ Wv
        r = xr @ Wr
        sum_k = jnp.cumsum(k, axis=1)
        kv = k * v
        t_idx = jnp.arange(Tx)
        d = t_idx[:, None] - t_idx[None, :]
        W = jnp.where(d >= 0, time_w[jnp.clip(maxlen - 1 - d, 0, maxlen - 1)], 0.0)
        wkv = jnp.einsum('tu,buc->btc', W, kv)
        rwkv = jax.nn.sigmoid(r) * wkv / sum_k
        return rwkv @ Wo

    def _L1_ffn_ref(x, Wq_pk, pk_keys, Wq, keys_table, values_table, Wo):
        import jax, jax.numpy as jnp
        import numpy as np
        DIM = 64
        HEADS = 8
        NUM_KEYS = 64
        NUM_KV = NUM_KEYS ** 2
        PK_TOPK = 16
        FINAL_TOPK = 16
        DIM_KEY = DIM // 2
        P = 2

        def _pk(x, Wq_pk, pk_keys):
            b, n, _ = x.shape
            q = (x @ Wq_pk).reshape(b, n, P, HEADS, DIM_KEY).transpose(2, 0, 1, 3, 4)
            sim = jnp.einsum('pbnhd,pkhd->pbnhk', q, pk_keys)
            scores, idx = jax.lax.top_k(sim, PK_TOPK)
            idx0 = idx[0]
            idx1 = idx[1] * NUM_KEYS
            index = (idx0[..., :, None] + idx1[..., None, :]).reshape(b, n, HEADS, PK_TOPK * PK_TOPK)
            score = (scores[0][..., :, None] + scores[1][..., None, :]).reshape(b, n, HEADS, PK_TOPK * PK_TOPK)
            final_scores, pk_idx = jax.lax.top_k(score, FINAL_TOPK)
            final_indices = jnp.take_along_axis(index, pk_idx, axis=-1)
            final_scores = jax.nn.softmax(final_scores, axis=-1)
            return (final_scores, final_indices)
        b, n, d = x.shape
        q = (x @ Wq).reshape(b, n, HEADS, DIM) * DIM ** (-0.5)
        kv_scores, indices = _pk(x, Wq_pk, pk_keys)
        offsets = jnp.arange(HEADS, dtype=indices.dtype) * NUM_KV
        ind = indices + offsets[None, None, :, None]
        k = jnp.einsum('bnhk,bnhkd->bnhd', kv_scores, keys_table[ind])
        v = jnp.einsum('bnhk,bnhkd->bnhd', kv_scores, values_table[ind])
        sim = jnp.einsum('bihd,bjhd->bhij', q, k)
        neg = -jnp.finfo(sim.dtype).max
        causal = jnp.tril(jnp.ones((n, n), dtype=bool))
        sim = jnp.where(causal, sim, neg)
        attn = jax.nn.softmax(sim, axis=-1)
        out = jnp.einsum('bhij,bjhd->bhid', attn, v)
        out = out.transpose(0, 2, 1, 3).reshape(b, n, HEADS * DIM)
        return out @ Wo

    def _L2_attn_ref(x, W_ih_0, W_hh_0, b_ih_0, b_hh_0, W_ih_1, W_hh_1, b_ih_1, b_hh_1, fc_w, fc_b):
        import jax, jax.numpy as jnp
        import numpy as np
        B, S, I, H, O = (64, 128, 64, 256, 64)

        def _rnn_layer(inp, W_ih, W_hh, b_ih, b_hh):
            pre = jnp.einsum('bsi,hi->bsh', inp, W_ih) + (b_ih + b_hh)
            h0 = jnp.zeros((inp.shape[0], W_hh.shape[0]), dtype=inp.dtype)

            def step(h, p_t):
                h = jnp.tanh(p_t + h @ W_hh.T)
                return (h, h)
            _, hs = jax.lax.scan(step, h0, jnp.swapaxes(pre, 0, 1))
            return jnp.swapaxes(hs, 0, 1)
        h = _rnn_layer(x, W_ih_0, W_hh_0, b_ih_0, b_hh_0)
        h = _rnn_layer(h, W_ih_1, W_hh_1, b_ih_1, b_hh_1)
        return h @ fc_w.T + fc_b

    def _L2_ffn_ref(x, Wg, bg, bias, W1, b1, W2, b2):
        import jax, jax.numpy as jnp
        import numpy as np
        D_MODEL = 64
        EXPERT_DIM = 128
        NUM_EXPERTS = 8
        TOP_K = 2
        SEQ_LEN = 512
        BATCH = 2
        x_flat = x.reshape(-1, D_MODEL)
        gate_logits = x_flat @ Wg + bg + bias
        topk_vals, topk_idx = jax.lax.top_k(gate_logits, TOP_K)
        topk_w = jax.nn.softmax(topk_vals, axis=-1)
        combine = (jax.nn.one_hot(topk_idx, NUM_EXPERTS, dtype=x.dtype) * topk_w[..., None]).sum(axis=1)
        h = jax.nn.relu(jnp.einsum('td,edh->teh', x_flat, W1) + b1)
        y = jnp.einsum('teh,ehd->ted', h, W2) + b2
        out = jnp.einsum('ted,te->td', y, combine)
        return out.reshape(x.shape)

    def _L3_attn_ref(q_input, Wq, Wk, Wv, Wo):
        import jax, jax.numpy as jnp
        import numpy as np
        B, S, F, H = (4, 256, 64, 8)
        SCALE = float(F) ** 0.5
        b, s, f = q_input.shape
        h = Wq.shape[1] // f
        q = (q_input.reshape(b * s, f) @ Wq).reshape(b, s, f, h)
        k = (q_input.reshape(b * s, f) @ Wk).reshape(b, s, f, h)
        v = (q_input.reshape(b * s, f) @ Wv).reshape(b, s, f, h)
        qkt = jnp.einsum('bifh,bjfh->bijh', q, k)
        attn = jax.nn.sigmoid(qkt * SCALE)
        wv = jnp.einsum('bijh,bjfh->bifh', attn, v)
        wv = wv.reshape(b * s, f * h)
        out = jax.nn.relu(wv @ Wo)
        return out.reshape(b, s, f)

    def _L3_ffn_ref(x, Wr, br, ln_g, ln_b, W1, b1, W2, b2):
        import jax, jax.numpy as jnp
        import numpy as np
        TOP_K = 2
        LN_EPS = 1e-05
        B, S, D = x.shape
        N = B * S
        xt = x.reshape(N, D)
        logits = xt @ Wr + br
        probs = jax.nn.softmax(logits, axis=-1)
        top_p, top_idx = jax.lax.top_k(probs, TOP_K)
        weights = top_p / top_p.sum(axis=-1, keepdims=True)
        mu = xt.mean(axis=-1, keepdims=True)
        var = ((xt - mu) ** 2).mean(axis=-1, keepdims=True)
        xn = (xt - mu) * jax.lax.rsqrt(var + LN_EPS)
        xe = xn[None, :, :] * ln_g[:, None, :] + ln_b[:, None, :]
        h = jax.nn.gelu(jnp.einsum('end,edh->enh', xe, W1) + b1[:, None, :], approximate=False)
        y = jnp.einsum('enh,ehd->end', h, W2) + b2[:, None, :]
        y_tok = jnp.transpose(y, (1, 0, 2))
        sel = jnp.take_along_axis(y_tok, top_idx[:, :, None], axis=1)
        out = (weights[:, :, None] * sel).sum(axis=1)
        return out.reshape(B, S, D)
    h = _L0_tok_ref(x, L0_tok_W_qry, L0_tok_W_key, L0_tok_v, L0_tok_b)
    h = h + _L0_attn_ref(_layernorm(h, axis=-1), L0_attn_in_proj_w, L0_attn_conv_w, L0_attn_conv_b, L0_attn_x_proj_w, L0_attn_dt_proj_w, L0_attn_dt_proj_b, L0_attn_A_log, L0_attn_D, L0_attn_conv_w_b, L0_attn_conv_b_b, L0_attn_x_proj_w_b, L0_attn_dt_proj_w_b, L0_attn_dt_proj_b_b, L0_attn_A_b_log, L0_attn_D_b, L0_attn_out_proj_w)
    h = h + _L0_ffn_ref(_layernorm(h, axis=-1), L0_ffn_W_gat, L0_ffn_att_src, L0_ffn_att_dst, L0_ffn_b_gat, L0_ffn_ln_gamma, L0_ffn_ln_beta, L0_ffn_W1, L0_ffn_b1, L0_ffn_W2, L0_ffn_b2, L0_ffn_edge_index)
    h = h + _L1_attn_ref(_layernorm(h, axis=-1), L1_attn_time_w, L1_attn_time_mix_k, L1_attn_time_mix_v, L1_attn_time_mix_r, L1_attn_Wk, L1_attn_Wv, L1_attn_Wr, L1_attn_Wo)
    h = h + _L1_ffn_ref(_layernorm(h, axis=-1), L1_ffn_Wq_pk, L1_ffn_pk_keys, L1_ffn_Wq, L1_ffn_keys_table, L1_ffn_values_table, L1_ffn_Wo)
    h = h + _L2_attn_ref(_layernorm(h, axis=-1), L2_attn_W_ih_0, L2_attn_W_hh_0, L2_attn_b_ih_0, L2_attn_b_hh_0, L2_attn_W_ih_1, L2_attn_W_hh_1, L2_attn_b_ih_1, L2_attn_b_hh_1, L2_attn_fc_w, L2_attn_fc_b)
    h = h + _L2_ffn_ref(_layernorm(h, axis=-1), L2_ffn_Wg, L2_ffn_bg, L2_ffn_bias, L2_ffn_W1, L2_ffn_b1, L2_ffn_W2, L2_ffn_b2)
    h = h + _L3_attn_ref(_layernorm(h, axis=-1), L3_attn_Wq, L3_attn_Wk, L3_attn_Wv, L3_attn_Wo)
    h = h + _L3_ffn_ref(_layernorm(h, axis=-1), L3_ffn_Wr, L3_ffn_br, L3_ffn_ln_g, L3_ffn_ln_b, L3_ffn_W1, L3_ffn_b1, L3_ffn_W2, L3_ffn_b2)
    return h

_drawn_inputs = setup_inputs


def setup_inputs(seed=0):
    import zlib

    import numpy as np

    out = dict(_drawn_inputs(seed))
    spreads = {'L0_tok_b': (0.0, 0.423),
     'L0_attn_conv_b': (0.0, 0.366),
     'L0_attn_dt_proj_b': (-4.599999904632568, 0.6),
     'L0_attn_D': (1.0, 0.6),
     'L0_attn_conv_b_b': (0.0, 0.352),
     'L0_attn_dt_proj_b_b': (-4.599999904632568, 0.6),
     'L0_attn_D_b': (1.0, 0.6),
     'L0_ffn_b_gat': (0.0, 0.1),
     'L0_ffn_ln_gamma': (1.0, 0.2),
     'L0_ffn_ln_beta': (0.0, 0.1),
     'L0_ffn_b1': (0.0, 0.1),
     'L0_ffn_b2': (0.0, 0.1),
     'L2_ffn_bias': (0.0, 0.1),
     'L3_ffn_br': (0.0, 0.1),
     'L3_ffn_ln_g': (1.0, 0.2),
     'L3_ffn_ln_b': (0.0, 0.342),
     'L3_ffn_b1': (0.0, 0.37),
     'L3_ffn_b2': (0.0, 0.283)}
    factors = {'L0_attn_conv_w': 2.771,
     'L0_attn_x_proj_w': 8.0,
     'L0_attn_dt_proj_w': 8.0,
     'L0_attn_A_log': 8.0,
     'L0_attn_conv_w_b': 2.693,
     'L0_attn_x_proj_w_b': 8.0,
     'L0_attn_dt_proj_w_b': 8.0,
     'L0_attn_A_b_log': 8.0,
     'L0_ffn_att_src': 3.925,
     'L0_ffn_att_dst': 5.499,
     'L1_attn_time_mix_k': 8.0,
     'L1_attn_time_mix_v': 8.0,
     'L1_attn_time_mix_r': 8.0,
     'L1_attn_Wk': 8.0,
     'L1_attn_Wv': 3.405,
     'L1_attn_Wr': 8.0,
     'L1_attn_Wo': 3.144,
     'L1_ffn_Wq_pk': 4.93,
     'L1_ffn_pk_keys': 5.249,
     'L1_ffn_Wq': 64.0,
     'L1_ffn_keys_table': 64.0,
     'L1_ffn_values_table': 4.206,
     'L1_ffn_Wo': 4.989,
     'L2_ffn_bg': 2.749,
     'L2_ffn_b1': 3.385}
    for name, (base, spread) in spreads.items():
        noise = np.random.default_rng([zlib.crc32(name.encode()), seed]).standard_normal(out[name].shape)
        drawn = base * np.exp(spread * noise) if base else spread * noise
        out[name] = jnp.asarray(drawn.astype(out[name].dtype))
    for name, factor in factors.items():
        out[name] = (out[name] * factor).astype(out[name].dtype)
    return out
```

```python
from contextlib import ExitStack

import concourse.bass as bass
from concourse import mybir

F32 = mybir.dt.float32
BF16 = mybir.dt.bfloat16
I32 = mybir.dt.int32
U32 = mybir.dt.uint32
ALU = mybir.AluOpType
ACT = mybir.ActivationFunctionType
AX = mybir.AxisListType
RMAX = bass.bass_isa.ReduceOp.max

P = 128
B = 16
T_IN = 250
WIN = 9
T = T_IN - WIN + 1
C = 64
N = B * T
TP = T // 2
NT = N // TP
GT = 4
NG = NT // GT
GC = GT * TP
BANK = 512
EPS = 1e-5


class Stage:

    def __init__(self, nc, name):
        self.nc, self.name, self.ctx = nc, name, ExitStack()

    def __enter__(self):
        self.ctx.__enter__()
        return self

    def __exit__(self, *e):
        return self.ctx.__exit__(*e)

    def sb(self, name, shape, dt=F32):
        return self.ctx.enter_context(self.nc.sbuf_tensor(f"{self.name}_{name}", shape, dt))

    def ps(self, name, shape, dt=F32):
        return self.ctx.enter_context(self.nc.psum_tensor(f"{self.name}_{name}", shape, dt))

    def sem(self, name):
        return self.nc.alloc_semaphore(f"{self.name}_{name}")

    def block(self):
        return self.ctx.enter_context(self.nc.Block())


class Steps:

    def __init__(self, eng, sem, base=0):
        self.eng, self.sem, self.base, self.n = eng, sem, base, 0

    def done(self, ins):
        self.n += 1
        ins.then_inc(self.sem, 1)

    def then(self, ins):
        self.done(ins)
        self.eng.wait_ge(self.sem, self.base + self.n)


def bc(ap, shape):
    return ap.to_broadcast(shape)


def pool_windows(nc, g, A):
    HB = B // 2
    COLS = HB * T
    with Stage(nc, "pw") as s:
        wq, wk, vv = (s.sb(n, [P, P]) for n in ("wq", "wk", "vv"))
        bias, vcol = s.sb("bias", [P, 1]), s.sb("vcol", [P, 1])
        xT = s.sb("xT", [P, HB, T_IN])
        q, k = s.sb("q", [P, HB, T_IN]), s.sb("k", [P, HB, T_IN])
        score = s.sb("score", [P, WIN, HB, T])
        work = s.sb("work", [P, 2, HB, T])
        top, den, num = (s.sb(n, [P, HB, T]) for n in ("top", "den", "num"))
        proj = s.ps("proj", [P, 8, BANK])
        loads, projected, copied = s.sem("loads"), s.sem("projected"), s.sem("copied")
        summed, squashed, scored, kept = s.sem("summed"), s.sem("squashed"), s.sem("scored"), s.sem("kept")
        shifted, raised, done, steps_v = s.sem("shifted"), s.sem("raised"), s.sem("done"), s.sem("steps_v")
        turned, steps_z, v_ready = s.sem("turned"), s.sem("steps_z"), s.sem("v_ready")
        block = s.block()

        @block.sync
        def _(sp):
            sp.wait_ge(steps_z, 3)
            sp.dma_start(xT[:], A["xT"]).then_inc(loads, 16)
            for half in range(2):
                r = slice(C * half, C * half + C)
                sp.dma_start(wq[r, r], A["L0_tok_W_qry"]).then_inc(loads, 16)
                sp.dma_start(wk[r, r], A["L0_tok_W_key"]).then_inc(loads, 16)
                sp.dma_start(vcol[r, :], A["L0_tok_v"].unsqueeze(1)).then_inc(loads, 16)
                sp.dma_start(bias[r, :], A["L0_tok_b"].unsqueeze(1)).then_inc(loads, 16)

        @block.tensor
        def _(pe):
            pe.wait_ge(loads, 16 * 9)
            for n, w in enumerate((wq, wk)):
                for c in range(4):
                    nc.tensor.matmul(proj[:, 4 * n + c, 0:2 * T_IN], w[:], xT[:, 2 * c:2 * c + 2, :],
                                     start=True, stop=True).then_inc(projected, 1)
            pe.wait_ge(v_ready, 2)
            for w in range(WIN):
                pe.wait_ge(squashed, w + 1)
                if w < 2:
                    pe.wait_ge(copied, w + 1)
                else:
                    pe.wait_ge(kept, w - 1)
                for c in range(4):
                    ins = nc.tensor.matmul(proj[:, 4 * (w % 2) + c, 0:2 * T], vv[:],
                                           work[:, w % 2, 2 * c:2 * c + 2, :], start=True, stop=True)
                ins.then_inc(scored, 1)
            pe.wait_ge(done, 1)
            pe.wait_ge(kept, WIN)
            for t in range(HB * 2):
                b, half = divmod(t, 2)
                ins = nc.tensor.transpose(proj[0:TP, t // 4, P * (t % 4):P * (t % 4) + P],
                                          num[:, b, TP * half:TP * half + TP], g.ident[:])
                if t % 4 == 3:
                    ins.then_inc(turned, 1)

        @block.scalar
        def _(act):
            for n, dst in enumerate((q, k)):
                act.wait_ge(projected, 4 * n + 4)
                nc.scalar.copy(dst[:].rearrange("p (c b) t -> p c (b t)", c=4),
                               proj[:, 4 * n:4 * n + 4, 0:2 * T_IN]).then_inc(copied, 1)
            for w in range(WIN):
                act.wait_ge(summed, w + 1)
                nc.scalar.activation(work[:, w % 2], work[:, w % 2], ACT.Tanh, bias=bias[:]).then_inc(squashed, 1)
                act.wait_ge(scored, w + 1)
                nc.scalar.copy(score[:, w].rearrange("p (c b) t -> p c (b t)", c=4),
                               proj[:, 4 * (w % 2):4 * (w % 2) + 4, 0:2 * T]).then_inc(kept, 1)
            for w in range(WIN):
                act.wait_ge(shifted, w + 1)
                nc.scalar.activation(score[:, w], score[:, w], ACT.Exp).then_inc(raised, 1)
            for bank in range(4):
                act.wait_ge(turned, bank + 1)
                for half in range(2):
                    dst = g.h[:, 32 // 2 * half + 4 * bank:32 // 2 * half + 4 * bank + 4, :]
                    src = proj[0:TP, bank, :].rearrange("p (t h c) -> p t h c", t=4, h=2)[:, :, half, :]
                    nc.scalar.copy(dst, src)

        @block.vector
        def _(dve):
            st = Steps(dve, steps_v)
            for z in (wq, wk, vv):
                nc.vector.memset(z[:], 0.0).then_inc(steps_z, 1)
            dve.wait_ge(loads, 16 * 9)
            dve.wait_ge(steps_z, 3)
            for half in range(2):
                r = slice(C * half, C * half + C)
                nc.vector.tensor_copy(vv[r, r], bc(vcol[r, :], [C, C])).then_inc(v_ready, 1)
            dve.wait_ge(copied, 2)
            for w in range(WIN):
                if w >= 2:
                    dve.wait_ge(scored, w - 1)
                nc.vector.tensor_tensor(work[:, w % 2], q[:, :, WIN // 2:WIN // 2 + T], k[:, :, w:w + T],
                                        ALU.add).then_inc(summed, 1)
            dve.wait_ge(kept, 2)
            st.then(nc.vector.tensor_tensor(top[:], score[:, 0], score[:, 1], ALU.max))
            for w in range(2, WIN):
                dve.wait_ge(kept, w + 1)
                st.then(nc.vector.tensor_tensor(top[:], top[:], score[:, w], ALU.max))
            for w in range(WIN):
                nc.vector.tensor_tensor(score[:, w], score[:, w], top[:], ALU.subtract).then_inc(shifted, 1)
            dve.wait_ge(raised, 2)
            st.done(nc.vector.tensor_tensor(den[:], score[:, 0], score[:, 1], ALU.add))
            st.then(nc.vector.tensor_tensor(num[:], score[:, 0], xT[:, :, 0:T], ALU.mult))
            for w in range(1, WIN):
                dve.wait_ge(raised, w + 1)
                st.then(nc.vector.tensor_tensor(work[:, 0], score[:, w], xT[:, :, w:w + T], ALU.mult))
                st.done(nc.vector.tensor_tensor(num[:], num[:], work[:, 0], ALU.add))
                if w >= 2:
                    st.done(nc.vector.tensor_tensor(den[:], den[:], score[:, w], ALU.add))
                dve.wait_ge(steps_v, st.n)
            st.then(nc.vector.reciprocal(den[:], den[:]))
            nc.vector.tensor_tensor(num[:], num[:], den[:], ALU.mult).then_inc(done, 1)


def normalise(nc, g, name, src=None, kept=None):
    with Stage(nc, name) as s:
        src = g.h if src is None else src
        xc = s.sb("xc", [TP, NT, C]) if kept is None else kept
        sq = s.sb("sq", [TP, NT, C])
        mean, var = s.sb("mean", [TP, NT]), s.sb("var", [TP, NT])
        banks = s.ps("banks", [C, 8, BANK])
        steps, var_ready, root_ready = s.sem("steps"), s.sem("var_ready"), s.sem("root_ready")
        ready, turned = s.sem("ready"), s.sem("turned")
        block = s.block()

        @block.vector
        def _(dve):
            st = Steps(dve, steps)
            wide = [TP, NT, C]
            st.then(nc.vector.tensor_reduce(mean[:], src[:], AX.X, ALU.add))
            st.then(nc.vector.tensor_scalar(mean[:], mean[:], 1.0 / C, None, ALU.mult))
            st.then(nc.vector.tensor_tensor(xc[:], src[:], bc(mean[:].unsqueeze(2), wide), ALU.subtract))
            st.then(nc.vector.tensor_tensor(sq[:], xc[:], xc[:], ALU.mult))
            st.then(nc.vector.tensor_reduce(var[:], sq[:], AX.X, ALU.add))
            nc.vector.tensor_scalar(var[:], var[:], 1.0 / C, EPS, ALU.mult, ALU.add).then_inc(var_ready, 1)
            dve.wait_ge(root_ready, 1)
            st.then(nc.vector.reciprocal(mean[:], var[:]))
            nc.vector.tensor_tensor(xc[:], xc[:], bc(mean[:].unsqueeze(2), wide), ALU.mult).then_inc(ready, 1)

        @block.scalar
        def _(act):
            act.wait_ge(var_ready, 1)
            nc.scalar.activation(var[:], var[:], ACT.Sqrt).then_inc(root_ready, 1)
            for n in range(NG):
                act.wait_ge(turned, n + 1)
                nc.scalar.copy(g.xT[0:C, GC * n:GC * n + GC], banks[:, n, 0:GC])

        @block.tensor
        def _(pe):
            pe.wait_ge(ready, 1)
            for j in range(NT):
                ins = nc.tensor.transpose(banks[:, j // GT, TP * (j % GT):TP * (j % GT) + TP], xc[:, j, :],
                                          g.ident[0:TP, 0:TP])
                if j % GT == GT - 1:
                    ins.then_inc(turned, 1)


def choose_two(nc, s, dve, act_in, act_out, st, logits, gate, experts):
    shape = [TP, NT, experts]
    order, eq = s.sb("order", [TP, experts]), s.sb("eq", shape)
    first, second, left = s.sb("first", shape), s.sb("second", shape), s.sb("left", shape)
    best, at, diff = s.sb("two", [TP, 2, NT]), s.sb("at", [TP, NT]), s.sb("diff", [TP, NT])
    share = s.sb("share", [TP, 2, NT])

    def wide(x):
        return bc(x.unsqueeze(2), shape)

    def dve_part():
        for e in range(experts):
            st.done(nc.vector.memset(order[:, e:e + 1], float(experts - e)))
        for n, (src, chosen) in enumerate(((logits, first), (left, second))):
            st.then(nc.vector.tensor_reduce(best[:, n], src[:], AX.X, ALU.max))
            st.then(nc.vector.tensor_tensor(eq[:], src[:], wide(best[:, n]), ALU.is_equal))
            st.then(nc.vector.tensor_tensor(eq[:], eq[:], bc(order[:].unsqueeze(1), shape), ALU.mult))
            st.then(nc.vector.tensor_reduce(at[:], eq[:], AX.X, ALU.max))
            st.then(nc.vector.tensor_tensor(chosen[:], eq[:], wide(at[:]), ALU.is_equal))
            if n == 0:
                st.then(nc.vector.scalar_tensor_tensor(out=left[:], in0=first[:], scalar=-3e38, in1=logits[:],
                                                       op0=ALU.mult, op1=ALU.add))
        nc.vector.tensor_tensor(diff[:], best[:, 1], best[:, 0], ALU.subtract).then_inc(act_in, 1)
        dve.wait_ge(act_out, 1)
        st.then(nc.vector.tensor_scalar(share[:, 0], diff[:], 1.0, None, ALU.add))
        st.then(nc.vector.reciprocal(share[:, 0], share[:, 0]))
        st.then(nc.vector.tensor_tensor(share[:, 1], share[:, 0], diff[:], ALU.mult))
        st.done(nc.vector.tensor_tensor(first[:], first[:], wide(share[:, 0]), ALU.mult))
        st.then(nc.vector.tensor_tensor(second[:], second[:], wide(share[:, 1]), ALU.mult))
        st.then(nc.vector.tensor_tensor(gate[:], first[:], second[:], ALU.add))

    return dve_part, diff


def route(nc, g, name, wg_src, biases, gate, experts):
    with Stage(nc, name) as s:
        wg, more = s.sb("wg", [C + 1, experts]), s.sb("more", [C + 1, experts])
        logits = s.sb("logits", [TP, NT, experts])
        bank = s.ps("bank", [TP, BANK])
        loads, steps = s.sem("loads"), s.sem("steps")
        w_ready, logits_ready, diff_ready, exp_ready = (s.sem(n) for n in ("w_ready", "logits_ready", "diff_ready", "exp_ready"))
        st = Steps(nc.vector, steps)
        dve_part, diff = choose_two(nc, s, nc.vector, diff_ready, exp_ready, st, logits, gate, experts)
        block = s.block()

        @block.sync
        def _(sp):
            sp.dma_start(wg[0:C, :], wg_src).then_inc(loads, 16)
            for dst, b in zip((wg, more), biases):
                sp.dma_start(dst[C:C + 1, :], b.unsqueeze(0)).then_inc(loads, 16)

        @block.tensor
        def _(pe):
            pe.wait_ge(loads, 16 * (1 + len(biases)))
            pe.wait_ge(w_ready, 1)
            for j in range(NT):
                ins = nc.tensor.matmul(bank[:, experts * j:experts * j + experts], g.xT[:, TP * j:TP * j + TP], wg[:],
                                       start=True, stop=True)
            ins.then_inc(logits_ready, 1)

        @block.scalar
        def _(act):
            act.wait_ge(diff_ready, 1)
            nc.scalar.activation(diff[:], diff[:], ACT.Exp).then_inc(exp_ready, 1)

        @block.vector
        def _(dve):
            if len(biases) == 2:
                dve.wait_ge(loads, 16 * 3)
                nc.vector.tensor_tensor(wg[C:C + 1, :], wg[C:C + 1, :], more[C:C + 1, :], ALU.add).then_inc(w_ready, 1)
            else:
                dve.sem_inc(w_ready, 1)
            dve.wait_ge(logits_ready, 1)
            st.then(nc.vector.tensor_copy(logits[:].rearrange("p j e -> p (j e)"), bank[:, 0:NT * experts]))
            dve_part()


def run_experts(nc, g, name, gate, w1, w2, b2_src, experts, chunks, func, loads_first=()):
    K = experts * chunks
    W = experts * C
    with Stage(nc, name) as s:
        b2, ones = s.sb("b2", [1, W]), s.sb("one", [1, TP])
        hidden = s.sb("hidden", [P, 4, GC])
        gated, summed = s.sb("gated", [TP, GT, experts, C]), s.sb("summed", [TP, GT, C])
        up = s.ps("up", [P, 4, BANK])
        down = s.ps("down", [TP, GT, BANK])
        loads, ready, raised, squashed = (s.sem(n) for n in ("loads", "ready", "raised", "squashed"))
        used, taken, reduced, added = (s.sem(n) for n in ("used", "taken", "reduced", "added"))
        block = s.block()

        @block.sync
        def _(sp):
            sp.dma_start(b2[:], b2_src).then_inc(loads, 16)
            for dst, src in loads_first:
                sp.dma_start(dst, src).then_inc(loads, 16)

        @block.tensor
        def _(pe):
            pe.wait_ge(ready, 1)
            pe.wait_ge(loads, 16 * (1 + len(loads_first)))
            with pe.Fori(0, NG) as n:
                for k in range(K + 1):
                    if k < K:
                        if k >= 4:
                            pe.wait_ge(squashed, K * n + k - 3)
                        nc.tensor.matmul(up[:, k % 4, 0:GC], w1[:, P * k:P * k + P], g.xT[:, bass.ds(GC * n, GC)],
                                         start=True, stop=True).then_inc(raised, 1)
                    if k == 1:
                        pe.wait_ge(taken, n + 1)
                        for t in range(GT):
                            nc.tensor.matmul(down[:, t, 0:W], ones[:], b2[:], start=True, stop=False,
                                             skip_group_check=True)
                    if k:
                        c = k - 1
                        e = c // chunks
                        pe.wait_ge(squashed, K * n + c + 1)
                        for t in range(GT):
                            ins = nc.tensor.matmul(down[:, t, C * e:C * e + C], hidden[:, c % 4, TP * t:TP * t + TP],
                                                   w2[:, c, :], start=False, stop=(c == K - 1), skip_group_check=True)
                        ins.then_inc(used, 1)

        @block.scalar
        def _(act):
            with act.Fori(0, NG) as n:
                for k in range(K):
                    act.wait_ge(raised, K * n + k + 1)
                    if k >= 4:
                        act.wait_ge(used, K * n + k - 3)
                    nc.scalar.activation(hidden[:, k % 4], up[:, k % 4, 0:GC], func).then_inc(squashed, 1)

        @block.vector
        def _(dve):
            dve.sem_inc(taken, 1)
            nc.vector.memset(ones[:], 1.0).then_inc(ready, 1)
            with dve.Fori(0, NG) as n:
                dve.wait_ge(used, K * n + K)
                nc.vector.tensor_tensor(gated[:], down[:, :, 0:W].rearrange("p t (e c) -> p t e c", c=C),
                                        bc(gate[:, bass.ds(GT * n, GT), :].unsqueeze(3), [TP, GT, experts, C]),
                                        ALU.mult).then_inc(taken, 1)
                dve.wait_ge(taken, n + 2)
                nc.vector.tensor_reduce(summed[:], gated[:].rearrange("p t e c -> p t c e"), AX.X,
                                        ALU.add).then_inc(reduced, 1)
                dve.wait_ge(reduced, n + 1)
                part = g.h[:, bass.ds(GT * n, GT), :]
                nc.vector.tensor_tensor(part, part, summed[:], ALU.add).then_inc(added, 1)
                dve.wait_ge(added, n + 1)


def mamba(nc, g, A):
    DI, DS, DR, DC = 128, 16, 16, 4
    PAD = DC - 1
    HB = B // 2
    HN = HB * T
    QC = 2 * T
    with Stage(nc, "ma") as s:
        w_in, w_out = s.sb("w_in", [C, 2 * DI]), s.sb("w_out", [DI, C])
        w_dt, w_bc = s.sb("w_dt", [DI, 2, DR]), s.sb("w_bc", [DI, 2, 6 * DS])
        w_delta = s.sb("w_delta", [DR, 2, DI])
        conv_w, conv_b = s.sb("conv_w", [DI, 2, DC]), s.sb("conv_b", [DI, 2])
        delta_b, skip, a_log = s.sb("delta_b", [DI, 2]), s.sb("skip", [DI, 2]), s.sb("a_log", [DI, 2, DS])
        pick = s.sb("pick", [96, 2 * DS, P], BF16)
        xpad = s.sb("xpad", [DI, B, T + 2 * PAD])
        gate, y = s.sb("gate", [DI, B, T]), s.sb("y", [DI, B, T])
        u, delta, du = s.sb("u", [DI, B, T]), s.sb("delta", [DI, B, T]), s.sb("du", [DI, B, T])
        dt = s.sb("dt", [DR, N])
        acc = s.sb("acc", [DI, B, T])
        bc_parts = s.sb("bc_parts", [96, N], BF16)
        low = s.sb("low", [96, HN], BF16)
        decay, state = s.sb("decay", [DI, 2, HB, T]), s.sb("state", [DI, 2, HB, T])
        rest = decay[0:96, 0].rearrange("p b t -> p (b t)")
        banks = s.ps("banks", [P, 8, BANK])
        loads, cleared, picked = s.sem("loads"), s.sem("cleared"), s.sem("picked")
        projected, evacuated, relued, split = s.sem("projected"), s.sem("evacuated"), s.sem("relued"), s.sem("split")
        convolved, u_ready, ln_ready, steps_v = s.sem("convolved"), s.sem("u_ready"), s.sem("ln_ready"), s.sem("steps_v")
        steps_a = s.sem("steps_a")
        b_ready, c_ready, decay_ready, driven = s.sem("b_ready"), s.sem("c_ready"), s.sem("decay_ready"), s.sem("driven")
        scanned, weighted, added, y_ready = s.sem("scanned"), s.sem("weighted"), s.sem("added"), s.sem("y_ready")
        out_ready, du_ready, acc_ready = s.sem("out_ready"), s.sem("du_ready"), s.sem("acc_ready")
        restarted = s.sem("restarted")
        block = s.block()

        @block.sync
        def _(sp):
            names = ("", "_b")
            sp.dma_start(w_in[:], A["L0_attn_in_proj_w"]).then_inc(loads, 16)
            sp.dma_start(w_out[:], A["L0_attn_out_proj_w"]).then_inc(loads, 16)
            for d, n in enumerate(names):
                sp.dma_start(w_dt[:, d], A["L0_attn_x_proj_w" + n][:, 0:DR]).then_inc(loads, 16)
                for q in range(3):
                    sp.dma_start(w_bc[:, d, 2 * DS * q:2 * DS * q + 2 * DS],
                                 A["L0_attn_x_proj_w" + n][:, DR:DR + 2 * DS]).then_inc(loads, 16)
                sp.dma_start(w_delta[:, d], A["L0_attn_dt_proj_w" + n]).then_inc(loads, 16)
                sp.dma_start(conv_w[:, d], A["L0_attn_conv_w" + n]).then_inc(loads, 16)
                sp.dma_start(conv_b[:, d:d + 1], A["L0_attn_conv_b" + n].unsqueeze(1)).then_inc(loads, 16)
                sp.dma_start(delta_b[:, d:d + 1], A["L0_attn_dt_proj_b" + n].unsqueeze(1)).then_inc(loads, 16)
                sp.dma_start(skip[:, d:d + 1], A["L0_attn_D" + n].unsqueeze(1)).then_inc(loads, 16)
                sp.dma_start(a_log[:, d], A["L0_attn_A" + n + "_log"]).then_inc(loads, 16)
        LOADS = 16 * (2 + 2 * 10)

        @block.tensor
        def _(pe):
            pe.wait_ge(loads, LOADS)
            for m in range(2):
                for c in range(8):
                    if m:
                        pe.wait_ge(evacuated, c + 1)
                    nc.tensor.matmul(banks[:, c, 0:QC], w_in[:, DI * m:DI * m + DI], g.xT[0:C, QC * c:QC * c + QC],
                                     start=True, stop=True).then_inc(projected, 1)
            pe.wait_ge(picked, 4)
            for d in range(2):
                done = 16 + 24 * d
                pe.wait_ge(u_ready, d + 1)
                if d:
                    pe.wait_ge(weighted, 1 + 32 * d)
                for c in range(8):
                    pe.wait_ge(evacuated, done if c == 0 else done - 8 + c + 1)
                    nc.tensor.matmul(banks[0:DR, c, 0:QC], w_dt[:, d], u[:, 2 * c:2 * c + 2, :],
                                     start=True, stop=True).then_inc(projected, 1)
                for c in range(8):
                    pe.wait_ge(evacuated, done + c + 1)
                    nc.tensor.matmul(banks[:, c, 0:QC], w_delta[:, d], dt[:, QC * c:QC * c + QC],
                                     start=True, stop=True).then_inc(projected, 1)
                for c in range(8):
                    pe.wait_ge(evacuated, done + 8 + c + 1)
                    nc.tensor.matmul(banks[0:96, c, 0:QC], w_bc[:, d], u[:, 2 * c:2 * c + 2, :],
                                     start=True, stop=True).then_inc(projected, 1)
                pe.wait_ge(split, 2 * d + 2)
                for half in range(2):
                    with pe.Fori(0, DS) as n:
                        k = (2 * d + half) * DS + n
                        for row, free, ready in ((0, driven, b_ready), (DS, weighted, c_ready)):
                            pe.wait_ge(free, k + 1)
                            for c in range(4):
                                ins = nc.tensor.matmul(banks[:, (4 if row else 0) + c, 0:QC], pick[:, row + n, :],
                                                       bc_parts[:, HN * half + QC * c:HN * half + QC * c + QC],
                                                       start=True, stop=True)
                            ins.then_inc(ready, 1)
            pe.wait_ge(y_ready, 1)
            for j in range(NT):
                ins = nc.tensor.matmul(banks[0:TP, j // 8, C * (j % 8):C * (j % 8) + C],
                                       y[:, j // 2, TP * (j % 2):TP * (j % 2) + TP], w_out[:], start=True, stop=True)
                if j % 8 == 7:
                    ins.then_inc(out_ready, 1)

        @block.scalar
        def _(act):
            st = Steps(act, steps_a)
            act.wait_ge(loads, LOADS)
            st.done(nc.scalar.activation(a_log[:], a_log[:], ACT.Exp))
            act.wait_ge(cleared, 1)
            for c in range(8):
                act.wait_ge(projected, c + 1)
                nc.scalar.copy(xpad[:, 2 * c:2 * c + 2, PAD:PAD + T],
                               banks[:, c, 0:QC].rearrange("p (b t) -> p b t", b=2)).then_inc(evacuated, 1)
            for c in range(8):
                act.wait_ge(projected, 8 + c + 1)
                nc.scalar.activation(gate[:, 2 * c:2 * c + 2, :].rearrange("p b t -> p (b t)"), banks[:, c, 0:QC],
                                     ACT.Silu).then_inc(evacuated, 1)
            act.wait_ge(steps_a, 1)
            st.then(nc.scalar.mul(a_log[:], a_log[:], -1.0))
            for d in range(2):
                done = 16 + 24 * d
                act.wait_ge(convolved, d + 1)
                nc.scalar.activation(u[:], u[:], ACT.Silu, bias=conv_b[:, d:d + 1]).then_inc(u_ready, 1)
                for c in range(8):
                    act.wait_ge(projected, done + c + 1)
                    nc.scalar.copy(dt[:, QC * c:QC * c + QC], banks[0:DR, c, 0:QC]).then_inc(evacuated, 1)
                flat = delta[:].rearrange("p b t -> p (b t)")
                for c in range(8):
                    act.wait_ge(projected, done + 8 + c + 1)
                    nc.scalar.activation(flat[:, QC * c:QC * c + QC], banks[:, c, 0:QC], ACT.Identity,
                                         bias=delta_b[:, d:d + 1]).then_inc(evacuated, 1)
                for c in range(8):
                    act.wait_ge(projected, done + 16 + c + 1)
                    nc.scalar.copy(bc_parts[:, QC * c:QC * c + QC], banks[0:96, c, 0:QC]).then_inc(evacuated, 1)
                act.wait_ge(relued, d + 1)
                st.then(nc.scalar.activation(delta[:], delta[:], ACT.Abs))
                st.then(nc.scalar.activation(delta[:], delta[:], ACT.Exp, scale=-1.0))
                nc.scalar.activation(delta[:], delta[:], ACT.Ln, bias=1.0).then_inc(ln_ready, 1)
                act.wait_ge(du_ready, d + 1)
                for half in range(2):
                    with act.Fori(0, DS // 2) as n2:
                        for b in range(2):
                            k = (2 * d + half) * DS + 2 * n2 + b
                            act.wait_ge(scanned, k + 1)
                            nc.scalar.activation(decay[:, b], delta[:, HB * half:HB * half + HB, :], ACT.Exp,
                                                 scale=a_log[:, d, bass.ds(2 * n2 + b, 1)]).then_inc(decay_ready, 1)

        @block.gpsimd
        def _(pool):
            nc.gpsimd.memset(pick[:], 0.0).then_inc(picked, 1)
            for q in range(3):
                pool.wait_ge(picked, q + 1)
                nc.gpsimd.affine_select(out=pick[:], in_=pick[:], compare_op=ALU.not_equal, fill=1.0,
                                        base=-2 * DS * q, pattern=[[-1, 2 * DS], [0, P]],
                                        channel_multiplier=1).then_inc(picked, 1)
            for d in range(2):
                pool.wait_ge(acc_ready, d + 1)
                for half in range(2):
                    part = acc[:, HB * half:HB * half + HB, :]
                    with pool.Fori(0, DS // 2) as n2:
                        for b in range(2):
                            k = (2 * d + half) * DS + 2 * n2 + b
                            pool.wait_ge(weighted, k + 2)
                            pool.wait_ge(added, k + 2)
                            nc.gpsimd.tensor_tensor(part, part, state[:, b], ALU.add).then_inc(added, 1)

        @block.vector
        def _(dve):
            st = Steps(dve, steps_v)
            dve.sem_inc(driven, 1)
            dve.sem_inc(weighted, 1)
            dve.sem_inc(scanned, 2)
            dve.sem_inc(added, 2)
            nc.vector.memset(xpad[:], 0.0).then_inc(cleared, 1)
            for d in range(2):
                done = 16 + 24 * d
                dve.wait_ge(evacuated, 16)
                for i in range(DC):
                    x_i = xpad[:, :, i:i + T] if d == 0 else xpad[:, :, 2 * PAD - i:2 * PAD - i + T][:, :, ::-1]
                    w_i = conv_w[:, d, i:i + 1]
                    if i == 0:
                        st.then(nc.vector.tensor_scalar(u[:], x_i, w_i, None, ALU.mult))
                    elif i < DC - 1:
                        st.then(nc.vector.scalar_tensor_tensor(out=u[:], in0=x_i, scalar=w_i, in1=u[:],
                                                               op0=ALU.mult, op1=ALU.add))
                    else:
                        nc.vector.scalar_tensor_tensor(out=u[:], in0=x_i, scalar=w_i, in1=u[:], op0=ALU.mult,
                                                       op1=ALU.add).then_inc(convolved, 1)
                nc.vector.memset(acc[:], 0.0).then_inc(acc_ready, 1)
                dve.wait_ge(evacuated, done + 16)
                nc.vector.tensor_scalar(du[:], delta[:], 0.0, None, ALU.max).then_inc(relued, 1)
                for half in range(2):
                    dve.wait_ge(evacuated, done + 16 + 4 * half + 4)
                    cols = slice(HN * half, HN * half + HN)
                    if half or d:
                        dve.wait_ge(split, 2 * d + half)
                    rest4 = rest.rearrange("p (c n) -> p c n", c=4)
                    mine = bc_parts[:, cols].rearrange("p (c n) -> p c n", c=4)
                    st.then(nc.vector.tensor_tensor(rest4, banks[0:96, 4 * half:4 * half + 4, 0:QC], mine, ALU.subtract))
                    st.done(nc.vector.tensor_copy(bc_parts[32:64, cols], rest[32:64, :]))
                    st.then(nc.vector.tensor_copy(low[64:96, :], rest[64:96, :]))
                    nc.vector.tensor_tensor(bc_parts[64:96, cols], rest[64:96, :], low[64:96, :],
                                            ALU.subtract).then_inc(split, 1)
                dve.wait_ge(ln_ready, d + 1)
                dve.wait_ge(relued, d + 1)
                st.then(nc.vector.tensor_tensor(delta[:], delta[:], du[:], ALU.add))
                nc.vector.tensor_tensor(du[:], delta[:], u[:], ALU.mult).then_inc(du_ready, 1)
                dve.wait_ge(du_ready, d + 1)
                for half in range(2):
                    part = du[:, HB * half:HB * half + HB, :].rearrange("p (c b) t -> p c (b t)", b=2)
                    with dve.Fori(0, DS // 2) as n2:
                        for b in range(2):
                            k = (2 * d + half) * DS + 2 * n2 + b
                            now = state[:, b].rearrange("p b t -> p (b t)")
                            now4 = state[:, b].rearrange("p (c b) t -> p c (b t)", b=2)
                            past = decay[:, b].rearrange("p b t -> p (b t)")
                            dve.wait_ge(b_ready, k + 1)
                            dve.wait_ge(added, k + 1)
                            nc.vector.tensor_tensor(now4, banks[:, 0:4, 0:QC], part, ALU.mult).then_inc(driven, 1)
                            dve.wait_ge(decay_ready, k + 1)
                            nc.vector.memset(decay[:, b, :, 0:1], 0.0).then_inc(restarted, 1)
                            dve.wait_ge(driven, k + 2)
                            dve.wait_ge(restarted, k + 1)
                            nc.vector.tensor_tensor_scan(now, past, now, 0.0, ALU.mult, ALU.add).then_inc(scanned, 1)
                            dve.wait_ge(scanned, k + 3)
                            dve.wait_ge(c_ready, k + 1)
                            nc.vector.tensor_tensor(now4, banks[:, 4:8, 0:QC], now4, ALU.mult).then_inc(weighted, 1)
                dve.wait_ge(added, 32 * (d + 1) + 2)
                if d == 0:
                    st.then(nc.vector.scalar_tensor_tensor(out=y[:], in0=u[:], scalar=skip[:, 0:1], in1=acc[:],
                                                           op0=ALU.mult, op1=ALU.add))
                else:
                    st.then(nc.vector.scalar_tensor_tensor(out=acc[:], in0=u[:], scalar=skip[:, 1:2], in1=acc[:],
                                                           op0=ALU.mult, op1=ALU.add))
                    st.then(nc.vector.tensor_tensor(y[:], y[:], acc[:, :, ::-1], ALU.add))
                    nc.vector.tensor_tensor(y[:], y[:], gate[:], ALU.mult).then_inc(y_ready, 1)
            for q in range(4):
                dve.wait_ge(out_ready, q + 1)
                part = g.h[:, 8 * q:8 * q + 8, :]
                nc.vector.tensor_tensor(part, part, banks[0:TP, q, :].rearrange("p (j c) -> p j c", j=8), ALU.add)


def graph_experts(nc, g, A):
    E, HEADS, TOPS = 4, 4, 16
    EDGES = 262144
    COLS = EDGES // P
    F = HEADS * E
    V = F + HEADS
    G = 8
    HIGH = 60.0
    ROUND = 12582912.0
    with Stage(nc, "ge") as s:
        gate = s.sb("gate", [TP, NT, E])
        w1, w2 = s.sb("w1", [C + 1, E * P]), s.sb("w2", [P, E, C])
        nodes, own = s.sb("nodes", [TP, NT, F + 2 * HEADS]), s.sb("own", [TP, NT, V])
        keys = s.sb("keys", [P, COLS])
        turns = s.sb("turns", [P, 1], I32)
        with Stage(nc, "gt") as t:
            make_tables(nc, g, A, t, nodes, own, keys, turns, E, HEADS, F, V, COLS, HIGH, ROUND)
        with Stage(nc, "gw") as t:
            walk_edges(nc, g, A, t, own, keys, turns, gate, E, HEADS, F, V, G)
        run_experts(nc, g, "gx", gate, w1, w2, A["L0_ffn_b2"], E, 1, ACT.Gelu,
                    ((w1[0:C, :], A["L0_ffn_W1"]), (w1[C:C + 1, :], A["L0_ffn_b1"]), (w2[:], A["L0_ffn_W2"])))


def make_tables(nc, g, A, s, nodes, own, keys, turns, E, HEADS, F, V, COLS, HIGH, ROUND):
    wg, fold = s.sb("wg", [C, F]), s.sb("fold", [F, F + 2 * HEADS])
    hT = s.sb("hT", [F, N])
    dst_rows, leaky = s.sb("dst_rows", [P, NT, 2 * HEADS]), s.sb("leaky", [TP, NT, HEADS])
    bound, top, topmost = s.sb("bound", [TP, NT, HEADS]), s.sb("top", [P, HEADS]), s.sb("topmost", [P, HEADS])
    src_i, dst_i = s.sb("src_i", [P, COLS], I32), s.sb("dst_i", [P, COLS], I32)
    src, dst, tile = (s.sb(n, [P, COLS]) for n in ("src", "dst", "tile"))
    count, most = s.sb("count", [P, 1]), s.sb("most", [P, 1])
    banks = s.ps("banks", [P, 8, BANK])
    loads, edges, projected, hT_ready, folded = (s.sem(n) for n in ("loads", "edges", "projected", "hT_ready", "folded"))
    nodes_ready, tops_ready, reduced, steps_v = (s.sem(n) for n in ("nodes_ready", "tops_ready", "reduced", "steps_v"))
    own_in, own_out, rows_ready, stored, steps_p = (s.sem(n) for n in ("own_in", "own_out", "rows_ready", "stored", "steps_p"))
    block = s.block()

    @block.sync
    def _(sp):
        sp.dma_start(wg[:], A["L0_ffn_W_gat"]).then_inc(loads, 16)
        sp.dma_start(fold[:], A["fold"]).then_inc(loads, 16)
        sp.dma_start(dst_i[:], A["L0_ffn_edge_index"][1].rearrange("(p n) -> p n", p=P)).then_inc(edges, 16)
        sp.dma_start(src_i[:], A["L0_ffn_edge_index"][0].rearrange("(p n) -> p n", p=P)).then_inc(edges, 16)
        sp.wait_ge(rows_ready, 1)
        sp.dma_start(g.src_table.rearrange("(j p) v -> p j v", p=TP), nodes[:, :, 0:V]).then_inc(stored, 16)
        sp.dma_start(g.dst_table.rearrange("(j p) v -> p j v", p=P), dst_rows[:]).then_inc(stored, 16)
        sp.wait_ge(stored, 32)

    @block.tensor
    def _(pe):
        pe.wait_ge(loads, 32)
        for c in range(NG):
            nc.tensor.matmul(banks[0:F, c, 0:GC], wg[:], g.xT[0:C, GC * c:GC * c + GC], start=True,
                             stop=True).then_inc(projected, 1)
        pe.wait_ge(hT_ready, NG)
        W = F + 2 * HEADS
        for j in range(NT):
            ins = nc.tensor.matmul(banks[0:TP, j // 16, W * (j % 16):W * (j % 16) + W], hT[:, TP * j:TP * j + TP],
                                   fold[:], start=True, stop=True)
        ins.then_inc(folded, 1)

    @block.scalar
    def _(act):
        for c in range(NG):
            act.wait_ge(projected, c + 1)
            nc.scalar.copy(hT[:, GC * c:GC * c + GC], banks[0:F, c, 0:GC]).then_inc(hT_ready, 1)
        act.wait_ge(folded, 1)
        nc.scalar.copy(nodes[:].rearrange("p (q j) w -> p q (j w)", q=2),
                       banks[0:TP, 0:2, 0:16 * (F + 2 * HEADS)]).then_inc(nodes_ready, 1)
        act.wait_ge(own_in, 1)
        nc.scalar.activation(own[:, :, F:V], own[:, :, F:V], ACT.Exp).then_inc(own_out, 1)

    @block.gpsimd
    def _(pool):
        pool.wait_ge(tops_ready, 1)
        nc.gpsimd.partition_all_reduce(topmost[:], top[:], P, RMAX).then_inc(reduced, 1)
        pool.wait_ge(tops_ready, 2)
        pool.wait_ge(reduced, 1)
        nc.gpsimd.partition_all_reduce(most[:], count[:], P, RMAX).then_inc(reduced, 1)

    @block.vector
    def _(dve):
        st = Steps(dve, steps_v)
        src_score, dst_score = nodes[:, :, F:V], nodes[:, :, V:V + HEADS]
        st.done(nc.vector.memset(dst_rows[:], 0.0))
        st.then(nc.vector.memset(top[:], -3e38))
        dve.wait_ge(nodes_ready, 1)
        nc.vector.tensor_reduce(top[0:TP, :], src_score.rearrange("p j h -> p h j"), AX.X, ALU.max).then_inc(tops_ready, 1)
        st.done(nc.vector.tensor_copy(dst_rows[0:TP, :, 0:HEADS], dst_score))
        st.then(nc.vector.tensor_tensor(leaky[:], src_score, dst_score, ALU.add))
        st.then(nc.vector.scalar_tensor_tensor(out=leaky[:], in0=leaky[:], scalar=0.2, in1=leaky[:], op0=ALU.mult, op1=ALU.max))
        dve.wait_ge(reduced, 1)
        st.then(nc.vector.tensor_tensor(bound[:], dst_score, bc(topmost[0:TP, :].unsqueeze(1), [TP, NT, HEADS]), ALU.add))
        st.then(nc.vector.scalar_tensor_tensor(out=bound[:], in0=bound[:], scalar=0.2, in1=bound[:], op0=ALU.mult, op1=ALU.max))
        st.then(nc.vector.scalar_tensor_tensor(out=dst_rows[0:TP, :, HEADS:], in0=bound[:], scalar=-HIGH, in1=leaky[:],
                                               op0=ALU.add, op1=ALU.max))
        nc.vector.tensor_tensor(own[:, :, F:V], leaky[:], dst_rows[0:TP, :, HEADS:], ALU.subtract).then_inc(own_in, 1)
        dve.sem_inc(rows_ready, 1)
        dve.wait_ge(edges, 32)
        st.done(nc.vector.tensor_copy(src[:], src_i[:]))
        st.then(nc.vector.tensor_copy(dst[:], dst_i[:]))
        st.then(nc.vector.tensor_scalar(tile[:], dst[:], float(TP // 2), 1.0 / TP, ALU.subtract, ALU.mult))
        st.then(nc.vector.tensor_scalar(tile[:], tile[:], ROUND, None, ALU.add))
        st.then(nc.vector.tensor_scalar(tile[:], tile[:], ROUND, None, ALU.subtract))
        st.then(nc.vector.scalar_tensor_tensor(out=keys[:], in0=tile[:], scalar=float(P - TP), in1=dst[:], op0=ALU.mult,
                                               op1=ALU.add))
        st.then(nc.vector.tensor_scalar(src[:], src[:], float(N - 1), 1.0, ALU.min, ALU.add))
        st.then(nc.vector.scalar_tensor_tensor(out=keys[:], in0=keys[:], scalar=4096.0, in1=src[:], op0=ALU.mult, op1=ALU.add))
        st.then(nc.vector.tensor_scalar(dst[:], dst[:], float(N), None, ALU.is_lt))
        st.done(nc.vector.tensor_reduce(count[:], dst[:], AX.X, ALU.add))
        st.then(nc.vector.tensor_tensor(keys[:], keys[:], dst[:], ALU.mult))
        st.then(nc.vector.tensor_scalar(keys[:], keys[:], -1.0, None, ALU.add))
        dve.sem_inc(tops_ready, 1)
        dve.wait_ge(own_out, 1)
        w = bc(own[:, :, F:V].unsqueeze(3), [TP, NT, HEADS, E])
        st.done(nc.vector.tensor_tensor(own[:, :, 0:F].rearrange("p j (h e) -> p j h e", h=HEADS),
                                        nodes[:, :, 0:F].rearrange("p j (h e) -> p j h e", h=HEADS), w, ALU.mult))
        dve.wait_ge(reduced, 2)
        st.then(nc.vector.tensor_scalar(turns[:], most[:], 1.0, 15.0, ALU.max, ALU.add))
        st.then(nc.vector.tensor_scalar(turns[:], turns[:], 4, None, ALU.arith_shift_right))


def walk_edges(nc, g, A, s, own, keys, turns, gate, E, HEADS, F, V, G):
    MOST = keys.shape[1] // (2 * G)
    best = s.sb("largest", [P, G])
    code = s.sb("code", [P, G], I32)
    src_at, dst_at = s.sb("src_at", [P, 2, G], I32), s.sb("dst_at", [P, 2, G], I32)
    part_i = s.sb("part_i", [P, 2, G], I32)
    tile, row = s.sb("tile", [P, 2, G]), s.sb("row", [P, 2, G])
    src_rows, dst_rows = s.sb("src_rows", [P, 2, G, V]), s.sb("dst_rows", [P, 2, G, 2 * HEADS])
    score = s.sb("score", [P, G, HEADS])
    value = s.sb("value", [P, G, V])
    row_hot, tile_hot = s.sb("row_hot", [P, 2, G, TP]), s.sb("tile_hot", [P, G, NT])
    spread = s.sb("spread", [P, 2, G, NT, V])
    ramp_i, ramp, zeros = s.sb("ramp_i", [P, P], I32), s.sb("ramp", [P, P]), s.sb("zeros", [1, BANK])
    total = s.sb("total", [TP, NT, V])
    gamma, beta, b_gat = (s.sb(n, [TP, F]) for n in ("gamma", "beta", "b_gat"))
    mean, var, sq = s.sb("mean", [TP, NT]), s.sb("var", [TP, NT]), s.sb("sq", [TP, NT, F])
    scores = s.sb("scores", [TP, NT, E])
    sums = s.ps("sums", [TP, 2, BANK])
    W = NT // 2 * V
    loads, consts, picked, steps_v = (s.sem(n) for n in ("loads", "consts", "picked", "steps_v"))
    gathered = [s.sem(f"gathered{b}") for b in range(2)]
    consumed, score_in, score_out = s.sem("consumed"), s.sem("score_in"), s.sem("score_out")
    spread_ready, summed, root_in, root_out = (s.sem(n) for n in ("spread_ready", "summed", "root_in", "root_out"))
    diff_ready, exp_ready = s.sem("diff_ready"), s.sem("exp_ready")
    steps_end, waited = s.sem("steps_end"), s.sem("waited")
    st_end = Steps(nc.vector, steps_end)
    dve_part, diff = choose_two(nc, s, nc.vector, diff_ready, exp_ready, st_end, scores, gate, E)
    block = s.block()

    def turns_of(eng):
        return eng.value_load(turns[0:1, 0:1], min_val=1, max_val=MOST)

    @block.sync
    def _(sp):
        for dst, name in ((gamma, "ln_gamma"), (beta, "ln_beta"), (b_gat, "b_gat")):
            sp.dma_start(dst[:], A["L0_ffn_" + name].unsqueeze(0).to_broadcast([TP, F])).then_inc(loads, 16)

    @block.gpsimd
    def _(pool):
        nc.gpsimd.iota(ramp_i[:], pattern=[[1, P]], base=0, channel_multiplier=0).then_inc(consts, 1)
        with pool.Fori(0, turns_of(pool)) as i:
            for b in range(2):
                pool.wait_ge(picked, 2 * i + b + 1)
                pool.wait_ge(consumed, 2 * i + b + 1)
                pool.sem_inc(waited, 1)
                for k in range(G):
                    for rows, at, table in ((src_rows, src_at, g.src_table), (dst_rows, dst_at, g.dst_table)):
                        nc.gpsimd.indirect_dma_start(
                            out=rows[:, b, k, :], out_offset=None, in_=table,
                            in_offset=bass.IndirectOffsetOnAxis(ap=at[:, b, k:k + 1], axis=0)).then_inc(gathered[b], 16)

    @block.scalar
    def _(act):
        with act.Fori(0, turns_of(act)) as i:
            for b in range(2):
                act.wait_ge(score_in, 2 * i + b + 1)
                nc.scalar.activation(value[:, :, F:V], score[:], ACT.Exp).then_inc(score_out, 1)
        act.wait_ge(root_in, 1)
        nc.scalar.activation(var[:], var[:], ACT.Sqrt).then_inc(root_out, 1)
        act.wait_ge(diff_ready, 1)
        nc.scalar.activation(diff[:], diff[:], ACT.Exp).then_inc(exp_ready, 1)

    @block.tensor
    def _(pe):
        pe.wait_ge(consts, 3)
        for q in range(2):
            nc.tensor.matmul(sums[:, q, 0:W], zeros[:, 0:TP], zeros[:, 0:W], start=True, stop=False,
                             skip_group_check=True)
        with pe.Fori(0, turns_of(pe)) as i:
            for b in range(2):
                pe.wait_ge(spread_ready, 2 * i + b + 1)
                for k in range(G):
                    for q in range(2):
                        half = spread[:, b, k, NT // 2 * q:NT // 2 * q + NT // 2, :].rearrange("p j v -> p (j v)")
                        ins = nc.tensor.matmul(sums[:, q, 0:W], row_hot[:, b, k, :], half, start=False, stop=False,
                                               skip_group_check=True)
                ins.then_inc(summed, 1)

    @block.vector
    def _(dve):
        st = Steps(dve, steps_v)
        dve.sem_inc(consumed, 2)
        dve.sem_inc(summed, 2)
        dve.wait_ge(consts, 1)
        nc.vector.memset(zeros[:], 0.0).then_inc(consts, 1)
        nc.vector.tensor_copy(ramp[:], ramp_i[:]).then_inc(consts, 1)
        dve.wait_ge(consts, 3)

        def pick(turn, b, st):
            dve.sem_inc(waited, 1)
            st.then(nc.vector.max(out=best[:], in_=keys[:]))
            dve.sem_inc(waited, 1)
            st.done(nc.vector.match_replace(out=keys[:], in_to_replace=best[:], in_values=keys[:], imm_value=-1.0))
            st.then(nc.vector.tensor_copy(code[:], best[:]))
            st.done(nc.vector.tensor_scalar(src_at[:, b], code[:], 4095, None, ALU.bitwise_and))
            st.done(nc.vector.tensor_scalar(dst_at[:, b], code[:], 12, None, ALU.arith_shift_right))
            st.then(nc.vector.tensor_scalar(part_i[:, 0], code[:], 19, None, ALU.arith_shift_right))
            st.done(nc.vector.tensor_copy(tile[:, b], part_i[:, 0]))
            st.then(nc.vector.tensor_scalar(part_i[:, 1], dst_at[:, b], P - 1, None, ALU.bitwise_and))
            st.done(nc.vector.tensor_copy(row[:, b], part_i[:, 1]))
            st.done(nc.vector.tensor_scalar(src_at[:, b], src_at[:, b], float(N - 1), None, ALU.min))
            st.then(nc.vector.tensor_scalar(dst_at[:, b], dst_at[:, b], 0.0, None, ALU.max))
            dve.sem_inc(picked, 1)

        def spread_out(turn, b, st):
            dve.wait_ge(gathered[b], 256 * (turn + 1))
            st.then(nc.vector.tensor_tensor(score[:], src_rows[:, b, :, F:V], dst_rows[:, b, :, 0:HEADS], ALU.add))
            st.then(nc.vector.scalar_tensor_tensor(out=score[:], in0=score[:], scalar=0.2, in1=score[:], op0=ALU.mult,
                                                   op1=ALU.max))
            nc.vector.tensor_tensor(score[:], score[:], dst_rows[:, b, :, HEADS:], ALU.subtract).then_inc(score_in, 1)
            dve.wait_ge(summed, 2 * turn + b + 1)
            st.done(nc.vector.tensor_tensor(row_hot[:, b], bc(ramp[:, 0:TP].unsqueeze(1), [P, G, TP]),
                                            bc(row[:, b].unsqueeze(2), [P, G, TP]), ALU.is_equal))
            st.done(nc.vector.tensor_tensor(tile_hot[:], bc(ramp[:, 0:NT].unsqueeze(1), [P, G, NT]),
                                            bc(tile[:, b].unsqueeze(2), [P, G, NT]), ALU.is_equal))
            dve.wait_ge(score_out, 2 * turn + b + 1)
            w = bc(value[:, :, F:V].unsqueeze(3), [P, G, HEADS, E])
            st.then(nc.vector.tensor_tensor(value[:, :, 0:F].rearrange("p k (h e) -> p k h e", h=HEADS),
                                            src_rows[:, b, :, 0:F].rearrange("p k (h e) -> p k h e", h=HEADS), w,
                                            ALU.mult))
            dve.sem_inc(consumed, 1)
            nc.vector.tensor_tensor(spread[:, b], bc(tile_hot[:].unsqueeze(3), [P, G, NT, V]),
                                    bc(value[:].unsqueeze(2), [P, G, NT, V]), ALU.mult).then_inc(spread_ready, 1)
            dve.wait_ge(spread_ready, 2 * turn + b + 1)

        pick(0, 0, st)
        first = st.n
        PICK, SPREAD = 11, 5
        count = turns_of(dve)
        with dve.Fori(0, count) as i:
            st = Steps(dve, steps_v, first + 2 * (PICK + SPREAD) * i)
            for b in range(2):
                pick(i, 1 - b, st)
                spread_out(i, b, st)
            assert st.n == 2 * (PICK + SPREAD)
        st = st_end
        dve.wait_ge(summed, 2 * count + 2)
        for q in range(2):
            part = slice(NT // 2 * q, NT // 2 * q + NT // 2)
            st.done(nc.vector.tensor_tensor(total[:, part], sums[:, q, 0:W].rearrange("p (j v) -> p j v", v=V),
                                            own[:, part], ALU.add))
        dve.wait_ge(steps_end, st.n)
        den = total[:, :, F:V]
        st.then(nc.vector.tensor_scalar(den, den, 1e-16, None, ALU.add))
        st.then(nc.vector.reciprocal(den, den))
        agg = total[:, :, 0:F]
        agg4 = agg.rearrange("p j (h e) -> p j h e", h=HEADS)
        wide = [TP, NT, F]
        st.then(nc.vector.tensor_tensor(agg4, agg4, bc(den.unsqueeze(3), [TP, NT, HEADS, E]), ALU.mult))
        dve.wait_ge(loads, 48)
        st.then(nc.vector.tensor_tensor(agg, agg, bc(b_gat[:].unsqueeze(1), wide), ALU.add))
        st.then(nc.vector.tensor_reduce(mean[:], agg, AX.X, ALU.add))
        st.then(nc.vector.tensor_scalar(mean[:], mean[:], 1.0 / F, None, ALU.mult))
        st.then(nc.vector.tensor_tensor(agg, agg, bc(mean[:].unsqueeze(2), wide), ALU.subtract))
        st.then(nc.vector.tensor_tensor(sq[:], agg, agg, ALU.mult))
        st.then(nc.vector.tensor_reduce(var[:], sq[:], AX.X, ALU.add))
        nc.vector.tensor_scalar(var[:], var[:], 1.0 / F, EPS, ALU.mult, ALU.add).then_inc(root_in, 1)
        dve.wait_ge(root_out, 1)
        st.then(nc.vector.reciprocal(mean[:], var[:]))
        st.then(nc.vector.tensor_tensor(agg, agg, bc(mean[:].unsqueeze(2), wide), ALU.mult))
        st.then(nc.vector.tensor_tensor(agg, agg, bc(gamma[:].unsqueeze(1), wide), ALU.mult))
        st.then(nc.vector.tensor_tensor(agg, agg, bc(beta[:].unsqueeze(1), wide), ALU.add))
        st.then(nc.vector.tensor_reduce(scores[:], agg.rearrange("p j (h e) -> p j e h", h=HEADS), AX.X, ALU.add))
        st.then(nc.vector.tensor_scalar(scores[:], scores[:], 1.0 / HEADS, None, ALU.mult))
        dve_part()


def rwkv(nc, g, A):
    with Stage(nc, "rw") as s:
        mix, rest = s.sb("mix", [C, 3]), s.sb("rest", [C, 3])
        w3, wo = s.sb("w3", [C, 3, C]), s.sb("wo", [C, C])
        decay, steps = s.sb("decay", [TP, 2, TP]), s.sb("ones", [TP, 2, TP])
        windows = s.sb("windows", [TP, 2, 2, TP])
        mixed = s.sb("mixed", [C, 3, B, T])
        k, kv, r, z = (s.sb(n, [TP, NT, C]) for n in ("k", "kv", "r", "z"))
        inv = s.sb("inv", [TP, 4, BANK])
        zT = s.sb("zT", [C, N])
        banks = s.ps("banks", [P, 8, BANK])
        loads, steps_v = s.sem("loads"), s.sem("steps_v")
        mix_ready, projected, k_clipped, k_ready = s.sem("mix_ready"), s.sem("projected"), s.sem("k_clipped"), s.sem("k_ready")
        kv_ready, r_ready, summed, z_ready = s.sem("kv_ready"), s.sem("r_ready"), s.sem("summed"), s.sem("z_ready")
        turned, zT_ready, out_ready = s.sem("turned"), s.sem("zT_ready"), s.sem("out_ready")
        turned_round = s.sem("turned_round")
        block = s.block()
        x = g.xT[0:C, :].rearrange("c (b t) -> c b t", b=B)

        @block.sync
        def _(sp):
            for n, m in enumerate("kvr"):
                sp.dma_start(mix[:, n:n + 1], A["L1_attn_time_mix_" + m].rearrange("a b c -> c (a b)")).then_inc(loads, 16)
                sp.dma_start(w3[:, n], A["L1_attn_W" + m]).then_inc(loads, 16)
            sp.dma_start(wo[:], A["L1_attn_Wo"]).then_inc(loads, 16)
            for far in range(2):
                for n, name in enumerate(("time_curve", "time_steps")):
                    curve = A[name]
                    window = bass.AP(tensor=curve.tensor, offset=curve.shape[0] - 2 * TP - TP * far,
                                     ap=[[1, TP], [1, TP]])
                    sp.dma_start(windows[:, n, far], window).then_inc(loads, 16)

        @block.vector
        def _(dve):
            st = Steps(dve, steps_v)
            dve.wait_ge(loads, 16 * 11)
            nc.vector.tensor_copy(decay[:], windows[:, 0, :, ::-1]).then_inc(turned_round, 1)
            nc.vector.tensor_copy(steps[:], windows[:, 1, :, ::-1]).then_inc(turned_round, 1)
            st.then(nc.vector.tensor_scalar(rest[:], mix[:], -1.0, 1.0, ALU.mult, ALU.add))
            for n in range(3):
                st.then(nc.vector.tensor_scalar(mixed[:, n], x, mix[:, n:n + 1], None, ALU.mult))
                nc.vector.scalar_tensor_tensor(out=mixed[:, n, :, 1:T], in0=x[:, :, 0:T - 1], scalar=rest[:, n:n + 1],
                                               in1=mixed[:, n, :, 1:T], op0=ALU.mult, op1=ALU.add).then_inc(mix_ready, 1)
            dve.wait_ge(projected, 4)
            nc.vector.tensor_scalar(k[:], banks[0:TP, 0:4, :].rearrange("p q (j c) -> p (q j) c", c=C), 30.0, -60.0,
                                    ALU.min, ALU.max).then_inc(k_clipped, 1)
            dve.wait_ge(projected, 8)
            dve.wait_ge(k_ready, 1)
            nc.vector.tensor_tensor(kv[:], banks[0:TP, 4:8, :].rearrange("p q (j c) -> p (q j) c", c=C), k[:],
                                    ALU.mult).then_inc(kv_ready, 1)
            dve.wait_ge(summed, 1)
            st.then(nc.vector.reciprocal(inv[:], banks[0:TP, 0:4, :]))
            dve.wait_ge(r_ready, 1)
            dve.wait_ge(summed, 2)
            for half in range(2):
                zh = z[:].rearrange("p (b t) c -> p t b c", t=2)[:, half]
                rh = r[:].rearrange("p (b t) c -> p t b c", t=2)[:, half]
                w = banks[0:TP, 4 + 2 * half:6 + 2 * half, :].rearrange("p q (b c) -> p (q b) c", c=C)
                i = inv[:, 2 * half:2 * half + 2, :].rearrange("p q (b c) -> p (q b) c", c=C)
                st.then(nc.vector.tensor_tensor(zh, w, rh, ALU.mult))
                nc.vector.tensor_tensor(zh, zh, i, ALU.mult).then_inc(z_ready, 1)
            for q in range(4):
                dve.wait_ge(out_ready, q + 1)
                part = g.h[:, 8 * q:8 * q + 8, :]
                nc.vector.tensor_tensor(part, part, banks[0:TP, q, :].rearrange("p (j c) -> p j c", j=8), ALU.add)

        @block.scalar
        def _(act):
            act.wait_ge(k_clipped, 1)
            nc.scalar.activation(k[:], k[:], ACT.Exp).then_inc(k_ready, 1)
            act.wait_ge(projected, 12)
            nc.scalar.activation(r[:], banks[0:TP, 0:4, :].rearrange("p q (j c) -> p (q j) c", c=C),
                                 ACT.Sigmoid).then_inc(r_ready, 1)
            for n in range(NG):
                act.wait_ge(turned, n + 1)
                nc.scalar.copy(zT[:, GC * n:GC * n + GC], banks[0:C, n, 0:GC]).then_inc(zT_ready, 1)

        @block.tensor
        def _(pe):
            pe.wait_ge(loads, 16 * 11)
            for n in range(3):
                pe.wait_ge(mix_ready, n + 1)
                if n == 2:
                    pe.wait_ge(k_clipped, 1)
                for j in range(NT):
                    ins = nc.tensor.matmul(banks[0:TP, 4 * (n % 2) + j // 8, C * (j % 8):C * (j % 8) + C],
                                           mixed[:, n, j // 2, TP * (j % 2):TP * (j % 2) + TP], w3[:, n],
                                           start=True, stop=True)
                    if j % 8 == 7:
                        ins.then_inc(projected, 1)
            pe.wait_ge(turned_round, 2)
            for src, tri, bank, waits in ((k, steps, 0, ((k_ready, 1), (r_ready, 1))), (kv, decay, 4, ((kv_ready, 1),))):
                for sem, value in waits:
                    pe.wait_ge(sem, value)
                halves = src[:].rearrange("p (b t) c -> p t b c", t=2)
                for half in range(2):
                    for q in range(2):
                        out = banks[0:TP, bank + 2 * half + q, :]
                        for u in range(half + 1):
                            ins = nc.tensor.matmul(out, tri[:, half - u], halves[:, u, 8 * q:8 * q + 8, :],
                                                   start=(u == 0), stop=(u == half))
                ins.then_inc(summed, 1)
            pe.wait_ge(z_ready, 2)
            for j in range(NT):
                ins = nc.tensor.transpose(banks[0:C, j // GT, TP * (j % GT):TP * (j % GT) + TP], z[:, j, :],
                                          g.ident[0:TP, 0:TP])
                if j % GT == GT - 1:
                    ins.then_inc(turned, 1)
            pe.wait_ge(zT_ready, NG)
            for j in range(NT):
                ins = nc.tensor.matmul(banks[0:TP, j // 8, C * (j % 8):C * (j % 8) + C], zT[:, TP * j:TP * j + TP],
                                       wo[:], start=True, stop=True)
                if j % 8 == 7:
                    ins.then_inc(out_ready, 1)


def memory_attention(nc, g, A):
    HEADS, D, KEYS, TOP = 8, C, 64, 16
    RUNS = [TOP // (r + 1) for r in range(TOP // 2)]
    CAND = sum(RUNS) + TOP // 2
    NUM_KV = KEYS * KEYS
    SEEN = TP + T
    PAIRS = HEADS // 2
    BODY_STEPS = 552
    with Stage(nc, "me") as s:
        wpkT, keysT = s.sb("wpkT", [D // 2, 2 * HEADS, C]), s.sb("keysT", [D // 2, 2 * HEADS, KEYS])
        wsim = s.sb("wsim", [C, 2, HEADS * KEYS])
        wq, wo = s.sb("wq", [C, HEADS * D]), s.sb("wo", [D, HEADS, C])
        ramp_i, ramp = s.sb("ramp_i", [TP, CAND], I32), s.sb("ramp", [TP, CAND])
        mask = s.sb("mask", [TP, SEEN])
        x = s.sb("x", [C, 2, TP])
        best = [s.sb(f"best{p}", [TP, 2, TOP]) for p in range(2)]
        place, left = s.sb("place", [TP, 2, TOP], U32), s.sb("left", [TP, KEYS])
        cand, cand_left = s.sb("cand", [TP, 2, CAND]), s.sb("cand_left", [TP, CAND])
        final, at, atf = s.sb("final", [TP, 2, HEADS, TOP]), s.sb("at", [TP, TOP], U32), s.sb("atf", [TP, TOP])
        hot, rowf = s.sb("hot", [TP, TOP, CAND]), s.sb("rowf", [TP, TOP])
        row = s.sb("row", [TP, 2, HEADS, TOP], I32)
        lowest, weight = s.sb("lowest", [TP, 2, HEADS]), s.sb("weight", [TP, 2, HEADS, TOP])
        total = s.sb("total", [TP, 2, HEADS])
        rows = s.sb("rows", [TP, 2, TOP, 2 * D])
        kv = s.sb("kv", [TP, 2, 2, HEADS, D])
        kT, v, q = s.sb("kT", [P, PAIRS, T]), s.sb("v", [TP, 2, HEADS, D]), s.sb("q", [P, PAIRS, T])
        seen, neg = s.sb("seen", [TP, 2, SEEN]), s.sb("neg", [TP, 2, 2])
        norm = s.sb("norm", [TP, 2, 2])
        pT, oT = s.sb("pT", [TP, 2, SEEN]), s.sb("oT", [D, 2, T])
        sims = s.ps("sims", [P, 2, BANK])
        qbank = s.ps("qbank", [P, 2, BANK])
        score, turned, outT, out = (s.ps(n, [P, BANK]) for n in ("score", "turned", "outT", "out"))

        loads, folded, ramp_ready = s.sem("loads"), s.sem("folded"), s.sem("ramp_ready")
        mask_zero, mask_ready = s.sem("mask_zero"), s.sem("mask_ready")
        x_ready, sims_ready, chosen, exp_ready = (s.sem(n) for n in ("x_ready", "sims_ready", "chosen", "exp_ready"))
        row_ready, waited = s.sem("row_ready"), s.sem("waited")
        gathered = [s.sem(f"gathered{b}") for b in range(2)]
        weighed, steps_v, steps_l = s.sem("weighed"), s.sem("steps_v"), s.sem("steps_l")
        q_done, q_ready, k_turned, k_ready = (s.sem(n) for n in ("q_done", "q_ready", "k_turned", "k_ready"))
        scored, lowered, raised, inverted = (s.sem(n) for n in ("scored", "lowered", "raised", "inverted"))
        normed, p_turned, p_ready, o_done = (s.sem(n) for n in ("normed", "p_turned", "p_ready", "o_done"))
        o_ready, out_ready, added, waited_v = (s.sem(n) for n in ("o_ready", "out_ready", "added", "waited_v"))
        block = s.block()
        table = A["memory"]

        @block.sync
        def _(sp):
            for dst, src in ((wpkT[:], A["L1_ffn_Wq_pk"]), (keysT[:], A["L1_ffn_pk_keys"]), (wq[:], A["L1_ffn_Wq"]),
                             (wo[:], A["L1_ffn_Wo"])):
                sp.dma_start(dst, src).then_inc(loads, 16)

        @block.gpsimd
        def _(pool):
            nc.gpsimd.iota(ramp_i[:], pattern=[[1, CAND]], base=0, channel_multiplier=0).then_inc(ramp_ready, 1)
            pool.wait_ge(mask_zero, 1)
            for n, start in enumerate((0, TP + TP)):
                part = mask[:, start:start + TP]
                nc.gpsimd.affine_select(out=part, in_=part, compare_op=ALU.is_ge, fill=-3e38, base=0,
                                        pattern=[[-1, TP]], channel_multiplier=1).then_inc(mask_ready, 1)
                pool.wait_ge(mask_ready, n + 1)
            with pool.Fori(0, B) as b:
                for e in range(2):
                    for head in range(HEADS):
                        unit = 2 * HEADS * b + HEADS * e + head
                        buf = head % 2
                        pool.wait_ge(row_ready, unit + 1)
                        pool.wait_ge(weighed, unit + 1)
                        pool.sem_inc(waited, 1)
                        for k in range(TOP):
                            nc.gpsimd.indirect_dma_start(
                                out=rows[:, buf, k, :], out_offset=None, in_=table,
                                in_offset=bass.IndirectOffsetOnAxis(ap=row[:, e, head, k:k + 1], axis=0)) \
                                .then_inc(gathered[buf], 16)

        @block.vector
        def _(dve):
            def tile_of(b, e):
                return 2 * b + e

            def choose(j, e, head, st):
                if head == 0:
                    dve.wait_ge(sims_ready, j + 1)
                for p in range(2):
                    mine = sims[0:TP, p, KEYS * head:KEYS * head + KEYS]
                    vals = best[p][:, 0]
                    dve.sem_inc(waited_v, 1)
                    st.then(nc.vector.max(out=vals[:, 0:8], in_=mine))
                    dve.sem_inc(waited_v, 1)
                    st.done(nc.vector.max_index(out=place[:, p, 0:8], in_max=vals[:, 0:8], in_values=mine))
                    st.then(nc.vector.match_replace(out=left[:], in_to_replace=vals[:, 0:8], in_values=mine,
                                                    imm_value=-3e38))
                    dve.sem_inc(waited_v, 1)
                    st.then(nc.vector.max(out=vals[:, 8:16], in_=left[:]))
                    dve.sem_inc(waited_v, 1)
                    st.then(nc.vector.max_index(out=place[:, p, 8:16], in_max=vals[:, 8:16], in_values=left[:]))
                st.done(nc.vector.tensor_scalar(best[0][:, 1], place[:, 0], float(NUM_KV * head), None, ALU.add))
                st.then(nc.vector.tensor_scalar(best[1][:, 1], place[:, 1], float(KEYS), None, ALU.mult))
                start = 0
                for r, n in enumerate(RUNS):
                    st.done(nc.vector.tensor_tensor(cand[:, :, start:start + n], best[1][:, :, 0:n],
                                                    bc(best[0][:, :, r:r + 1], [TP, 2, n]), ALU.add))
                    start += n
                st.then(nc.vector.tensor_tensor(cand[:, :, start:CAND], best[0][:, :, 8:16],
                                                bc(best[1][:, :, 0:1], [TP, 2, 8]), ALU.add))
                top = final[:, e, head]
                dve.sem_inc(waited_v, 1)
                st.then(nc.vector.max(out=top[:, 0:8], in_=cand[:, 0]))
                dve.sem_inc(waited_v, 1)
                st.done(nc.vector.max_index(out=at[:, 0:8], in_max=top[:, 0:8], in_values=cand[:, 0]))
                st.then(nc.vector.match_replace(out=cand_left[:], in_to_replace=top[:, 0:8], in_values=cand[:, 0],
                                                imm_value=-3e38))
                dve.sem_inc(waited_v, 1)
                st.then(nc.vector.max(out=top[:, 8:16], in_=cand_left[:]))
                dve.sem_inc(waited_v, 1)
                st.done(nc.vector.max_index(out=at[:, 8:16], in_max=top[:, 8:16], in_values=cand_left[:]))
                nc.vector.tensor_scalar(lowest[:, e, head:head + 1], top[:, 0:1], -1.0, None,
                                        ALU.mult).then_inc(chosen, 1)
                dve.wait_ge(st.sem, st.base + st.n)
                st.then(nc.vector.tensor_copy(atf[:], at[:]))
                st.then(nc.vector.tensor_tensor(hot[:], bc(ramp[:].unsqueeze(1), [TP, TOP, CAND]),
                                                bc(atf[:].unsqueeze(2), [TP, TOP, CAND]), ALU.is_equal))
                st.then(nc.vector.tensor_tensor(hot[:], hot[:], bc(cand[:, 1].unsqueeze(1), [TP, TOP, CAND]), ALU.mult))
                st.then(nc.vector.tensor_reduce(rowf[:], hot[:], AX.X, ALU.add))
                nc.vector.tensor_copy(row[:, e, head, :], rowf[:]).then_inc(row_ready, 1)

            def weigh(j, e, head, st):
                unit = HEADS * j + head
                buf = head % 2
                w = weight[:, e, head]
                dve.wait_ge(exp_ready, unit + 1)
                st.then(nc.vector.reciprocal(total[:, e, head:head + 1], total[:, e, head:head + 1]))
                st.then(nc.vector.tensor_scalar(w, w, total[:, e, head:head + 1], None, ALU.mult))
                dve.wait_ge(gathered[buf], 256 * (HEADS // 2 * j + head // 2 + 1))
                st.then(nc.vector.tensor_tensor(rows[:, buf], rows[:, buf], bc(w.unsqueeze(2), [TP, TOP, 2 * D]),
                                                ALU.mult))
                if head == 0 and e == 0:
                    dve.wait_ge(k_ready, 3 * now[0])
                nc.vector.tensor_reduce(kv[:, :, e, head, :], rows[:, buf].rearrange("p k (n d) -> p n d k", n=2),
                                        AX.X, ALU.add).then_inc(weighed, 1)
                dve.wait_ge(weighed, unit + 3)

            def invert(b, head, st):
                dve.wait_ge(raised, 2 * (HEADS * b + head) + 2)
                nc.vector.reciprocal(norm[:, head % 2], norm[:, head % 2]).then_inc(inverted, 1)

            def lower(b, head, st):
                dve.wait_ge(scored, HEADS * b + head + 1)
                mine = seen[:, head % 2]
                st.then(nc.vector.tensor_tensor(mine, score[0:TP, 0:SEEN], mask[:], ALU.add))
                st.done(nc.vector.tensor_reduce(neg[:, head % 2, 0:1], mine[:, 0:TP], AX.X, ALU.max))
                st.then(nc.vector.tensor_reduce(neg[:, head % 2, 1:2], mine[:, TP:SEEN], AX.X, ALU.max))
                nc.vector.tensor_scalar(neg[:, head % 2], neg[:, head % 2], -1.0, None, ALU.mult).then_inc(lowered, 1)

            def add_out(b):
                dve.wait_ge(out_ready, b + 1)
                part = g.h[:, bass.ds(2 * b, 2), :]
                nc.vector.tensor_tensor(part, part, out[0:TP, 0:2 * C].rearrange("p (j c) -> p j c", j=2),
                                        ALU.add).then_inc(added, 1)

            def body(b, attend=True, more=True, st=None):
                now[0] = b
                for e in range(2):
                    if attend and e == 1:
                        invert(b - 1, HEADS - 1, st)
                    for head in range(HEADS):
                        if e == 0 or more:
                            choose(tile_of(b, e) + 1, 1 - e, head, st)
                        weigh(tile_of(b, e), e, head, st)
                        if attend and e == 0:
                            if head:
                                invert(b - 1, head - 1, st)
                            lower(b - 1, head, st)
                    if attend and e == 1:
                        add_out(b - 1)

            now = [0]
            dve.wait_ge(folded, 1)
            nc.vector.tensor_copy(wsim[:], sims[0:C, :, :]).then_inc(folded, 1)
            nc.vector.memset(mask[:], 0.0).then_inc(mask_zero, 1)
            dve.sem_inc(weighed, 2)
            dve.wait_ge(ramp_ready, 1)
            st = Steps(dve, steps_v)
            st.then(nc.vector.tensor_copy(ramp[:], ramp_i[:]))
            dve.wait_ge(mask_ready, 2)
            for head in range(HEADS):
                choose(0, 0, head, st)
            body(0, attend=False, st=st)
            with dve.Fori(1, B - 1) as b:
                loop = Steps(dve, steps_l, BODY_STEPS * (b - 1))
                body(b, st=loop)
                assert loop.n == BODY_STEPS, loop.n
            body(B - 1, more=False, st=st)
            for head in range(HEADS):
                if head:
                    invert(B - 1, head - 1, st)
                lower(B - 1, head, st)
            invert(B - 1, HEADS - 1, st)
            add_out(B - 1)

        @block.scalar
        def _(act):
            def stage_x(j, buf):
                nc.scalar.copy(x[:, buf, :], g.xT[0:C, bass.ds(TP * j, TP)]).then_inc(x_ready, 1)

            def weights(j, e, head):
                act.wait_ge(chosen, HEADS * j + head + 1)
                nc.scalar.activation(weight[:, e, head], final[:, e, head], ACT.Exp, bias=lowest[:, e, head:head + 1],
                                     accum_out=total[:, e, head:head + 1]).then_inc(exp_ready, 1)

            def attend(b, head):
                n = HEADS * b + head
                act.wait_ge(lowered, n + 1)
                mine = seen[:, head % 2]
                for i, cols in enumerate((slice(0, TP), slice(TP, SEEN))):
                    nc.scalar.activation(mine[:, cols], mine[:, cols], ACT.Exp, bias=neg[:, head % 2, i:i + 1],
                                         accum_out=norm[:, head % 2, i:i + 1]).then_inc(raised, 1)
                act.wait_ge(inverted, n + 1)
                for i, cols in enumerate((slice(0, TP), slice(TP, SEEN))):
                    nc.scalar.activation(mine[:, cols], mine[:, cols], ACT.Copy,
                                         scale=norm[:, head % 2, i:i + 1]).then_inc(normed, 1)
                act.wait_ge(p_turned, n + 1)
                nc.scalar.copy(pT[:, head % 2], turned[0:TP, 0:SEEN]).then_inc(p_ready, 1)
                act.wait_ge(o_done, n + 1)
                nc.scalar.copy(oT[:, head % 2], outT[0:D, 0:T]).then_inc(o_ready, 1)

            def body(b, attending=True, more=True):
                stage_x(2 * b + 1, 1)
                for head in range(HEADS):
                    weights(2 * b + 1, 1, head)
                    if attending:
                        attend(b - 1, head)
                for bank in range(2):
                    act.wait_ge(q_done, 2 * b + bank + 1)
                    nc.scalar.mul(q[:, 2 * bank:2 * bank + 2].rearrange("p h t -> p (h t)"), qbank[:, bank, 0:2 * T],
                                  D ** -0.5).then_inc(q_ready, 1)
                if more:
                    stage_x(2 * b + 2, 0)
                    for head in range(HEADS):
                        weights(2 * b + 2, 0, head)
                for e, src in enumerate((turned, outT)):
                    act.wait_ge(k_turned, 2 * b + e + 1)
                    nc.scalar.copy(kT[:, :, TP * e:TP * e + TP], src[:, 0:4 * TP].rearrange("p (n t) -> p n t", n=4)) \
                        .then_inc(k_ready, 1)
                nc.scalar.copy(v[:], kv[:, 1]).then_inc(k_ready, 1)

            stage_x(0, 0)
            for head in range(HEADS):
                weights(0, 0, head)
            body(0, attending=False)
            with act.Fori(1, B - 1) as b:
                body(b)
            body(B - 1, more=False)
            for head in range(HEADS):
                attend(B - 1, head)

        @block.tensor
        def _(pe):
            def find(j, buf):
                pe.wait_ge(x_ready, j + 1)
                pe.wait_ge(row_ready, HEADS * j)
                for p in range(2):
                    ins = nc.tensor.matmul(sims[0:TP, p, :], x[:, buf, :], wsim[:, p, :], start=True, stop=True)
                ins.then_inc(sims_ready, 1)

            def attend_scores(b, head):
                n = HEADS * b + head
                if head == 0:
                    pe.wait_ge(k_ready, 3 * b + 3)
                    pe.wait_ge(q_ready, 2 * b + 2)
                pe.wait_ge(lowered, n)
                r = slice(D * (head % 2), D * (head % 2) + D)
                nc.tensor.matmul(score[0:TP, 0:TP], q[r, head // 2, 0:TP], kT[r, head // 2, 0:TP], start=True, stop=True)
                nc.tensor.matmul(score[0:TP, TP:SEEN], q[r, head // 2, TP:T], kT[r, head // 2, :], start=True,
                                 stop=True).then_inc(scored, 1)

            def attend_rest(b, head):
                n = HEADS * b + head
                pe.wait_ge(normed, 2 * n + 2)
                pe.wait_ge(p_ready, n)
                probs = seen[:, head % 2]
                for i in range(3):
                    ins = nc.tensor.transpose(turned[0:TP, TP * i:TP * i + TP], probs[:, TP * i:TP * i + TP],
                                              g.ident[0:TP, 0:TP])
                ins.then_inc(p_turned, 1)
                pe.wait_ge(p_ready, n + 1)
                pe.wait_ge(o_ready, n)
                nc.tensor.matmul(outT[0:D, 0:T], v[:, 0, head], pT[:, head % 2, 0:T], start=True, stop=False,
                                 skip_group_check=True)
                nc.tensor.matmul(outT[0:D, TP:T], v[:, 1, head], pT[:, head % 2, T:SEEN], start=False, stop=True,
                                 skip_group_check=True).then_inc(o_done, 1)
                pe.wait_ge(o_ready, n + 1)
                if head == 0:
                    pe.wait_ge(added, b)
                for i in range(2):
                    ins = nc.tensor.matmul(out[0:TP, C * i:C * i + C], oT[:, head % 2, TP * i:TP * i + TP], wo[:, head],
                                           start=(head == 0 and i == 0), stop=(head == HEADS - 1),
                                           skip_group_check=True)
                if head == HEADS - 1:
                    ins.then_inc(out_ready, 1)

            def attend(b):
                for head in range(HEADS):
                    attend_scores(b, head)
                    if head:
                        attend_rest(b, head - 1)
                attend_rest(b, HEADS - 1)

            def body(b, attending=True, more=True):
                find(2 * b + 1, 1)
                if attending:
                    attend(b - 1)
                pe.wait_ge(q_ready, 2 * b)
                for pair in range(PAIRS):
                    ins = nc.tensor.matmul(qbank[:, pair // 2, T * (pair % 2):T * (pair % 2) + T],
                                           wq[:, P * pair:P * pair + P], x[:].rearrange("c e t -> c (e t)"),
                                           start=True, stop=True)
                    if pair % 2:
                        ins.then_inc(q_done, 1)
                if more:
                    find(2 * b + 2, 0)
                for e, dst in enumerate((turned, outT)):
                    pe.wait_ge(weighed, 2 + HEADS * (2 * b + e + 1))
                    for pair in range(PAIRS):
                        ins = nc.tensor.transpose(dst[:, TP * pair:TP * pair + TP],
                                                  kv[:, 0, e, 2 * pair:2 * pair + 2, :].rearrange("p h d -> p (h d)"),
                                                  g.ident[0:TP, 0:TP])
                    ins.then_inc(k_turned, 1)

            pe.wait_ge(loads, 16 * 4)
            for n in range(2 * HEADS):
                ins = nc.tensor.matmul(sims[0:C, n // HEADS, KEYS * (n % HEADS):KEYS * (n % HEADS) + KEYS], wpkT[:, n],
                                       keysT[:, n], start=True, stop=True)
            ins.then_inc(folded, 1)
            pe.wait_ge(folded, 2)
            find(0, 0)
            body(0, attending=False)
            with pe.Fori(1, B - 1) as b:
                body(b)
            body(B - 1, more=False)
            attend(B - 1)


def rnn(nc, g, A):
    HID, KC, S = 256, 2, 11
    CHUNKS = T // S
    with Stage(nc, "rc") as s:
        wi0, more0 = s.sb("wi0", [C + 1, HID]), s.sb("more0", [C + 1, HID])
        wh0, wi1, wh1 = (s.sb(n, [P, KC, HID]) for n in ("wh0", "wi1", "wh1"))
        bi1, more1 = s.sb("bi1", [1, HID]), s.sb("more1", [1, HID])
        fc, fc_b, ones = s.sb("fc", [P, KC, C]), s.sb("fc_b", [1, C]), s.sb("ones", [1, S * B])
        h0 = s.sb("h0", [P, 2, KC, S, B])
        h1 = s.sb("h1", [P, KC, B, T])
        sum0, sum1 = s.ps("sum0", [P, 2, BANK]), s.ps("sum1", [P, 2, BANK])
        final = s.ps("final", [TP, 4, BANK])
        loads, ready = s.sem("loads"), s.sem("ready")
        summed0, summed1, tanh0, tanh1, out_ready = (s.sem(n) for n in ("summed0", "summed1", "tanh0", "tanh1", "out_ready"))
        block = s.block()
        x = g.xT[:].rearrange("c (b t) -> c t b", b=B)

        @block.sync
        def _(sp):
            for dst, name in ((wi0[0:C, :], "W_ih_0"), (wi0[C:C + 1, :], "b_ih_0"), (more0[C:C + 1, :], "b_hh_0"),
                              (wh0[:], "W_hh_0"), (wi1[:], "W_ih_1"), (wh1[:], "W_hh_1"), (bi1[:], "b_ih_1"),
                              (more1[:], "b_hh_1"), (fc[:], "fc_w"), (fc_b[:], "fc_b")):
                sp.dma_start(dst, A["L2_attn_" + name]).then_inc(loads, 16)

        @block.vector
        def _(dve):
            dve.wait_ge(loads, 16 * 10)
            nc.vector.memset(ones[:], 1.0).then_inc(ready, 1)
            nc.vector.tensor_tensor(wi0[C:C + 1, :], wi0[C:C + 1, :], more0[C:C + 1, :], ALU.add).then_inc(ready, 1)
            nc.vector.tensor_tensor(bi1[:], bi1[:], more1[:], ALU.add).then_inc(ready, 1)
            for q in range(4):
                dve.wait_ge(out_ready, q + 1)
                part = g.h[:, 8 * q:8 * q + 8, :]
                nc.vector.tensor_tensor(part, part, final[:, q, :].rearrange("p (j c) -> p j c", j=8), ALU.add)

        @block.tensor
        def _(pe):
            def columns(bank, m, t=None):
                cols = bank[:, S * B * m:S * B * m + S * B]
                return cols if t is None else cols[:, B * t:B * t + B]

            def input0(c, buf):
                for m in range(KC):
                    ins = nc.tensor.matmul(columns(sum0[:, buf], m), wi0[:, P * m:P * m + P], x[:, bass.ds(S * c, S), :],
                                           start=(m == 0), stop=False, skip_group_check=True)
                return ins

            def input1(c, buf):
                pe.wait_ge(tanh0, S * c + S)
                for m in range(KC):
                    nc.tensor.matmul(columns(sum1[:, buf], m), bi1[:, P * m:P * m + P], ones[:], start=(m == 0),
                                     stop=False, skip_group_check=True)
                    for k in range(KC):
                        ins = nc.tensor.matmul(columns(sum1[:, buf], m), wi1[:, k, P * m:P * m + P],
                                               h0[:, buf, k].rearrange("p s b -> p (s b)"), start=False, stop=False,
                                               skip_group_check=True)
                return ins

            def step(bank, w, t, last):
                for m in range(KC):
                    for k in range(KC):
                        ins = nc.tensor.matmul(columns(bank, m, t), w[:, k, P * m:P * m + P], last(k), start=False,
                                               stop=(k == KC - 1), skip_group_check=True)
                return ins

            def turn(c, buf, has0=True, has1=True, start0=False, start1=False, more=True):
                for t in range(S):
                    if has0 and not (start0 and t == 0):
                        pe.wait_ge(tanh0, S * c + t)
                        prev = (buf, t - 1) if t else (1 - buf, S - 1)
                        step(sum0[:, buf], wh0, t, lambda k: h0[:, prev[0], k, prev[1]]).then_inc(summed0, 1)
                    if has1:
                        if t == 0:
                            ins = input1(c - 1, 1 - buf)
                            if start1:
                                ins.then_inc(summed1, 1)
                        if not (start1 and t == 0):
                            pe.wait_ge(tanh1, S * (c - 1) + t)
                            step(sum1[:, 1 - buf], wh1, t,
                                 lambda k: h1[:, k, :, bass.ds(S * (c - 1) + t - 1, 1)]
                                 .rearrange("p b o -> p (b o)")).then_inc(summed1, 1)
                    if t == S // 2 and has0 and more:
                        input0(c + 1, 1 - buf)

            pe.wait_ge(ready, 3)
            input0(0, 0).then_inc(summed0, 1)
            turn(0, 0, has1=False, start0=True)
            turn(1, 1, start1=True)
            with pe.Fori(1, CHUNKS // 2 - 1) as i:
                turn(2 * i, 0)
                turn(2 * i + 1, 1)
            turn(CHUNKS - 2, 0)
            turn(CHUNKS - 1, 1, more=False)
            turn(CHUNKS, 0, has0=False)
            pe.wait_ge(tanh1, T)
            for j in range(NT):
                out = final[:, j // 8, C * (j % 8):C * (j % 8) + C]
                nc.tensor.matmul(out, ones[:, 0:TP], fc_b[:], start=True, stop=False)
                for k in range(KC):
                    ins = nc.tensor.matmul(out, h1[:, k, j // 2, TP * (j % 2):TP * (j % 2) + TP], fc[:, k],
                                           start=False, stop=(k == KC - 1))
                if j % 8 == 7:
                    ins.then_inc(out_ready, 1)

        @block.scalar
        def _(act):
            def turn(c, buf, has0=True, has1=True):
                for t in range(S):
                    cols = slice(B * t, B * t + B)
                    if has0:
                        act.wait_ge(summed0, S * c + t + 1)
                        nc.scalar.activation(h0[:, buf, :, t], sum0[:, buf, 0:KC * S * B].rearrange(
                            "p (m n) -> p m n", m=KC)[:, :, cols], ACT.Tanh).then_inc(tanh0, 1)
                    if has1:
                        act.wait_ge(summed1, S * (c - 1) + t + 1)
                        nc.scalar.activation(
                            h1[:, :, :, bass.ds(S * (c - 1) + t, 1)].rearrange("p m b o -> p m (b o)"),
                            sum1[:, 1 - buf, 0:KC * S * B].rearrange("p (m n) -> p m n", m=KC)[:, :, cols],
                            ACT.Tanh).then_inc(tanh1, 1)

            turn(0, 0, has1=False)
            turn(1, 1)
            with act.Fori(1, CHUNKS // 2) as i:
                turn(2 * i, 0)
                turn(2 * i + 1, 1)
            turn(CHUNKS, 0, has0=False)


def experts(nc, g, A):
    E, HID = 8, 128
    with Stage(nc, "ex") as s:
        gate = s.sb("gate", [TP, NT, E])
        w1, w2 = s.sb("w1", [C + 1, E * HID]), s.sb("w2", [HID, E, C])
        route(nc, g, "er", A["L2_ffn_Wg"], (A["L2_ffn_bg"], A["L2_ffn_bias"]), gate, E)
        run_experts(nc, g, "ee", gate, w1, w2, A["L2_ffn_b2"], E, 1, ACT.Relu,
                    ((w1[0:C, :], A["L2_ffn_W1"]), (w1[C:C + 1, :], A["L2_ffn_b1"]), (w2[:], A["L2_ffn_W2"])))


def sigmoid_attention(nc, g, A):
    HEADS, F = 8, C
    SCALE = float(F) ** 0.5
    PER = 2 * HEADS
    with Stage(nc, "sa") as s:
        wqT, wkT, wvT = (s.sb(n, [F, HEADS, C]) for n in ("wqT", "wkT", "wvT"))
        wo = s.sb("wo", [F, HEADS, C])
        wqk, wvo = s.sb("wqk", [C, HEADS, C]), s.sb("wvo", [C, HEADS, C])
        x = s.sb("x", [2 * C, 2, T])
        v, q = s.sb("v", [TP, 2, 2, HEADS * C]), s.sb("q", [2 * C, 2, HEADS // 2, T])
        probs = s.sb("probs", [TP, 2, 2, T])
        banks = s.ps("banks", [P, 8, BANK])
        loads, folded, folded_out = s.sem("loads"), s.sem("folded"), s.sem("folded_out")
        x_ready, v_done, v_ready = s.sem("x_ready"), s.sem("v_done"), s.sem("v_ready")
        q_done, q_ready, scored, squashed = s.sem("q_done"), s.sem("q_ready"), s.sem("scored"), s.sem("squashed")
        weighted, added = s.sem("weighted"), s.sem("added")
        block = s.block()

        @block.sync
        def _(sp):
            for dst, name in ((wqT, "Wq"), (wkT, "Wk"), (wvT, "Wv"), (wo, "Wo")):
                sp.dma_start(dst[:], A["L3_attn_" + name]).then_inc(loads, 16)

        @block.tensor
        def _(pe):
            pe.wait_ge(loads, 16 * 4)
            for n, (a, b) in enumerate(((wqT, wkT), (wvT, wo))):
                for head in range(HEADS):
                    ins = nc.tensor.matmul(banks[0:C, n, C * head:C * head + C], a[:, head], b[:, head],
                                           start=True, stop=True)
                ins.then_inc(folded, 1)

            def project(b, buf):
                pe.wait_ge(x_ready, 2 * b + 2)
                pe.wait_ge(v_ready, b + 1)
                for half in range(2):
                    ins = nc.tensor.matmul(banks[0:TP, half, :], x[0:C, buf, TP * half:TP * half + TP],
                                           wvo[:].rearrange("c h o -> c (h o)"), start=True, stop=True)
                ins.then_inc(v_done, 1)
                for pair in range(HEADS // 2):
                    pe.wait_ge(q_ready, 4 * b + pair + 1)
                    nc.tensor.matmul(banks[:, 2 + pair % 2, 0:T],
                                     wqk[:, 2 * pair:2 * pair + 2].rearrange("c h o -> c (h o)"),
                                     x[0:C, buf, :], start=True, stop=True).then_inc(q_done, 1)

            def attend(b, buf, more):
                for head in range(HEADS + 1):
                    if head < HEADS:
                        if head % 2 == 0:
                            pe.wait_ge(q_ready, 4 * b + head // 2 + 3)
                        pe.wait_ge(squashed, 8 * b + head + 1)
                        rows = slice(C * (head % 2), C * (head % 2) + C)
                        for half in range(2):
                            ins = nc.tensor.matmul(banks[0:TP, 4 + head % 2, T * half:T * half + T],
                                                   x[rows, buf, TP * half:TP * half + TP], q[rows, buf, head // 2],
                                                   start=True, stop=True)
                        ins.then_inc(scored, 1)
                    if head:
                        hd = head - 1
                        if hd == 0:
                            pe.wait_ge(v_ready, b + 2)
                            pe.wait_ge(added, b + 1)
                        pe.wait_ge(squashed, 8 * b + hd + 3)
                        for tile in range(2):
                            for u in range(2):
                                ins = nc.tensor.matmul(
                                    banks[0:TP, 6, C * tile:C * tile + C],
                                    probs[:, hd % 2, u, TP * tile:TP * tile + TP], v[:, buf, u, C * hd:C * hd + C],
                                    start=(hd == 0 and tile == 0 and u == 0), stop=(hd == HEADS - 1 and u == 1),
                                    skip_group_check=True)
                        ins.then_inc(weighted, 1)
                    if head == 1 and more:
                        project(b + 1, 1 - buf)

            pe.wait_ge(folded_out, 2)
            project(0, 0)
            with pe.Fori(0, B // 2 - 1) as i:
                attend(2 * i, 0, True)
                attend(2 * i + 1, 1, True)
            attend(B - 2, 0, True)
            attend(B - 1, 1, False)

        @block.scalar
        def _(act):
            act.sem_inc(squashed, 2)
            with act.Fori(0, B) as b:
                for head in range(HEADS):
                    act.wait_ge(scored, 8 * b + head + 1)
                    act.wait_ge(weighted, 8 * b + head + 1)
                    nc.scalar.activation(probs[:, head % 2].rearrange("p u t -> p (u t)"),
                                         banks[0:TP, 4 + head % 2, 0:2 * T], ACT.Sigmoid,
                                         scale=SCALE).then_inc(squashed, 1)

        @block.vector
        def _(dve):
            dve.wait_ge(folded, 1)
            nc.vector.tensor_copy(wqk[:].rearrange("c h o -> c (h o)"), banks[0:C, 0, :]).then_inc(folded_out, 1)
            dve.wait_ge(folded, 2)
            nc.vector.tensor_copy(wvo[:].rearrange("c h o -> c (h o)"), banks[0:C, 1, :]).then_inc(folded_out, 1)
            dve.sem_inc(v_ready, 1)
            dve.sem_inc(q_ready, 2)
            dve.sem_inc(added, 1)
            dve.sem_inc(weighted, 2)

            def load(b, buf):
                for e in range(2):
                    nc.vector.tensor_copy(x[C * e:C * e + C, buf, :], g.xT[0:C, bass.ds(T * b, T)]).then_inc(x_ready, 1)

            def take(b, buf):
                dve.wait_ge(v_done, b + 1)
                nc.vector.tensor_copy(v[:, buf], banks[0:TP, 0:2, :]).then_inc(v_ready, 1)
                for pair in range(HEADS // 2):
                    dve.wait_ge(q_done, 4 * b + pair + 1)
                    nc.vector.tensor_copy(q[:, buf, pair, :], banks[:, 2 + pair % 2, 0:T]).then_inc(q_ready, 1)

            def add(b):
                dve.wait_ge(weighted, 8 * b + 8 + 2)
                part = g.h[:, bass.ds(2 * b, 2), :]
                nc.vector.scalar_tensor_tensor(out=part, in0=banks[0:TP, 6, 0:2 * C].rearrange("p (j c) -> p j c", j=2),
                                               scalar=0.0, in1=part, op0=ALU.max, op1=ALU.add).then_inc(added, 1)

            load(0, 0)
            take(0, 0)
            with dve.Fori(0, B // 2 - 1) as i:
                for e in range(2):
                    dve.wait_ge(added, 2 * i + e + 1)
                    load(2 * i + e + 1, 1 - e)
                    take(2 * i + e + 1, 1 - e)
                    add(2 * i + e)
            dve.wait_ge(added, B - 1)
            load(B - 1, 1)
            take(B - 1, 1)
            add(B - 2)
            add(B - 1)


def routed_experts(nc, g, A):
    E, HID = 8, 256
    with Stage(nc, "re") as s:
        gate = s.sb("gate", [TP, NT, E])
        w1, w2 = s.sb("w1", [C + 1, E * HID]), s.sb("w2", [P, 2 * E, C])
        xn = s.sb("xn", [TP, NT, C])
        normalise(nc, g, "rn", kept=xn)
        route(nc, g, "rr", A["L3_ffn_Wr"], (A["L3_ffn_br"],), gate, E)
        normalise(nc, g, "rm", src=xn)
        with Stage(nc, "rf") as f:
            plain, b1 = f.sb("plain", [C, E, HID]), f.sb("b1", [C + 1, E * HID])
            gain, shift = f.sb("gain", [C, E]), f.sb("shift", [C, E])
            bias = f.ps("bias", [1, 4, BANK])
            loads, shifted = f.sem("loads"), f.sem("shifted")
            block = f.block()

            @block.sync
            def _(sp):
                for dst, name in ((plain[:], "W1"), (gain[:], "ln_g"), (shift[:], "ln_b"), (b1[C:C + 1, :], "b1")):
                    sp.dma_start(dst, A["L3_ffn_" + name]).then_inc(loads, 16)

            @block.tensor
            def _(pe):
                pe.wait_ge(loads, 16 * 4)
                for e in range(E):
                    nc.tensor.matmul(bias[:, e // 2, HID * (e % 2):HID * (e % 2) + HID], shift[:, e:e + 1],
                                     plain[:, e], start=True, stop=True).then_inc(shifted, 1)

            @block.vector
            def _(dve):
                dve.wait_ge(loads, 16 * 4)
                for e in range(E):
                    nc.vector.tensor_scalar(w1[0:C, HID * e:HID * e + HID], plain[:, e], gain[:, e:e + 1], None, ALU.mult)
                dve.wait_ge(shifted, E)
                nc.vector.tensor_tensor(w1[C:C + 1, :], bias[:].rearrange("p q n -> p (q n)"), b1[C:C + 1, :], ALU.add)

        run_experts(nc, g, "ru", gate, w1, w2, A["L3_ffn_b2"], E, 2, ACT.Gelu, ((w2[:], A["L3_ffn_W2"]),))


def constants(nc, g, A):
    with Stage(nc, "co") as s:
        cleared, filled = s.sem("cleared"), s.sem("filled")
        block = s.block()

        @block.gpsimd
        def _(pool):
            nc.gpsimd.memset(g.ident[:], 0.0).then_inc(cleared, 1)
            pool.wait_ge(cleared, 1)
            nc.gpsimd.affine_select(out=g.ident[:], in_=g.ident[:], compare_op=ALU.not_equal, fill=1.0,
                                    base=0, pattern=[[-1, P]], channel_multiplier=1)

        @block.vector
        def _(dve):
            nc.vector.memset(g.xT[C:C + 1, :], 1.0)


def store(nc, g, out):
    with Stage(nc, "st") as s:
        stored = s.sem("stored")
        block = s.block()

        @block.sync
        def _(sp):
            sp.dma_start(out.rearrange("b (t p) c -> p (b t) c", p=TP), g.h[:]).then_inc(stored, 16)
            sp.wait_ge(stored, 16)


class Held:

    def __init__(self, nc, ctx):
        self.h = ctx.enter_context(nc.sbuf_tensor("h", [TP, NT, C], F32))
        self.xT = ctx.enter_context(nc.sbuf_tensor("xT", [C + 1, N], F32))
        self.src_table = nc.dram_tensor("src_table", (N, 20), F32).ap()
        self.dst_table = nc.dram_tensor("dst_table", (NT * P, 8), F32).ap()
        self.ident = ctx.enter_context(nc.sbuf_tensor("ident", [P, P], F32))


def layouts(I):
    import numpy as np
    x = np.asarray(I["x"])
    out = {k: np.asarray(v) for k, v in I.items() if k != "x"}
    out["xT"] = x.reshape(2, B // 2, T_IN, C).transpose(0, 3, 1, 2).reshape(P, B // 2, T_IN)
    for k in ("L0_attn_in_proj_w", "L0_attn_x_proj_w", "L0_attn_x_proj_w_b", "L0_attn_dt_proj_w",
              "L0_attn_dt_proj_w_b", "L0_attn_out_proj_w"):
        out[k] = np.ascontiguousarray(out[k].T)
    for k in ("Wq", "Wk", "Wv"):
        out["L3_attn_" + k] = out["L3_attn_" + k].reshape(C, C, 8).transpose(1, 2, 0)
    out["L3_attn_Wo"] = out["L3_attn_Wo"].reshape(C, 8, C)
    for k in ("L0_ffn", "L2_ffn", "L3_ffn"):
        e, _, hid = out[k + "_W1"].shape
        out[k + "_W1"] = out[k + "_W1"].transpose(1, 0, 2).reshape(C, e * hid)
        out[k + "_W2"] = out[k + "_W2"].reshape(e * hid // P, P, C).transpose(1, 0, 2)
        out[k + "_b1"] = out[k + "_b1"].reshape(1, e * hid)
        out[k + "_b2"] = out[k + "_b2"].reshape(1, e * C)
    out["L3_ffn_W1"] = out["L3_ffn_W1"].reshape(C, 8, 256)
    out["L3_ffn_ln_g"], out["L3_ffn_ln_b"] = out["L3_ffn_ln_g"].T, out["L3_ffn_ln_b"].T
    for k in ("W_ih_0", "W_hh_0", "W_ih_1", "W_hh_1", "fc_w"):
        w = out["L2_attn_" + k].T
        out["L2_attn_" + k] = w if k == "W_ih_0" else w.reshape(2, P, w.shape[1]).transpose(1, 0, 2)
    for k in ("b_ih_0", "b_hh_0", "b_ih_1", "b_hh_1", "fc_b"):
        out["L2_attn_" + k] = out["L2_attn_" + k].reshape(1, -1)
    fold = np.zeros((16, 24), np.float32)
    fold[:, 0:16] = np.eye(16, dtype=np.float32)
    for head in range(4):
        fold[4 * head:4 * head + 4, 16 + head] = out["L0_ffn_att_src"][head]
        fold[4 * head:4 * head + 4, 20 + head] = out["L0_ffn_att_dst"][head]
    out["fold"] = fold
    out["L1_ffn_Wq_pk"] = out["L1_ffn_Wq_pk"].reshape(C, 16, 32).transpose(2, 1, 0)
    out["L1_ffn_pk_keys"] = out["L1_ffn_pk_keys"].transpose(3, 0, 2, 1).reshape(32, 16, 64)
    out["L1_ffn_Wo"] = out["L1_ffn_Wo"].reshape(8, C, C).transpose(1, 0, 2)
    out["memory"] = np.concatenate([out.pop("L1_ffn_keys_table"), out.pop("L1_ffn_values_table")], axis=1)
    after = np.zeros(TP, np.float32)
    out["time_curve"] = np.concatenate([out["L1_attn_time_w"], after])
    out["time_steps"] = np.concatenate([np.ones(2 * TP, np.float32), after])
    return out


def recycle(nc, start):
    nc.clear_and_free_semaphores(nc.allocated_since(start))
    nc.all_engine_barrier()


def audio_tower(nc, A, out):
    with ExitStack() as ctx:
        g = Held(nc, ctx)
        start = nc.snapshot_sems()
        constants(nc, g, A)
        pool_windows(nc, g, A)
        stages = (mamba, graph_experts, rwkv, memory_attention, rnn, experts, sigmoid_attention)
        for n, stage in enumerate(stages):
            normalise(nc, g, f"n{n}")
            stage(nc, g, A)
            if n % 2:
                recycle(nc, start)
        recycle(nc, start)
        routed_experts(nc, g, A)
        store(nc, g, out)


def kernel(**inputs):
    import numpy as np
    import concourse.bacc as bacc
    from concourse.bass_utils import run_bass_kernel_spmd

    nc = bacc.Bacc("TRN2", target_bir_lowering=False, num_devices=1)
    arrays, A = {}, {}
    for name, a in layouts(inputs).items():
        a = np.ascontiguousarray(a)
        arrays[f"in_{name}"] = a
        A[name] = nc.dram_tensor(f"in_{name}", a.shape, mybir.dt.from_np(a.dtype), kind="ExternalInput").ap()
    out = nc.dram_tensor("out", (B, T, C), F32, kind="ExternalOutput").ap()
    audio_tower(nc, A, out)
    return run_bass_kernel_spmd(nc, [arrays], core_ids=[0]).results[0]["out"]
```

```python
from contextlib import ExitStack

import concourse.bass as bass
from concourse import mybir

F32 = mybir.dt.float32
BF16 = mybir.dt.bfloat16
I32 = mybir.dt.int32
U32 = mybir.dt.uint32
ALU = mybir.AluOpType
ACT = mybir.ActivationFunctionType
AX = mybir.AxisListType
RMAX = bass.bass_isa.ReduceOp.max

P = 128
B = 16
T_IN = 250
WIN = 9
T = T_IN - WIN + 1
C = 64
N = B * T
TP = T // 2
NT = N // TP
GT = 4
NG = NT // GT
GC = GT * TP
BANK = 512
EPS = 1e-5


class Stage:

    def __init__(self, nc, name):
        self.nc, self.name, self.ctx = nc, name, ExitStack()

    def __enter__(self):
        self.ctx.__enter__()
        return self

    def __exit__(self, *e):
        return self.ctx.__exit__(*e)

    def sb(self, name, shape, dt=F32):
        return self.ctx.enter_context(self.nc.sbuf_tensor(f"{self.name}_{name}", shape, dt))

    def ps(self, name, shape, dt=F32):
        return self.ctx.enter_context(self.nc.psum_tensor(f"{self.name}_{name}", shape, dt))

    def sem(self, name):
        return self.nc.alloc_semaphore(f"{self.name}_{name}")

    def block(self):
        return self.ctx.enter_context(self.nc.Block())


class Steps:

    def __init__(self, eng, sem, base=0):
        self.eng, self.sem, self.base, self.n = eng, sem, base, 0

    def done(self, ins):
        self.n += 1
        ins.then_inc(self.sem, 1)

    def then(self, ins):
        self.done(ins)
        self.eng.wait_ge(self.sem, self.base + self.n)


def bc(ap, shape):
    return ap.to_broadcast(shape)


def pool_windows(nc, g, A):
    HB = B // 2
    COLS = HB * T
    with Stage(nc, "pw") as s:
        wq, wk, vv = (s.sb(n, [P, P]) for n in ("wq", "wk", "vv"))
        bias, vcol = s.sb("bias", [P, 1]), s.sb("vcol", [P, 1])
        xT = s.sb("xT", [P, HB, T_IN])
        q, k = s.sb("q", [P, HB, T_IN]), s.sb("k", [P, HB, T_IN])
        score = s.sb("score", [P, WIN, HB, T])
        work = s.sb("work", [P, 2, HB, T])
        top, den, num = (s.sb(n, [P, HB, T]) for n in ("top", "den", "num"))
        proj = s.ps("proj", [P, 8, BANK])
        loads, projected, copied = s.sem("loads"), s.sem("projected"), s.sem("copied")
        summed, squashed, scored, kept = s.sem("summed"), s.sem("squashed"), s.sem("scored"), s.sem("kept")
        shifted, raised, done, steps_v = s.sem("shifted"), s.sem("raised"), s.sem("done"), s.sem("steps_v")
        turned, steps_z, v_ready = s.sem("turned"), s.sem("steps_z"), s.sem("v_ready")
        block = s.block()

        @block.sync
        def _(sp):
            sp.wait_ge(steps_z, 3)
            sp.dma_start(xT[:], A["xT"]).then_inc(loads, 16)
            for half in range(2):
                r = slice(C * half, C * half + C)
                sp.dma_start(wq[r, r], A["L0_tok_W_qry"]).then_inc(loads, 16)
                sp.dma_start(wk[r, r], A["L0_tok_W_key"]).then_inc(loads, 16)
                sp.dma_start(vcol[r, :], A["L0_tok_v"].unsqueeze(1)).then_inc(loads, 16)
                sp.dma_start(bias[r, :], A["L0_tok_b"].unsqueeze(1)).then_inc(loads, 16)

        @block.tensor
        def _(pe):
            pe.wait_ge(loads, 16 * 9)
            for n, w in enumerate((wq, wk)):
                for c in range(4):
                    nc.tensor.matmul(proj[:, 4 * n + c, 0:2 * T_IN], w[:], xT[:, 2 * c:2 * c + 2, :],
                                     start=True, stop=True).then_inc(projected, 1)
            pe.wait_ge(v_ready, 2)
            for w in range(WIN):
                pe.wait_ge(squashed, w + 1)
                if w < 2:
                    pe.wait_ge(copied, w + 1)
                else:
                    pe.wait_ge(kept, w - 1)
                for c in range(4):
                    ins = nc.tensor.matmul(proj[:, 4 * (w % 2) + c, 0:2 * T], vv[:],
                                           work[:, w % 2, 2 * c:2 * c + 2, :], start=True, stop=True)
                ins.then_inc(scored, 1)
            pe.wait_ge(done, 1)
            pe.wait_ge(kept, WIN)
            for t in range(HB * 2):
                b, half = divmod(t, 2)
                ins = nc.tensor.transpose(proj[0:TP, t // 4, P * (t % 4):P * (t % 4) + P],
                                          num[:, b, TP * half:TP * half + TP], g.ident[:])
                if t % 4 == 3:
                    ins.then_inc(turned, 1)

        @block.scalar
        def _(act):
            for n, dst in enumerate((q, k)):
                act.wait_ge(projected, 4 * n + 4)
                nc.scalar.copy(dst[:].rearrange("p (c b) t -> p c (b t)", c=4),
                               proj[:, 4 * n:4 * n + 4, 0:2 * T_IN]).then_inc(copied, 1)
            for w in range(WIN):
                act.wait_ge(summed, w + 1)
                nc.scalar.activation(work[:, w % 2], work[:, w % 2], ACT.Tanh, bias=bias[:]).then_inc(squashed, 1)
                act.wait_ge(scored, w + 1)
                nc.scalar.copy(score[:, w].rearrange("p (c b) t -> p c (b t)", c=4),
                               proj[:, 4 * (w % 2):4 * (w % 2) + 4, 0:2 * T]).then_inc(kept, 1)
            for w in range(WIN):
                act.wait_ge(shifted, w + 1)
                nc.scalar.activation(score[:, w], score[:, w], ACT.Exp).then_inc(raised, 1)
            for bank in range(4):
                act.wait_ge(turned, bank + 1)
                for half in range(2):
                    dst = g.h[:, 32 // 2 * half + 4 * bank:32 // 2 * half + 4 * bank + 4, :]
                    src = proj[0:TP, bank, :].rearrange("p (t h c) -> p t h c", t=4, h=2)[:, :, half, :]
                    nc.scalar.copy(dst, src)

        @block.vector
        def _(dve):
            st = Steps(dve, steps_v)
            for z in (wq, wk, vv):
                nc.vector.memset(z[:], 0.0).then_inc(steps_z, 1)
            dve.wait_ge(loads, 16 * 9)
            dve.wait_ge(steps_z, 3)
            for half in range(2):
                r = slice(C * half, C * half + C)
                nc.vector.tensor_copy(vv[r, r], bc(vcol[r, :], [C, C])).then_inc(v_ready, 1)
            dve.wait_ge(copied, 2)
            for w in range(WIN):
                if w >= 2:
                    dve.wait_ge(scored, w - 1)
                nc.vector.tensor_tensor(work[:, w % 2], q[:, :, WIN // 2:WIN // 2 + T], k[:, :, w:w + T],
                                        ALU.add).then_inc(summed, 1)
            dve.wait_ge(kept, 2)
            st.then(nc.vector.tensor_tensor(top[:], score[:, 0], score[:, 1], ALU.max))
            for w in range(2, WIN):
                dve.wait_ge(kept, w + 1)
                st.then(nc.vector.tensor_tensor(top[:], top[:], score[:, w], ALU.max))
            for w in range(WIN):
                nc.vector.tensor_tensor(score[:, w], score[:, w], top[:], ALU.subtract).then_inc(shifted, 1)
            dve.wait_ge(raised, 2)
            st.done(nc.vector.tensor_tensor(den[:], score[:, 0], score[:, 1], ALU.add))
            st.then(nc.vector.tensor_tensor(num[:], score[:, 0], xT[:, :, 0:T], ALU.mult))
            for w in range(1, WIN):
                dve.wait_ge(raised, w + 1)
                st.then(nc.vector.tensor_tensor(work[:, 0], score[:, w], xT[:, :, w:w + T], ALU.mult))
                st.done(nc.vector.tensor_tensor(num[:], num[:], work[:, 0], ALU.add))
                if w >= 2:
                    st.done(nc.vector.tensor_tensor(den[:], den[:], score[:, w], ALU.add))
                dve.wait_ge(steps_v, st.n)
            st.then(nc.vector.reciprocal(den[:], den[:]))
            nc.vector.tensor_tensor(num[:], num[:], den[:], ALU.mult).then_inc(done, 1)


def normalise(nc, g, name, src=None, kept=None):
    with Stage(nc, name) as s:
        src = g.h if src is None else src
        xc = s.sb("xc", [TP, NT, C]) if kept is None else kept
        sq = s.sb("sq", [TP, NT, C])
        mean, var = s.sb("mean", [TP, NT]), s.sb("var", [TP, NT])
        banks = s.ps("banks", [C, 8, BANK])
        steps, var_ready, root_ready = s.sem("steps"), s.sem("var_ready"), s.sem("root_ready")
        ready, turned = s.sem("ready"), s.sem("turned")
        block = s.block()

        @block.vector
        def _(dve):
            st = Steps(dve, steps)
            wide = [TP, NT, C]
            st.then(nc.vector.tensor_reduce(mean[:], src[:], AX.X, ALU.add))
            st.then(nc.vector.tensor_scalar(mean[:], mean[:], 1.0 / C, None, ALU.mult))
            st.then(nc.vector.tensor_tensor(xc[:], src[:], bc(mean[:].unsqueeze(2), wide), ALU.subtract))
            st.then(nc.vector.tensor_tensor(sq[:], xc[:], xc[:], ALU.mult))
            st.then(nc.vector.tensor_reduce(var[:], sq[:], AX.X, ALU.add))
            nc.vector.tensor_scalar(var[:], var[:], 1.0 / C, EPS, ALU.mult, ALU.add).then_inc(var_ready, 1)
            dve.wait_ge(root_ready, 1)
            st.then(nc.vector.reciprocal(mean[:], var[:]))
            nc.vector.tensor_tensor(xc[:], xc[:], bc(mean[:].unsqueeze(2), wide), ALU.mult).then_inc(ready, 1)

        @block.scalar
        def _(act):
            act.wait_ge(var_ready, 1)
            nc.scalar.activation(var[:], var[:], ACT.Sqrt).then_inc(root_ready, 1)
            for n in range(NG):
                act.wait_ge(turned, n + 1)
                nc.scalar.copy(g.xT[0:C, GC * n:GC * n + GC], banks[:, n, 0:GC])

        @block.tensor
        def _(pe):
            pe.wait_ge(ready, 1)
            for j in range(NT):
                ins = nc.tensor.transpose(banks[:, j // GT, TP * (j % GT):TP * (j % GT) + TP], xc[:, j, :],
                                          g.ident[0:TP, 0:TP])
                if j % GT == GT - 1:
                    ins.then_inc(turned, 1)


def choose_two(nc, s, dve, act_in, act_out, st, logits, gate, experts):
    shape = [TP, NT, experts]
    order, eq = s.sb("order", [TP, experts]), s.sb("eq", shape)
    first, second, left = s.sb("first", shape), s.sb("second", shape), s.sb("left", shape)
    best, at, diff = s.sb("two", [TP, 2, NT]), s.sb("at", [TP, NT]), s.sb("diff", [TP, NT])
    share = s.sb("share", [TP, 2, NT])

    def wide(x):
        return bc(x.unsqueeze(2), shape)

    def dve_part():
        for e in range(experts):
            st.done(nc.vector.memset(order[:, e:e + 1], float(experts - e)))
        for n, (src, chosen) in enumerate(((logits, first), (left, second))):
            st.then(nc.vector.tensor_reduce(best[:, n], src[:], AX.X, ALU.max))
            st.then(nc.vector.tensor_tensor(eq[:], src[:], wide(best[:, n]), ALU.is_equal))
            st.then(nc.vector.tensor_tensor(eq[:], eq[:], bc(order[:].unsqueeze(1), shape), ALU.mult))
            st.then(nc.vector.tensor_reduce(at[:], eq[:], AX.X, ALU.max))
            st.then(nc.vector.tensor_tensor(chosen[:], eq[:], wide(at[:]), ALU.is_equal))
            if n == 0:
                st.then(nc.vector.scalar_tensor_tensor(out=left[:], in0=first[:], scalar=-3e38, in1=logits[:],
                                                       op0=ALU.mult, op1=ALU.add))
        nc.vector.tensor_tensor(diff[:], best[:, 1], best[:, 0], ALU.subtract).then_inc(act_in, 1)
        dve.wait_ge(act_out, 1)
        st.then(nc.vector.tensor_scalar(share[:, 0], diff[:], 1.0, None, ALU.add))
        st.then(nc.vector.reciprocal(share[:, 0], share[:, 0]))
        st.then(nc.vector.tensor_tensor(share[:, 1], share[:, 0], diff[:], ALU.mult))
        st.done(nc.vector.tensor_tensor(first[:], first[:], wide(share[:, 0]), ALU.mult))
        st.then(nc.vector.tensor_tensor(second[:], second[:], wide(share[:, 1]), ALU.mult))
        st.then(nc.vector.tensor_tensor(gate[:], first[:], second[:], ALU.add))

    return dve_part, diff


def route(nc, g, name, wg_src, biases, gate, experts):
    with Stage(nc, name) as s:
        wg, more = s.sb("wg", [C + 1, experts]), s.sb("more", [C + 1, experts])
        logits = s.sb("logits", [TP, NT, experts])
        bank = s.ps("bank", [TP, BANK])
        loads, steps = s.sem("loads"), s.sem("steps")
        w_ready, logits_ready, diff_ready, exp_ready = (s.sem(n) for n in ("w_ready", "logits_ready", "diff_ready", "exp_ready"))
        st = Steps(nc.vector, steps)
        dve_part, diff = choose_two(nc, s, nc.vector, diff_ready, exp_ready, st, logits, gate, experts)
        block = s.block()

        @block.sync
        def _(sp):
            sp.dma_start(wg[0:C, :], wg_src).then_inc(loads, 16)
            for dst, b in zip((wg, more), biases):
                sp.dma_start(dst[C:C + 1, :], b.unsqueeze(0)).then_inc(loads, 16)

        @block.tensor
        def _(pe):
            pe.wait_ge(loads, 16 * (1 + len(biases)))
            pe.wait_ge(w_ready, 1)
            for j in range(NT):
                ins = nc.tensor.matmul(bank[:, experts * j:experts * j + experts], g.xT[:, TP * j:TP * j + TP], wg[:],
                                       start=True, stop=True)
            ins.then_inc(logits_ready, 1)

        @block.scalar
        def _(act):
            act.wait_ge(diff_ready, 1)
            nc.scalar.activation(diff[:], diff[:], ACT.Exp).then_inc(exp_ready, 1)

        @block.vector
        def _(dve):
            if len(biases) == 2:
                dve.wait_ge(loads, 16 * 3)
                nc.vector.tensor_tensor(wg[C:C + 1, :], wg[C:C + 1, :], more[C:C + 1, :], ALU.add).then_inc(w_ready, 1)
            else:
                dve.sem_inc(w_ready, 1)
            dve.wait_ge(logits_ready, 1)
            st.then(nc.vector.tensor_copy(logits[:].rearrange("p j e -> p (j e)"), bank[:, 0:NT * experts]))
            dve_part()


def split_tokens(g, eng, n, x12, x13, x_rest, led, left, split, first=False, held=None):
    lo, hi, cols = slice(0, C), slice(C, P), bass.ds(GC * n, GC)
    x = g.xT[lo, cols]
    eng.tensor_copy(x12[lo, cols], x).then_inc(led, 1)
    eng.wait_ge(led, n + 1)
    if not first:
        eng.wait_ge(split, 3 * n)
    if held:
        eng.sem_inc(held, 1)
    eng.tensor_tensor(x_rest[hi, :], x, x12[lo, cols], ALU.subtract).then_inc(left, 1)
    eng.tensor_tensor(x12[hi, cols], x, x12[lo, cols], ALU.subtract).then_inc(split, 1)
    eng.tensor_copy(x13[lo, cols], x12[lo, cols]).then_inc(split, 1)
    eng.wait_ge(left, n + 1)
    eng.wait_ge(split, 3 * n + 2)
    if held:
        eng.sem_inc(held, 1)
    eng.tensor_tensor(x13[hi, cols], x_rest[hi, :], x12[hi, cols], ALU.subtract).then_inc(split, 1)


def run_experts(nc, g, name, gate, w1, b1, w2, b2_src, experts, chunks, func, loads_first=()):
    K = experts * chunks
    W = experts * C
    with Stage(nc, name) as s:
        b2, ones = s.sb("b2", [1, W]), s.sb("one", [1, TP])
        w11, w22, w31 = (s.sb(n, [P, K * P], BF16) for n in ("w11", "w22", "w31"))
        w_rest, x_rest = s.sb("w_rest", [C, K * P]), s.sb("x_rest", [P, GC])
        x12, x13 = s.sb("x12", [P, N], BF16), s.sb("x13", [P, N], BF16)
        hidden = s.sb("hidden", [P, 4, GC])
        gated, summed = s.sb("gated", [TP, GT, experts, C]), s.sb("summed", [TP, GT, C])
        up = s.ps("up", [P, 4, BANK])
        down = s.ps("down", [TP, GT, BANK])
        loads, ready, raised, squashed = (s.sem(n) for n in ("loads", "ready", "raised", "squashed"))
        used, taken, reduced, added = (s.sem(n) for n in ("used", "taken", "reduced", "added"))
        steps_w, led, left, split = (s.sem(n) for n in ("steps_w", "led", "left", "split"))
        LOADS = 16 * (1 + len(loads_first))
        lo, hi = slice(0, C), slice(C, P)
        block = s.block()

        @block.sync
        def _(sp):
            sp.dma_start(b2[:], b2_src).then_inc(loads, 16)
            for dst, src in loads_first:
                sp.dma_start(dst, src).then_inc(loads, 16)

        @block.tensor
        def _(pe):
            pe.wait_ge(ready, 2)
            pe.wait_ge(loads, LOADS)
            with pe.Fori(0, NG) as n:
                pe.wait_ge(split, 3 * n + 3)
                for k in range(K + 1):
                    if k < K:
                        if k >= 4:
                            pe.wait_ge(squashed, K * n + k - 3)
                        for i, (w, x) in enumerate(((w11, x12), (w22, x12), (w31, x13))):
                            ins = nc.tensor.matmul(up[:, k % 4, 0:GC], w[:, P * k:P * k + P], x[:, bass.ds(GC * n, GC)],
                                                   start=(i == 0), stop=(i == 2))
                        ins.then_inc(raised, 1)
                    if k == 1:
                        pe.wait_ge(taken, n + 1)
                        for t in range(GT):
                            nc.tensor.matmul(down[:, t, 0:W], ones[:], b2[:], start=True, stop=False,
                                             skip_group_check=True)
                    if k:
                        c = k - 1
                        e = c // chunks
                        pe.wait_ge(squashed, K * n + c + 1)
                        for t in range(GT):
                            ins = nc.tensor.matmul(down[:, t, C * e:C * e + C], hidden[:, c % 4, TP * t:TP * t + TP],
                                                   w2[:, c, :], start=False, stop=(c == K - 1), skip_group_check=True)
                        ins.then_inc(used, 1)

        @block.scalar
        def _(act):
            act.wait_ge(loads, LOADS)
            with act.Fori(0, NG) as n:
                for k in range(K):
                    act.wait_ge(raised, K * n + k + 1)
                    if k >= 4:
                        act.wait_ge(used, K * n + k - 3)
                    nc.scalar.activation(hidden[:, k % 4], up[:, k % 4, 0:GC], func,
                                         bias=b1[:, k:k + 1]).then_inc(squashed, 1)

        @block.vector
        def _(dve):
            dve.sem_inc(taken, 1)
            nc.vector.memset(ones[:], 1.0).then_inc(ready, 1)
            st = Steps(dve, steps_w)
            dve.wait_ge(loads, LOADS)
            st.then(nc.vector.tensor_copy(w11[:], w1[:]))
            st.done(nc.vector.tensor_tensor(w22[:], w1[:], w11[:], ALU.subtract))
            st.done(nc.vector.tensor_tensor(w_rest[:], w1[lo, :], w11[lo, :], ALU.subtract))
            st.then(nc.vector.tensor_copy(w31[hi, :], w11[hi, :]))
            nc.vector.tensor_tensor(w31[lo, :], w_rest[:], w22[lo, :], ALU.subtract).then_inc(ready, 1)

            def add_group(n):
                dve.wait_ge(used, K * n + K)
                nc.vector.tensor_tensor(gated[:], down[:, :, 0:W].rearrange("p t (e c) -> p t e c", c=C),
                                        bc(gate[:, bass.ds(GT * n, GT), :].unsqueeze(3), [TP, GT, experts, C]),
                                        ALU.mult).then_inc(taken, 1)
                dve.wait_ge(taken, n + 2)
                nc.vector.tensor_reduce(summed[:], gated[:].rearrange("p t e c -> p t c e"), AX.X,
                                        ALU.add).then_inc(reduced, 1)
                dve.wait_ge(reduced, n + 1)
                part = g.h[:, bass.ds(GT * n, GT), :]
                nc.vector.tensor_tensor(part, part, summed[:], ALU.add).then_inc(added, 1)
                dve.wait_ge(added, n + 1)

            split_tokens(g, nc.vector, 0, x12, x13, x_rest, led, left, split, first=True)
            with dve.Fori(0, NG - 1) as n:
                split_tokens(g, nc.vector, n + 1, x12, x13, x_rest, led, left, split)
                add_group(n)
            add_group(NG - 1)




def mamba(nc, g, A):
    DI, DS, DR, DC = 128, 16, 16, 4
    PAD = DC - 1
    HB = B // 2
    HN = HB * T
    QC = 2 * T
    with Stage(nc, "ma") as s:
        w_in, w_out = s.sb("w_in", [C, 2 * DI]), s.sb("w_out", [DI, C])
        w_dt, w_bc = s.sb("w_dt", [DI, 2, DR]), s.sb("w_bc", [DI, 2, 6 * DS])
        w_delta = s.sb("w_delta", [DR, 2, DI])
        conv_w, conv_b = s.sb("conv_w", [DI, 2, DC]), s.sb("conv_b", [DI, 2])
        delta_b, skip, a_log = s.sb("delta_b", [DI, 2]), s.sb("skip", [DI, 2]), s.sb("a_log", [DI, 2, DS])
        pick = s.sb("pick", [96, 2 * DS, P], BF16)
        xpad = s.sb("xpad", [DI, B, T + 2 * PAD])
        gate, y = s.sb("gate", [DI, B, T]), s.sb("y", [DI, B, T])
        u, delta, du = s.sb("u", [DI, B, T]), s.sb("delta", [DI, B, T]), s.sb("du", [DI, B, T])
        dt = s.sb("dt", [DR, N])
        acc = s.sb("acc", [DI, B, T])
        bc_parts = s.sb("bc_parts", [96, N], BF16)
        low = s.sb("low", [96, HN], BF16)
        decay, state = s.sb("decay", [DI, 2, HB, T]), s.sb("state", [DI, 2, HB, T])
        small = state[:].rearrange("p k b t -> p (k b) t")
        lost = decay[:].rearrange("p k b t -> p (k b) t")
        rest = decay[0:96, 0].rearrange("p b t -> p (b t)")
        banks = s.ps("banks", [P, 8, BANK])
        loads, cleared, picked = s.sem("loads"), s.sem("cleared"), s.sem("picked")
        projected, evacuated, relued, split = s.sem("projected"), s.sem("evacuated"), s.sem("relued"), s.sem("split")
        convolved, u_ready, ln_ready, steps_v = s.sem("convolved"), s.sem("u_ready"), s.sem("ln_ready"), s.sem("steps_v")
        steps_a = s.sem("steps_a")
        b_ready, c_ready, decay_ready, driven = s.sem("b_ready"), s.sem("c_ready"), s.sem("decay_ready"), s.sem("driven")
        scanned, weighted, added, y_ready = s.sem("scanned"), s.sem("weighted"), s.sem("added"), s.sem("y_ready")
        out_ready, du_ready, acc_ready = s.sem("out_ready"), s.sem("du_ready"), s.sem("acc_ready")
        restarted, e_ready = s.sem("restarted"), s.sem("e_ready")
        block = s.block()

        @block.sync
        def _(sp):
            names = ("", "_b")
            sp.dma_start(w_in[:], A["L0_attn_in_proj_w"]).then_inc(loads, 16)
            sp.dma_start(w_out[:], A["L0_attn_out_proj_w"]).then_inc(loads, 16)
            for d, n in enumerate(names):
                sp.dma_start(w_dt[:, d], A["L0_attn_x_proj_w" + n][:, 0:DR]).then_inc(loads, 16)
                for q in range(3):
                    sp.dma_start(w_bc[:, d, 2 * DS * q:2 * DS * q + 2 * DS],
                                 A["L0_attn_x_proj_w" + n][:, DR:DR + 2 * DS]).then_inc(loads, 16)
                sp.dma_start(w_delta[:, d], A["L0_attn_dt_proj_w" + n]).then_inc(loads, 16)
                sp.dma_start(conv_w[:, d], A["L0_attn_conv_w" + n]).then_inc(loads, 16)
                sp.dma_start(conv_b[:, d:d + 1], A["L0_attn_conv_b" + n].unsqueeze(1)).then_inc(loads, 16)
                sp.dma_start(delta_b[:, d:d + 1], A["L0_attn_dt_proj_b" + n].unsqueeze(1)).then_inc(loads, 16)
                sp.dma_start(skip[:, d:d + 1], A["L0_attn_D" + n].unsqueeze(1)).then_inc(loads, 16)
                sp.dma_start(a_log[:, d], A["L0_attn_A" + n + "_log"]).then_inc(loads, 16)
        LOADS = 16 * (2 + 2 * 10)

        @block.tensor
        def _(pe):
            pe.wait_ge(loads, LOADS)
            for m in range(2):
                for c in range(8):
                    if m:
                        pe.wait_ge(evacuated, c + 1)
                    nc.tensor.matmul(banks[:, c, 0:QC], w_in[:, DI * m:DI * m + DI], g.xT[0:C, QC * c:QC * c + QC],
                                     start=True, stop=True).then_inc(projected, 1)
            pe.wait_ge(picked, 4)
            for d in range(2):
                done = 16 + 24 * d
                pe.wait_ge(u_ready, d + 1)
                if d:
                    pe.wait_ge(weighted, 1 + 32 * d)
                for c in range(8):
                    pe.wait_ge(evacuated, done if c == 0 else done - 8 + c + 1)
                    nc.tensor.matmul(banks[0:DR, c, 0:QC], w_dt[:, d], u[:, 2 * c:2 * c + 2, :],
                                     start=True, stop=True).then_inc(projected, 1)
                for c in range(8):
                    pe.wait_ge(evacuated, done + c + 1)
                    nc.tensor.matmul(banks[:, c, 0:QC], w_delta[:, d], dt[:, QC * c:QC * c + QC],
                                     start=True, stop=True).then_inc(projected, 1)
                for c in range(8):
                    pe.wait_ge(evacuated, done + 8 + c + 1)
                    nc.tensor.matmul(banks[0:96, c, 0:QC], w_bc[:, d], u[:, 2 * c:2 * c + 2, :],
                                     start=True, stop=True).then_inc(projected, 1)
                pe.wait_ge(split, 2 * d + 2)
                for half in range(2):
                    with pe.Fori(0, DS) as n:
                        k = (2 * d + half) * DS + n
                        for row, free, ready in ((0, driven, b_ready), (DS, weighted, c_ready)):
                            pe.wait_ge(free, k + 1)
                            for c in range(4):
                                ins = nc.tensor.matmul(banks[:, (4 if row else 0) + c, 0:QC], pick[:, row + n, :],
                                                       bc_parts[:, HN * half + QC * c:HN * half + QC * c + QC],
                                                       start=True, stop=True)
                            ins.then_inc(ready, 1)
            pe.wait_ge(y_ready, 1)
            for j in range(NT):
                ins = nc.tensor.matmul(banks[0:TP, j // 8, C * (j % 8):C * (j % 8) + C],
                                       y[:, j // 2, TP * (j % 2):TP * (j % 2) + TP], w_out[:], start=True, stop=True)
                if j % 8 == 7:
                    ins.then_inc(out_ready, 1)

        @block.scalar
        def _(act):
            st = Steps(act, steps_a)
            act.wait_ge(loads, LOADS)
            st.done(nc.scalar.activation(a_log[:], a_log[:], ACT.Exp))
            act.wait_ge(cleared, 1)
            for c in range(8):
                act.wait_ge(projected, c + 1)
                nc.scalar.copy(xpad[:, 2 * c:2 * c + 2, PAD:PAD + T],
                               banks[:, c, 0:QC].rearrange("p (b t) -> p b t", b=2)).then_inc(evacuated, 1)
            for c in range(8):
                act.wait_ge(projected, 8 + c + 1)
                nc.scalar.activation(gate[:, 2 * c:2 * c + 2, :].rearrange("p b t -> p (b t)"), banks[:, c, 0:QC],
                                     ACT.Silu).then_inc(evacuated, 1)
            act.wait_ge(steps_a, 1)
            st.then(nc.scalar.mul(a_log[:], a_log[:], -1.0))
            for d in range(2):
                done = 16 + 24 * d
                act.wait_ge(convolved, d + 1)
                nc.scalar.activation(u[:], u[:], ACT.Silu, bias=conv_b[:, d:d + 1]).then_inc(u_ready, 1)
                for c in range(8):
                    act.wait_ge(projected, done + c + 1)
                    nc.scalar.copy(dt[:, QC * c:QC * c + QC], banks[0:DR, c, 0:QC]).then_inc(evacuated, 1)
                flat = delta[:].rearrange("p b t -> p (b t)")
                for c in range(8):
                    act.wait_ge(projected, done + 8 + c + 1)
                    nc.scalar.activation(flat[:, QC * c:QC * c + QC], banks[:, c, 0:QC], ACT.Identity,
                                         bias=delta_b[:, d:d + 1]).then_inc(evacuated, 1)
                for c in range(8):
                    act.wait_ge(projected, done + 16 + c + 1)
                    nc.scalar.copy(bc_parts[:, QC * c:QC * c + QC], banks[0:96, c, 0:QC]).then_inc(evacuated, 1)
                act.wait_ge(relued, d + 1)
                st.then(nc.scalar.activation(delta[:], delta[:], ACT.Abs))
                nc.scalar.activation(small, delta[:], ACT.Exp, scale=-1.0).then_inc(e_ready, 1)
                act.wait_ge(e_ready, d + 1)
                nc.scalar.activation(delta[:], small, ACT.Ln, bias=1.0).then_inc(ln_ready, 1)
                act.wait_ge(du_ready, d + 1)
                for half in range(2):
                    with act.Fori(0, DS // 2) as n2:
                        for b in range(2):
                            k = (2 * d + half) * DS + 2 * n2 + b
                            act.wait_ge(scanned, k + 1)
                            nc.scalar.activation(decay[:, b], delta[:, HB * half:HB * half + HB, :], ACT.Exp,
                                                 scale=a_log[:, d, bass.ds(2 * n2 + b, 1)]).then_inc(decay_ready, 1)

        @block.gpsimd
        def _(pool):
            nc.gpsimd.memset(pick[:], 0.0).then_inc(picked, 1)
            for q in range(3):
                pool.wait_ge(picked, q + 1)
                nc.gpsimd.affine_select(out=pick[:], in_=pick[:], compare_op=ALU.not_equal, fill=1.0,
                                        base=-2 * DS * q, pattern=[[-1, 2 * DS], [0, P]],
                                        channel_multiplier=1).then_inc(picked, 1)
            for d in range(2):
                pool.wait_ge(acc_ready, d + 1)
                for half in range(2):
                    part = acc[:, HB * half:HB * half + HB, :]
                    with pool.Fori(0, DS // 2) as n2:
                        for b in range(2):
                            k = (2 * d + half) * DS + 2 * n2 + b
                            pool.wait_ge(weighted, k + 2)
                            pool.wait_ge(added, k + 2)
                            nc.gpsimd.tensor_tensor(part, part, state[:, b], ALU.add).then_inc(added, 1)

        @block.vector
        def _(dve):
            st = Steps(dve, steps_v)
            dve.sem_inc(driven, 1)
            dve.sem_inc(weighted, 1)
            dve.sem_inc(scanned, 2)
            dve.sem_inc(added, 2)
            nc.vector.memset(xpad[:], 0.0).then_inc(cleared, 1)
            for d in range(2):
                done = 16 + 24 * d
                dve.wait_ge(evacuated, 16)
                for i in range(DC):
                    x_i = xpad[:, :, i:i + T] if d == 0 else xpad[:, :, 2 * PAD - i:2 * PAD - i + T][:, :, ::-1]
                    w_i = conv_w[:, d, i:i + 1]
                    if i == 0:
                        st.then(nc.vector.tensor_scalar(u[:], x_i, w_i, None, ALU.mult))
                    elif i < DC - 1:
                        st.then(nc.vector.scalar_tensor_tensor(out=u[:], in0=x_i, scalar=w_i, in1=u[:],
                                                               op0=ALU.mult, op1=ALU.add))
                    else:
                        nc.vector.scalar_tensor_tensor(out=u[:], in0=x_i, scalar=w_i, in1=u[:], op0=ALU.mult,
                                                       op1=ALU.add).then_inc(convolved, 1)
                nc.vector.memset(acc[:], 0.0).then_inc(acc_ready, 1)
                dve.wait_ge(evacuated, done + 16)
                nc.vector.tensor_scalar(du[:], delta[:], 0.0, None, ALU.max).then_inc(relued, 1)
                for half in range(2):
                    dve.wait_ge(evacuated, done + 16 + 4 * half + 4)
                    cols = slice(HN * half, HN * half + HN)
                    if half or d:
                        dve.wait_ge(split, 2 * d + half)
                    rest4 = rest.rearrange("p (c n) -> p c n", c=4)
                    mine = bc_parts[:, cols].rearrange("p (c n) -> p c n", c=4)
                    st.then(nc.vector.tensor_tensor(rest4, banks[0:96, 4 * half:4 * half + 4, 0:QC], mine, ALU.subtract))
                    st.done(nc.vector.tensor_copy(bc_parts[32:64, cols], rest[32:64, :]))
                    st.then(nc.vector.tensor_copy(low[64:96, :], rest[64:96, :]))
                    nc.vector.tensor_tensor(bc_parts[64:96, cols], rest[64:96, :], low[64:96, :],
                                            ALU.subtract).then_inc(split, 1)
                dve.wait_ge(e_ready, d + 1)
                dve.wait_ge(split, 2 * d + 2)
                st.then(nc.vector.tensor_scalar(lost, small, 1.0, -1.0, ALU.add, ALU.add))
                st.then(nc.vector.tensor_tensor(lost, small, lost, ALU.subtract))
                dve.wait_ge(relued, d + 1)
                st.then(nc.vector.tensor_tensor(du[:], du[:], lost, ALU.add))
                dve.wait_ge(ln_ready, d + 1)
                st.then(nc.vector.tensor_tensor(delta[:], delta[:], du[:], ALU.add))
                nc.vector.tensor_tensor(du[:], delta[:], u[:], ALU.mult).then_inc(du_ready, 1)
                dve.wait_ge(du_ready, d + 1)
                for half in range(2):
                    part = du[:, HB * half:HB * half + HB, :].rearrange("p (c b) t -> p c (b t)", b=2)
                    with dve.Fori(0, DS // 2) as n2:
                        for b in range(2):
                            k = (2 * d + half) * DS + 2 * n2 + b
                            now = state[:, b].rearrange("p b t -> p (b t)")
                            now4 = state[:, b].rearrange("p (c b) t -> p c (b t)", b=2)
                            past = decay[:, b].rearrange("p b t -> p (b t)")
                            dve.wait_ge(b_ready, k + 1)
                            dve.wait_ge(added, k + 1)
                            nc.vector.tensor_tensor(now4, banks[:, 0:4, 0:QC], part, ALU.mult).then_inc(driven, 1)
                            dve.wait_ge(decay_ready, k + 1)
                            nc.vector.memset(decay[:, b, :, 0:1], 0.0).then_inc(restarted, 1)
                            dve.wait_ge(driven, k + 2)
                            dve.wait_ge(restarted, k + 1)
                            nc.vector.tensor_tensor_scan(now, past, now, 0.0, ALU.mult, ALU.add).then_inc(scanned, 1)
                            dve.wait_ge(scanned, k + 3)
                            dve.wait_ge(c_ready, k + 1)
                            nc.vector.tensor_tensor(now4, banks[:, 4:8, 0:QC], now4, ALU.mult).then_inc(weighted, 1)
                dve.wait_ge(added, 32 * (d + 1) + 2)
                if d == 0:
                    st.then(nc.vector.scalar_tensor_tensor(out=y[:], in0=u[:], scalar=skip[:, 0:1], in1=acc[:],
                                                           op0=ALU.mult, op1=ALU.add))
                else:
                    st.then(nc.vector.scalar_tensor_tensor(out=acc[:], in0=u[:], scalar=skip[:, 1:2], in1=acc[:],
                                                           op0=ALU.mult, op1=ALU.add))
                    st.then(nc.vector.tensor_tensor(y[:], y[:], acc[:, :, ::-1], ALU.add))
                    nc.vector.tensor_tensor(y[:], y[:], gate[:], ALU.mult).then_inc(y_ready, 1)
            for q in range(4):
                dve.wait_ge(out_ready, q + 1)
                part = g.h[:, 8 * q:8 * q + 8, :]
                nc.vector.tensor_tensor(part, part, banks[0:TP, q, :].rearrange("p (j c) -> p j c", j=8), ALU.add)


def graph_experts(nc, g, A):
    E, HEADS, TOPS = 4, 4, 16
    EDGES = 262144
    COLS = EDGES // P
    F = HEADS * E
    V = F + HEADS
    G = 8
    HIGH = 60.0
    ROUND = 12582912.0
    with Stage(nc, "ge") as s:
        gate = s.sb("gate", [TP, NT, E])
        w1, b1, w2 = s.sb("w1", [P, E * P]), s.sb("b1", [P, E]), s.sb("w2", [P, E, C])
        nodes, own = s.sb("nodes", [TP, NT, F + 2 * HEADS]), s.sb("own", [TP, NT, V])
        keys = s.sb("keys", [P, COLS])
        turns = s.sb("turns", [P, 1], I32)
        with Stage(nc, "gt") as t:
            make_tables(nc, g, A, t, nodes, own, keys, turns, E, HEADS, F, V, COLS, HIGH, ROUND)
        with Stage(nc, "gw") as t:
            walk_edges(nc, g, A, t, own, keys, turns, gate, E, HEADS, F, V, G)
        run_experts(nc, g, "gx", gate, w1, b1, w2, A["L0_ffn_b2"], E, 1, ACT.Gelu,
                    ((w1[0:C, :], A["L0_ffn_W1"]), (w1[C:P, :], A["L0_ffn_W1"]), (b1[:], A["L0_ffn_b1"]),
                     (w2[:], A["L0_ffn_W2"])))


def make_tables(nc, g, A, s, nodes, own, keys, turns, E, HEADS, F, V, COLS, HIGH, ROUND):
    wg, fold = s.sb("wg", [C, F]), s.sb("fold", [F, F + 2 * HEADS])
    hT = s.sb("hT", [F, N])
    dst_rows, leaky = s.sb("dst_rows", [P, NT, 2 * HEADS]), s.sb("leaky", [TP, NT, HEADS])
    bound, top, topmost = s.sb("bound", [TP, NT, HEADS]), s.sb("top", [P, HEADS]), s.sb("topmost", [P, HEADS])
    src_i, dst_i = s.sb("src_i", [P, COLS], I32), s.sb("dst_i", [P, COLS], I32)
    src, dst, tile = (s.sb(n, [P, COLS]) for n in ("src", "dst", "tile"))
    count, most = s.sb("count", [P, 1]), s.sb("most", [P, 1])
    banks = s.ps("banks", [P, 8, BANK])
    loads, edges, projected, hT_ready, folded = (s.sem(n) for n in ("loads", "edges", "projected", "hT_ready", "folded"))
    nodes_ready, tops_ready, reduced, steps_v = (s.sem(n) for n in ("nodes_ready", "tops_ready", "reduced", "steps_v"))
    own_in, own_out, rows_ready, stored, steps_p = (s.sem(n) for n in ("own_in", "own_out", "rows_ready", "stored", "steps_p"))
    block = s.block()

    @block.sync
    def _(sp):
        sp.dma_start(wg[:], A["L0_ffn_W_gat"]).then_inc(loads, 16)
        sp.dma_start(fold[:], A["fold"]).then_inc(loads, 16)
        sp.dma_start(dst_i[:], A["L0_ffn_edge_index"][1].rearrange("(p n) -> p n", p=P)).then_inc(edges, 16)
        sp.dma_start(src_i[:], A["L0_ffn_edge_index"][0].rearrange("(p n) -> p n", p=P)).then_inc(edges, 16)
        sp.wait_ge(rows_ready, 1)
        sp.dma_start(g.src_table.rearrange("(j p) v -> p j v", p=TP), nodes[:, :, 0:V]).then_inc(stored, 16)
        sp.dma_start(g.dst_table.rearrange("(j p) v -> p j v", p=P), dst_rows[:]).then_inc(stored, 16)
        sp.wait_ge(stored, 32)

    @block.tensor
    def _(pe):
        pe.wait_ge(loads, 32)
        for c in range(NG):
            nc.tensor.matmul(banks[0:F, c, 0:GC], wg[:], g.xT[0:C, GC * c:GC * c + GC], start=True,
                             stop=True).then_inc(projected, 1)
        pe.wait_ge(hT_ready, NG)
        W = F + 2 * HEADS
        for j in range(NT):
            ins = nc.tensor.matmul(banks[0:TP, j // 16, W * (j % 16):W * (j % 16) + W], hT[:, TP * j:TP * j + TP],
                                   fold[:], start=True, stop=True)
        ins.then_inc(folded, 1)

    @block.scalar
    def _(act):
        for c in range(NG):
            act.wait_ge(projected, c + 1)
            nc.scalar.copy(hT[:, GC * c:GC * c + GC], banks[0:F, c, 0:GC]).then_inc(hT_ready, 1)
        act.wait_ge(folded, 1)
        nc.scalar.copy(nodes[:].rearrange("p (q j) w -> p q (j w)", q=2),
                       banks[0:TP, 0:2, 0:16 * (F + 2 * HEADS)]).then_inc(nodes_ready, 1)
        act.wait_ge(own_in, 1)
        nc.scalar.activation(own[:, :, F:V], own[:, :, F:V], ACT.Exp).then_inc(own_out, 1)

    @block.gpsimd
    def _(pool):
        pool.wait_ge(tops_ready, 1)
        nc.gpsimd.partition_all_reduce(topmost[:], top[:], P, RMAX).then_inc(reduced, 1)
        pool.wait_ge(tops_ready, 2)
        pool.wait_ge(reduced, 1)
        nc.gpsimd.partition_all_reduce(most[:], count[:], P, RMAX).then_inc(reduced, 1)

    @block.vector
    def _(dve):
        st = Steps(dve, steps_v)
        src_score, dst_score = nodes[:, :, F:V], nodes[:, :, V:V + HEADS]
        st.done(nc.vector.memset(dst_rows[:], 0.0))
        st.then(nc.vector.memset(top[:], -3e38))
        dve.wait_ge(nodes_ready, 1)
        nc.vector.tensor_reduce(top[0:TP, :], src_score.rearrange("p j h -> p h j"), AX.X, ALU.max).then_inc(tops_ready, 1)
        st.done(nc.vector.tensor_copy(dst_rows[0:TP, :, 0:HEADS], dst_score))
        st.then(nc.vector.tensor_tensor(leaky[:], src_score, dst_score, ALU.add))
        st.then(nc.vector.scalar_tensor_tensor(out=leaky[:], in0=leaky[:], scalar=0.2, in1=leaky[:], op0=ALU.mult, op1=ALU.max))
        dve.wait_ge(reduced, 1)
        st.then(nc.vector.tensor_tensor(bound[:], dst_score, bc(topmost[0:TP, :].unsqueeze(1), [TP, NT, HEADS]), ALU.add))
        st.then(nc.vector.scalar_tensor_tensor(out=bound[:], in0=bound[:], scalar=0.2, in1=bound[:], op0=ALU.mult, op1=ALU.max))
        st.then(nc.vector.scalar_tensor_tensor(out=dst_rows[0:TP, :, HEADS:], in0=bound[:], scalar=-HIGH, in1=leaky[:],
                                               op0=ALU.add, op1=ALU.max))
        nc.vector.tensor_tensor(own[:, :, F:V], leaky[:], dst_rows[0:TP, :, HEADS:], ALU.subtract).then_inc(own_in, 1)
        dve.sem_inc(rows_ready, 1)
        dve.wait_ge(edges, 32)
        st.done(nc.vector.tensor_copy(src[:], src_i[:]))
        st.then(nc.vector.tensor_copy(dst[:], dst_i[:]))
        st.then(nc.vector.tensor_scalar(tile[:], dst[:], float(TP // 2), 1.0 / TP, ALU.subtract, ALU.mult))
        st.then(nc.vector.tensor_scalar(tile[:], tile[:], ROUND, None, ALU.add))
        st.then(nc.vector.tensor_scalar(tile[:], tile[:], ROUND, None, ALU.subtract))
        st.then(nc.vector.scalar_tensor_tensor(out=keys[:], in0=tile[:], scalar=float(P - TP), in1=dst[:], op0=ALU.mult,
                                               op1=ALU.add))
        st.then(nc.vector.tensor_scalar(src[:], src[:], float(N - 1), 1.0, ALU.min, ALU.add))
        st.then(nc.vector.scalar_tensor_tensor(out=keys[:], in0=keys[:], scalar=4096.0, in1=src[:], op0=ALU.mult, op1=ALU.add))
        st.then(nc.vector.tensor_scalar(dst[:], dst[:], float(N), None, ALU.is_lt))
        st.done(nc.vector.tensor_reduce(count[:], dst[:], AX.X, ALU.add))
        st.then(nc.vector.tensor_tensor(keys[:], keys[:], dst[:], ALU.mult))
        st.then(nc.vector.tensor_scalar(keys[:], keys[:], -1.0, None, ALU.add))
        dve.sem_inc(tops_ready, 1)
        dve.wait_ge(own_out, 1)
        w = bc(own[:, :, F:V].unsqueeze(3), [TP, NT, HEADS, E])
        st.done(nc.vector.tensor_tensor(own[:, :, 0:F].rearrange("p j (h e) -> p j h e", h=HEADS),
                                        nodes[:, :, 0:F].rearrange("p j (h e) -> p j h e", h=HEADS), w, ALU.mult))
        dve.wait_ge(reduced, 2)
        st.then(nc.vector.tensor_scalar(turns[:], most[:], 1.0, 15.0, ALU.max, ALU.add))
        st.then(nc.vector.tensor_scalar(turns[:], turns[:], 4, None, ALU.arith_shift_right))


def walk_edges(nc, g, A, s, own, keys, turns, gate, E, HEADS, F, V, G):
    MOST = keys.shape[1] // (2 * G)
    best = s.sb("largest", [P, G])
    code = s.sb("code", [P, G], I32)
    src_at, dst_at = s.sb("src_at", [P, 2, G], I32), s.sb("dst_at", [P, 2, G], I32)
    part_i = s.sb("part_i", [P, 2, G], I32)
    tile, row = s.sb("tile", [P, 2, G]), s.sb("row", [P, 2, G])
    src_rows, dst_rows = s.sb("src_rows", [P, 2, G, V]), s.sb("dst_rows", [P, 2, G, 2 * HEADS])
    score = s.sb("score", [P, G, HEADS])
    value = s.sb("value", [P, G, V])
    row_hot, tile_hot = s.sb("row_hot", [P, 2, G, TP]), s.sb("tile_hot", [P, G, NT])
    spread = s.sb("spread", [P, 2, G, NT, V])
    ramp_i, ramp, zeros = s.sb("ramp_i", [P, P], I32), s.sb("ramp", [P, P]), s.sb("zeros", [1, BANK])
    total = s.sb("total", [TP, NT, V])
    gamma, beta, b_gat = (s.sb(n, [TP, F]) for n in ("gamma", "beta", "b_gat"))
    mean, var, sq = s.sb("mean", [TP, NT]), s.sb("var", [TP, NT]), s.sb("sq", [TP, NT, F])
    scores = s.sb("scores", [TP, NT, E])
    sums = s.ps("sums", [TP, 2, BANK])
    W = NT // 2 * V
    loads, consts, picked, steps_v = (s.sem(n) for n in ("loads", "consts", "picked", "steps_v"))
    gathered = [s.sem(f"gathered{b}") for b in range(2)]
    consumed, score_in, score_out = s.sem("consumed"), s.sem("score_in"), s.sem("score_out")
    spread_ready, summed, root_in, root_out = (s.sem(n) for n in ("spread_ready", "summed", "root_in", "root_out"))
    diff_ready, exp_ready = s.sem("diff_ready"), s.sem("exp_ready")
    steps_end, waited = s.sem("steps_end"), s.sem("waited")
    st_end = Steps(nc.vector, steps_end)
    dve_part, diff = choose_two(nc, s, nc.vector, diff_ready, exp_ready, st_end, scores, gate, E)
    block = s.block()

    def turns_of(eng):
        return eng.value_load(turns[0:1, 0:1], min_val=1, max_val=MOST)

    @block.sync
    def _(sp):
        for dst, name in ((gamma, "ln_gamma"), (beta, "ln_beta"), (b_gat, "b_gat")):
            sp.dma_start(dst[:], A["L0_ffn_" + name].unsqueeze(0).to_broadcast([TP, F])).then_inc(loads, 16)

    @block.gpsimd
    def _(pool):
        nc.gpsimd.iota(ramp_i[:], pattern=[[1, P]], base=0, channel_multiplier=0).then_inc(consts, 1)
        with pool.Fori(0, turns_of(pool)) as i:
            for b in range(2):
                pool.wait_ge(picked, 2 * i + b + 1)
                pool.wait_ge(consumed, 2 * i + b + 1)
                pool.sem_inc(waited, 1)
                for k in range(G):
                    for rows, at, table in ((src_rows, src_at, g.src_table), (dst_rows, dst_at, g.dst_table)):
                        nc.gpsimd.indirect_dma_start(
                            out=rows[:, b, k, :], out_offset=None, in_=table,
                            in_offset=bass.IndirectOffsetOnAxis(ap=at[:, b, k:k + 1], axis=0)).then_inc(gathered[b], 16)

    @block.scalar
    def _(act):
        with act.Fori(0, turns_of(act)) as i:
            for b in range(2):
                act.wait_ge(score_in, 2 * i + b + 1)
                nc.scalar.activation(value[:, :, F:V], score[:], ACT.Exp).then_inc(score_out, 1)
        act.wait_ge(root_in, 1)
        nc.scalar.activation(var[:], var[:], ACT.Sqrt).then_inc(root_out, 1)
        act.wait_ge(diff_ready, 1)
        nc.scalar.activation(diff[:], diff[:], ACT.Exp).then_inc(exp_ready, 1)

    @block.tensor
    def _(pe):
        pe.wait_ge(consts, 3)
        for q in range(2):
            nc.tensor.matmul(sums[:, q, 0:W], zeros[:, 0:TP], zeros[:, 0:W], start=True, stop=False,
                             skip_group_check=True)
        with pe.Fori(0, turns_of(pe)) as i:
            for b in range(2):
                pe.wait_ge(spread_ready, 2 * i + b + 1)
                for k in range(G):
                    for q in range(2):
                        half = spread[:, b, k, NT // 2 * q:NT // 2 * q + NT // 2, :].rearrange("p j v -> p (j v)")
                        ins = nc.tensor.matmul(sums[:, q, 0:W], row_hot[:, b, k, :], half, start=False, stop=False,
                                               skip_group_check=True)
                ins.then_inc(summed, 1)

    @block.vector
    def _(dve):
        st = Steps(dve, steps_v)
        dve.sem_inc(consumed, 2)
        dve.sem_inc(summed, 2)
        dve.wait_ge(consts, 1)
        nc.vector.memset(zeros[:], 0.0).then_inc(consts, 1)
        nc.vector.tensor_copy(ramp[:], ramp_i[:]).then_inc(consts, 1)
        dve.wait_ge(consts, 3)

        def pick(turn, b, st):
            dve.sem_inc(waited, 1)
            st.then(nc.vector.max(out=best[:], in_=keys[:]))
            dve.sem_inc(waited, 1)
            st.done(nc.vector.match_replace(out=keys[:], in_to_replace=best[:], in_values=keys[:], imm_value=-1.0))
            st.then(nc.vector.tensor_copy(code[:], best[:]))
            st.done(nc.vector.tensor_scalar(src_at[:, b], code[:], 4095, None, ALU.bitwise_and))
            st.done(nc.vector.tensor_scalar(dst_at[:, b], code[:], 12, None, ALU.arith_shift_right))
            st.then(nc.vector.tensor_scalar(part_i[:, 0], code[:], 19, None, ALU.arith_shift_right))
            st.done(nc.vector.tensor_copy(tile[:, b], part_i[:, 0]))
            st.then(nc.vector.tensor_scalar(part_i[:, 1], dst_at[:, b], P - 1, None, ALU.bitwise_and))
            st.done(nc.vector.tensor_copy(row[:, b], part_i[:, 1]))
            st.done(nc.vector.tensor_scalar(src_at[:, b], src_at[:, b], float(N - 1), None, ALU.min))
            st.then(nc.vector.tensor_scalar(dst_at[:, b], dst_at[:, b], 0.0, None, ALU.max))
            dve.sem_inc(picked, 1)

        def spread_out(turn, b, st):
            dve.wait_ge(gathered[b], 256 * (turn + 1))
            st.then(nc.vector.tensor_tensor(score[:], src_rows[:, b, :, F:V], dst_rows[:, b, :, 0:HEADS], ALU.add))
            st.then(nc.vector.scalar_tensor_tensor(out=score[:], in0=score[:], scalar=0.2, in1=score[:], op0=ALU.mult,
                                                   op1=ALU.max))
            nc.vector.tensor_tensor(score[:], score[:], dst_rows[:, b, :, HEADS:], ALU.subtract).then_inc(score_in, 1)
            dve.wait_ge(summed, 2 * turn + b + 1)
            st.done(nc.vector.tensor_tensor(row_hot[:, b], bc(ramp[:, 0:TP].unsqueeze(1), [P, G, TP]),
                                            bc(row[:, b].unsqueeze(2), [P, G, TP]), ALU.is_equal))
            st.done(nc.vector.tensor_tensor(tile_hot[:], bc(ramp[:, 0:NT].unsqueeze(1), [P, G, NT]),
                                            bc(tile[:, b].unsqueeze(2), [P, G, NT]), ALU.is_equal))
            dve.wait_ge(score_out, 2 * turn + b + 1)
            w = bc(value[:, :, F:V].unsqueeze(3), [P, G, HEADS, E])
            st.then(nc.vector.tensor_tensor(value[:, :, 0:F].rearrange("p k (h e) -> p k h e", h=HEADS),
                                            src_rows[:, b, :, 0:F].rearrange("p k (h e) -> p k h e", h=HEADS), w,
                                            ALU.mult))
            dve.sem_inc(consumed, 1)
            nc.vector.tensor_tensor(spread[:, b], bc(tile_hot[:].unsqueeze(3), [P, G, NT, V]),
                                    bc(value[:].unsqueeze(2), [P, G, NT, V]), ALU.mult).then_inc(spread_ready, 1)
            dve.wait_ge(spread_ready, 2 * turn + b + 1)

        pick(0, 0, st)
        first = st.n
        PICK, SPREAD = 11, 5
        count = turns_of(dve)
        with dve.Fori(0, count) as i:
            st = Steps(dve, steps_v, first + 2 * (PICK + SPREAD) * i)
            for b in range(2):
                pick(i, 1 - b, st)
                spread_out(i, b, st)
            assert st.n == 2 * (PICK + SPREAD)
        st = st_end
        dve.wait_ge(summed, 2 * count + 2)
        for q in range(2):
            part = slice(NT // 2 * q, NT // 2 * q + NT // 2)
            st.done(nc.vector.tensor_tensor(total[:, part], sums[:, q, 0:W].rearrange("p (j v) -> p j v", v=V),
                                            own[:, part], ALU.add))
        dve.wait_ge(steps_end, st.n)
        den = total[:, :, F:V]
        st.then(nc.vector.tensor_scalar(den, den, 1e-16, None, ALU.add))
        st.then(nc.vector.reciprocal(den, den))
        agg = total[:, :, 0:F]
        agg4 = agg.rearrange("p j (h e) -> p j h e", h=HEADS)
        wide = [TP, NT, F]
        st.then(nc.vector.tensor_tensor(agg4, agg4, bc(den.unsqueeze(3), [TP, NT, HEADS, E]), ALU.mult))
        dve.wait_ge(loads, 48)
        st.then(nc.vector.tensor_tensor(agg, agg, bc(b_gat[:].unsqueeze(1), wide), ALU.add))
        st.then(nc.vector.tensor_reduce(mean[:], agg, AX.X, ALU.add))
        st.then(nc.vector.tensor_scalar(mean[:], mean[:], 1.0 / F, None, ALU.mult))
        st.then(nc.vector.tensor_tensor(agg, agg, bc(mean[:].unsqueeze(2), wide), ALU.subtract))
        st.then(nc.vector.tensor_tensor(sq[:], agg, agg, ALU.mult))
        st.then(nc.vector.tensor_reduce(var[:], sq[:], AX.X, ALU.add))
        nc.vector.tensor_scalar(var[:], var[:], 1.0 / F, EPS, ALU.mult, ALU.add).then_inc(root_in, 1)
        dve.wait_ge(root_out, 1)
        st.then(nc.vector.reciprocal(mean[:], var[:]))
        st.then(nc.vector.tensor_tensor(agg, agg, bc(mean[:].unsqueeze(2), wide), ALU.mult))
        st.then(nc.vector.tensor_tensor(agg, agg, bc(gamma[:].unsqueeze(1), wide), ALU.mult))
        st.then(nc.vector.tensor_tensor(agg, agg, bc(beta[:].unsqueeze(1), wide), ALU.add))
        st.then(nc.vector.tensor_reduce(scores[:], agg.rearrange("p j (h e) -> p j e h", h=HEADS), AX.X, ALU.add))
        st.then(nc.vector.tensor_scalar(scores[:], scores[:], 1.0 / HEADS, None, ALU.mult))
        dve_part()


def rwkv(nc, g, A):
    with Stage(nc, "rw") as s:
        mix, rest = s.sb("mix", [C, 3]), s.sb("rest", [C, 3])
        w3, wo = s.sb("w3", [C, 3, C]), s.sb("wo", [C, C])
        decay, steps = s.sb("decay", [TP, 2, TP]), s.sb("ones", [TP, 2, TP])
        windows = s.sb("windows", [TP, 2, 2, TP])
        mixed = s.sb("mixed", [C, 3, B, T])
        k, kv, r, z = (s.sb(n, [TP, NT, C]) for n in ("k", "kv", "r", "z"))
        inv = s.sb("inv", [TP, 4, BANK])
        zT = s.sb("zT", [C, N])
        banks = s.ps("banks", [P, 8, BANK])
        loads, steps_v = s.sem("loads"), s.sem("steps_v")
        mix_ready, projected, k_clipped, k_ready = s.sem("mix_ready"), s.sem("projected"), s.sem("k_clipped"), s.sem("k_ready")
        kv_ready, r_ready, summed, z_ready = s.sem("kv_ready"), s.sem("r_ready"), s.sem("summed"), s.sem("z_ready")
        turned, zT_ready, out_ready = s.sem("turned"), s.sem("zT_ready"), s.sem("out_ready")
        turned_round = s.sem("turned_round")
        block = s.block()
        x = g.xT[0:C, :].rearrange("c (b t) -> c b t", b=B)

        @block.sync
        def _(sp):
            for n, m in enumerate("kvr"):
                sp.dma_start(mix[:, n:n + 1], A["L1_attn_time_mix_" + m].rearrange("a b c -> c (a b)")).then_inc(loads, 16)
                sp.dma_start(w3[:, n], A["L1_attn_W" + m]).then_inc(loads, 16)
            sp.dma_start(wo[:], A["L1_attn_Wo"]).then_inc(loads, 16)
            for far in range(2):
                for n, name in enumerate(("time_curve", "time_steps")):
                    curve = A[name]
                    window = bass.AP(tensor=curve.tensor, offset=curve.shape[0] - 2 * TP - TP * far,
                                     ap=[[1, TP], [1, TP]])
                    sp.dma_start(windows[:, n, far], window).then_inc(loads, 16)

        @block.vector
        def _(dve):
            st = Steps(dve, steps_v)
            dve.wait_ge(loads, 16 * 11)
            nc.vector.tensor_copy(decay[:], windows[:, 0, :, ::-1]).then_inc(turned_round, 1)
            nc.vector.tensor_copy(steps[:], windows[:, 1, :, ::-1]).then_inc(turned_round, 1)
            st.then(nc.vector.tensor_scalar(rest[:], mix[:], -1.0, 1.0, ALU.mult, ALU.add))
            for n in range(3):
                st.then(nc.vector.tensor_scalar(mixed[:, n], x, mix[:, n:n + 1], None, ALU.mult))
                nc.vector.scalar_tensor_tensor(out=mixed[:, n, :, 1:T], in0=x[:, :, 0:T - 1], scalar=rest[:, n:n + 1],
                                               in1=mixed[:, n, :, 1:T], op0=ALU.mult, op1=ALU.add).then_inc(mix_ready, 1)
            dve.wait_ge(projected, 4)
            nc.vector.tensor_scalar(k[:], banks[0:TP, 0:4, :].rearrange("p q (j c) -> p (q j) c", c=C), 30.0, -60.0,
                                    ALU.min, ALU.max).then_inc(k_clipped, 1)
            dve.wait_ge(projected, 8)
            dve.wait_ge(k_ready, 1)
            nc.vector.tensor_tensor(kv[:], banks[0:TP, 4:8, :].rearrange("p q (j c) -> p (q j) c", c=C), k[:],
                                    ALU.mult).then_inc(kv_ready, 1)
            dve.wait_ge(summed, 1)
            st.then(nc.vector.reciprocal(inv[:], banks[0:TP, 0:4, :]))
            dve.wait_ge(r_ready, 1)
            dve.wait_ge(summed, 2)
            for half in range(2):
                zh = z[:].rearrange("p (b t) c -> p t b c", t=2)[:, half]
                rh = r[:].rearrange("p (b t) c -> p t b c", t=2)[:, half]
                w = banks[0:TP, 4 + 2 * half:6 + 2 * half, :].rearrange("p q (b c) -> p (q b) c", c=C)
                i = inv[:, 2 * half:2 * half + 2, :].rearrange("p q (b c) -> p (q b) c", c=C)
                st.then(nc.vector.tensor_tensor(zh, w, rh, ALU.mult))
                nc.vector.tensor_tensor(zh, zh, i, ALU.mult).then_inc(z_ready, 1)
            for q in range(4):
                dve.wait_ge(out_ready, q + 1)
                part = g.h[:, 8 * q:8 * q + 8, :]
                nc.vector.tensor_tensor(part, part, banks[0:TP, q, :].rearrange("p (j c) -> p j c", j=8), ALU.add)

        @block.scalar
        def _(act):
            act.wait_ge(k_clipped, 1)
            nc.scalar.activation(k[:], k[:], ACT.Exp).then_inc(k_ready, 1)
            act.wait_ge(projected, 12)
            nc.scalar.activation(r[:], banks[0:TP, 0:4, :].rearrange("p q (j c) -> p (q j) c", c=C),
                                 ACT.Sigmoid).then_inc(r_ready, 1)
            for n in range(NG):
                act.wait_ge(turned, n + 1)
                nc.scalar.copy(zT[:, GC * n:GC * n + GC], banks[0:C, n, 0:GC]).then_inc(zT_ready, 1)

        @block.tensor
        def _(pe):
            pe.wait_ge(loads, 16 * 11)
            for n in range(3):
                pe.wait_ge(mix_ready, n + 1)
                if n == 2:
                    pe.wait_ge(k_clipped, 1)
                for j in range(NT):
                    ins = nc.tensor.matmul(banks[0:TP, 4 * (n % 2) + j // 8, C * (j % 8):C * (j % 8) + C],
                                           mixed[:, n, j // 2, TP * (j % 2):TP * (j % 2) + TP], w3[:, n],
                                           start=True, stop=True)
                    if j % 8 == 7:
                        ins.then_inc(projected, 1)
            pe.wait_ge(turned_round, 2)
            for src, tri, bank, waits in ((k, steps, 0, ((k_ready, 1), (r_ready, 1))), (kv, decay, 4, ((kv_ready, 1),))):
                for sem, value in waits:
                    pe.wait_ge(sem, value)
                halves = src[:].rearrange("p (b t) c -> p t b c", t=2)
                for half in range(2):
                    for q in range(2):
                        out = banks[0:TP, bank + 2 * half + q, :]
                        for u in range(half + 1):
                            ins = nc.tensor.matmul(out, tri[:, half - u], halves[:, u, 8 * q:8 * q + 8, :],
                                                   start=(u == 0), stop=(u == half))
                ins.then_inc(summed, 1)
            pe.wait_ge(z_ready, 2)
            for j in range(NT):
                ins = nc.tensor.transpose(banks[0:C, j // GT, TP * (j % GT):TP * (j % GT) + TP], z[:, j, :],
                                          g.ident[0:TP, 0:TP])
                if j % GT == GT - 1:
                    ins.then_inc(turned, 1)
            pe.wait_ge(zT_ready, NG)
            for j in range(NT):
                ins = nc.tensor.matmul(banks[0:TP, j // 8, C * (j % 8):C * (j % 8) + C], zT[:, TP * j:TP * j + TP],
                                       wo[:], start=True, stop=True)
                if j % 8 == 7:
                    ins.then_inc(out_ready, 1)


def memory_attention(nc, g, A):
    HEADS, D, KEYS, TOP = 8, C, 64, 16
    RUNS = [TOP // (r + 1) for r in range(TOP // 2)]
    CAND = sum(RUNS) + TOP // 2
    NUM_KV = KEYS * KEYS
    SEEN = TP + T
    PAIRS = HEADS // 2
    BODY_STEPS = 552
    with Stage(nc, "me") as s:
        wpkT, keysT = s.sb("wpkT", [D // 2, 2 * HEADS, C]), s.sb("keysT", [D // 2, 2 * HEADS, KEYS])
        wsim = s.sb("wsim", [C, 2, HEADS * KEYS])
        wq, wo = s.sb("wq", [C, HEADS * D]), s.sb("wo", [D, HEADS, C])
        ramp_i, ramp = s.sb("ramp_i", [TP, CAND], I32), s.sb("ramp", [TP, CAND])
        mask = s.sb("mask", [TP, SEEN])
        x = s.sb("x", [C, 2, TP])
        best = [s.sb(f"best{p}", [TP, 2, TOP]) for p in range(2)]
        place, left = s.sb("place", [TP, 2, TOP], U32), s.sb("left", [TP, KEYS])
        cand, cand_left = s.sb("cand", [TP, 2, CAND]), s.sb("cand_left", [TP, CAND])
        final, at, atf = s.sb("final", [TP, 2, HEADS, TOP]), s.sb("at", [TP, TOP], U32), s.sb("atf", [TP, TOP])
        hot, rowf = s.sb("hot", [TP, TOP, CAND]), s.sb("rowf", [TP, TOP])
        row = s.sb("row", [TP, 2, HEADS, TOP], I32)
        lowest, weight = s.sb("lowest", [TP, 2, HEADS]), s.sb("weight", [TP, 2, HEADS, TOP])
        total = s.sb("total", [TP, 2, HEADS])
        rows = s.sb("rows", [TP, 2, TOP, 2 * D])
        kv = s.sb("kv", [TP, 2, 2, HEADS, D])
        kT, v, q = s.sb("kT", [P, PAIRS, T]), s.sb("v", [TP, 2, HEADS, D]), s.sb("q", [P, PAIRS, T])
        seen, neg = s.sb("seen", [TP, 2, SEEN]), s.sb("neg", [TP, 2, 2])
        norm = s.sb("norm", [TP, 2, 2])
        pT, oT = s.sb("pT", [TP, 2, SEEN]), s.sb("oT", [D, 2, T])
        sims = s.ps("sims", [P, 2, BANK])
        qbank = s.ps("qbank", [P, 2, BANK])
        score, turned, outT, out = (s.ps(n, [P, BANK]) for n in ("score", "turned", "outT", "out"))

        loads, folded, ramp_ready = s.sem("loads"), s.sem("folded"), s.sem("ramp_ready")
        mask_zero, mask_ready = s.sem("mask_zero"), s.sem("mask_ready")
        x_ready, sims_ready, chosen, exp_ready = (s.sem(n) for n in ("x_ready", "sims_ready", "chosen", "exp_ready"))
        row_ready, waited = s.sem("row_ready"), s.sem("waited")
        gathered = [s.sem(f"gathered{b}") for b in range(2)]
        weighed, steps_v, steps_l = s.sem("weighed"), s.sem("steps_v"), s.sem("steps_l")
        q_done, q_ready, k_turned, k_ready = (s.sem(n) for n in ("q_done", "q_ready", "k_turned", "k_ready"))
        scored, lowered, raised, inverted = (s.sem(n) for n in ("scored", "lowered", "raised", "inverted"))
        normed, p_turned, p_ready, o_done = (s.sem(n) for n in ("normed", "p_turned", "p_ready", "o_done"))
        o_ready, out_ready, added, waited_v = (s.sem(n) for n in ("o_ready", "out_ready", "added", "waited_v"))
        block = s.block()
        table = A["memory"]

        @block.sync
        def _(sp):
            for dst, src in ((wpkT[:], A["L1_ffn_Wq_pk"]), (keysT[:], A["L1_ffn_pk_keys"]), (wq[:], A["L1_ffn_Wq"]),
                             (wo[:], A["L1_ffn_Wo"])):
                sp.dma_start(dst, src).then_inc(loads, 16)

        @block.gpsimd
        def _(pool):
            nc.gpsimd.iota(ramp_i[:], pattern=[[1, CAND]], base=0, channel_multiplier=0).then_inc(ramp_ready, 1)
            pool.wait_ge(mask_zero, 1)
            for n, start in enumerate((0, TP + TP)):
                part = mask[:, start:start + TP]
                nc.gpsimd.affine_select(out=part, in_=part, compare_op=ALU.is_ge, fill=-3e38, base=0,
                                        pattern=[[-1, TP]], channel_multiplier=1).then_inc(mask_ready, 1)
                pool.wait_ge(mask_ready, n + 1)
            with pool.Fori(0, B) as b:
                for e in range(2):
                    for head in range(HEADS):
                        unit = 2 * HEADS * b + HEADS * e + head
                        buf = head % 2
                        pool.wait_ge(row_ready, unit + 1)
                        pool.wait_ge(weighed, unit + 1)
                        pool.sem_inc(waited, 1)
                        for k in range(TOP):
                            nc.gpsimd.indirect_dma_start(
                                out=rows[:, buf, k, :], out_offset=None, in_=table,
                                in_offset=bass.IndirectOffsetOnAxis(ap=row[:, e, head, k:k + 1], axis=0)) \
                                .then_inc(gathered[buf], 16)

        @block.vector
        def _(dve):
            def tile_of(b, e):
                return 2 * b + e

            def choose(j, e, head, st):
                if head == 0:
                    dve.wait_ge(sims_ready, j + 1)
                for p in range(2):
                    mine = sims[0:TP, p, KEYS * head:KEYS * head + KEYS]
                    vals = best[p][:, 0]
                    dve.sem_inc(waited_v, 1)
                    st.then(nc.vector.max(out=vals[:, 0:8], in_=mine))
                    dve.sem_inc(waited_v, 1)
                    st.done(nc.vector.max_index(out=place[:, p, 0:8], in_max=vals[:, 0:8], in_values=mine))
                    st.then(nc.vector.match_replace(out=left[:], in_to_replace=vals[:, 0:8], in_values=mine,
                                                    imm_value=-3e38))
                    dve.sem_inc(waited_v, 1)
                    st.then(nc.vector.max(out=vals[:, 8:16], in_=left[:]))
                    dve.sem_inc(waited_v, 1)
                    st.then(nc.vector.max_index(out=place[:, p, 8:16], in_max=vals[:, 8:16], in_values=left[:]))
                st.done(nc.vector.tensor_scalar(best[0][:, 1], place[:, 0], float(NUM_KV * head), None, ALU.add))
                st.then(nc.vector.tensor_scalar(best[1][:, 1], place[:, 1], float(KEYS), None, ALU.mult))
                start = 0
                for r, n in enumerate(RUNS):
                    st.done(nc.vector.tensor_tensor(cand[:, :, start:start + n], best[1][:, :, 0:n],
                                                    bc(best[0][:, :, r:r + 1], [TP, 2, n]), ALU.add))
                    start += n
                st.then(nc.vector.tensor_tensor(cand[:, :, start:CAND], best[0][:, :, 8:16],
                                                bc(best[1][:, :, 0:1], [TP, 2, 8]), ALU.add))
                top = final[:, e, head]
                dve.sem_inc(waited_v, 1)
                st.then(nc.vector.max(out=top[:, 0:8], in_=cand[:, 0]))
                dve.sem_inc(waited_v, 1)
                st.done(nc.vector.max_index(out=at[:, 0:8], in_max=top[:, 0:8], in_values=cand[:, 0]))
                st.then(nc.vector.match_replace(out=cand_left[:], in_to_replace=top[:, 0:8], in_values=cand[:, 0],
                                                imm_value=-3e38))
                dve.sem_inc(waited_v, 1)
                st.then(nc.vector.max(out=top[:, 8:16], in_=cand_left[:]))
                dve.sem_inc(waited_v, 1)
                st.done(nc.vector.max_index(out=at[:, 8:16], in_max=top[:, 8:16], in_values=cand_left[:]))
                nc.vector.tensor_scalar(lowest[:, e, head:head + 1], top[:, 0:1], -1.0, None,
                                        ALU.mult).then_inc(chosen, 1)
                dve.wait_ge(st.sem, st.base + st.n)
                st.then(nc.vector.tensor_copy(atf[:], at[:]))
                st.then(nc.vector.tensor_tensor(hot[:], bc(ramp[:].unsqueeze(1), [TP, TOP, CAND]),
                                                bc(atf[:].unsqueeze(2), [TP, TOP, CAND]), ALU.is_equal))
                st.then(nc.vector.tensor_tensor(hot[:], hot[:], bc(cand[:, 1].unsqueeze(1), [TP, TOP, CAND]), ALU.mult))
                st.then(nc.vector.tensor_reduce(rowf[:], hot[:], AX.X, ALU.add))
                nc.vector.tensor_copy(row[:, e, head, :], rowf[:]).then_inc(row_ready, 1)

            def weigh(j, e, head, st, first):
                unit = HEADS * j + head
                buf = head % 2
                w = weight[:, e, head]
                dve.wait_ge(exp_ready, unit + 1)
                st.then(nc.vector.reciprocal(total[:, e, head:head + 1], total[:, e, head:head + 1]))
                st.then(nc.vector.tensor_scalar(w, w, total[:, e, head:head + 1], None, ALU.mult))
                dve.wait_ge(gathered[buf], 256 * (HEADS // 2 * j + head // 2 + 1))
                st.then(nc.vector.tensor_tensor(rows[:, buf], rows[:, buf], bc(w.unsqueeze(2), [TP, TOP, 2 * D]),
                                                ALU.mult))
                if head == 0 and e == 0 and not first:
                    dve.wait_ge(k_ready, 3 * now[0])
                nc.vector.tensor_reduce(kv[:, :, e, head, :], rows[:, buf].rearrange("p k (n d) -> p n d k", n=2),
                                        AX.X, ALU.add).then_inc(weighed, 1)
                dve.wait_ge(weighed, unit + 3)

            def invert(b, head, st):
                dve.wait_ge(raised, 2 * (HEADS * b + head) + 2)
                nc.vector.reciprocal(norm[:, head % 2], norm[:, head % 2]).then_inc(inverted, 1)

            def lower(b, head, st):
                dve.wait_ge(scored, HEADS * b + head + 1)
                mine = seen[:, head % 2]
                st.then(nc.vector.tensor_tensor(mine, score[0:TP, 0:SEEN], mask[:], ALU.add))
                st.done(nc.vector.tensor_reduce(neg[:, head % 2, 0:1], mine[:, 0:TP], AX.X, ALU.max))
                st.then(nc.vector.tensor_reduce(neg[:, head % 2, 1:2], mine[:, TP:SEEN], AX.X, ALU.max))
                nc.vector.tensor_scalar(neg[:, head % 2], neg[:, head % 2], -1.0, None, ALU.mult).then_inc(lowered, 1)

            def add_out(b):
                dve.wait_ge(out_ready, b + 1)
                part = g.h[:, bass.ds(2 * b, 2), :]
                nc.vector.tensor_tensor(part, part, out[0:TP, 0:2 * C].rearrange("p (j c) -> p j c", j=2),
                                        ALU.add).then_inc(added, 1)

            def body(b, attend=True, more=True, st=None):
                now[0] = b
                for e in range(2):
                    if attend and e == 1:
                        invert(b - 1, HEADS - 1, st)
                    for head in range(HEADS):
                        if e == 0 or more:
                            choose(tile_of(b, e) + 1, 1 - e, head, st)
                        weigh(tile_of(b, e), e, head, st, first=not attend)
                        if attend and e == 0:
                            if head:
                                invert(b - 1, head - 1, st)
                            lower(b - 1, head, st)
                    if attend and e == 1:
                        add_out(b - 1)

            now = [0]
            dve.wait_ge(folded, 1)
            nc.vector.tensor_copy(wsim[:], sims[0:C, :, :]).then_inc(folded, 1)
            nc.vector.memset(mask[:], 0.0).then_inc(mask_zero, 1)
            dve.sem_inc(weighed, 2)
            dve.sem_inc(lowered, 1)
            dve.sem_inc(added, 1)
            dve.wait_ge(ramp_ready, 1)
            st = Steps(dve, steps_v)
            st.then(nc.vector.tensor_copy(ramp[:], ramp_i[:]))
            dve.wait_ge(mask_ready, 2)
            for head in range(HEADS):
                choose(0, 0, head, st)
            body(0, attend=False, st=st)
            with dve.Fori(1, B - 1) as b:
                loop = Steps(dve, steps_l, BODY_STEPS * (b - 1))
                body(b, st=loop)
                assert loop.n == BODY_STEPS, loop.n
            body(B - 1, more=False, st=st)
            for head in range(HEADS):
                if head:
                    invert(B - 1, head - 1, st)
                lower(B - 1, head, st)
            invert(B - 1, HEADS - 1, st)
            add_out(B - 1)

        @block.scalar
        def _(act):
            def stage_x(j, buf):
                nc.scalar.copy(x[:, buf, :], g.xT[0:C, bass.ds(TP * j, TP)]).then_inc(x_ready, 1)

            def weights(j, e, head):
                act.wait_ge(chosen, HEADS * j + head + 1)
                nc.scalar.activation(weight[:, e, head], final[:, e, head], ACT.Exp, bias=lowest[:, e, head:head + 1],
                                     accum_out=total[:, e, head:head + 1]).then_inc(exp_ready, 1)

            def attend(b, head):
                n = HEADS * b + head
                act.wait_ge(lowered, n + 2)
                mine = seen[:, head % 2]
                for i, cols in enumerate((slice(0, TP), slice(TP, SEEN))):
                    nc.scalar.activation(mine[:, cols], mine[:, cols], ACT.Exp, bias=neg[:, head % 2, i:i + 1],
                                         accum_out=norm[:, head % 2, i:i + 1]).then_inc(raised, 1)
                act.wait_ge(inverted, n + 1)
                for i, cols in enumerate((slice(0, TP), slice(TP, SEEN))):
                    nc.scalar.activation(mine[:, cols], mine[:, cols], ACT.Copy,
                                         scale=norm[:, head % 2, i:i + 1]).then_inc(normed, 1)
                act.wait_ge(p_turned, n + 1)
                nc.scalar.copy(pT[:, head % 2], turned[0:TP, 0:SEEN]).then_inc(p_ready, 1)
                act.wait_ge(o_done, n + 1)
                nc.scalar.copy(oT[:, head % 2], outT[0:D, 0:T]).then_inc(o_ready, 1)

            def body(b, attending=True, more=True):
                stage_x(2 * b + 1, 1)
                for head in range(HEADS):
                    weights(2 * b + 1, 1, head)
                    if attending:
                        attend(b - 1, head)
                for bank in range(2):
                    act.wait_ge(q_done, 2 * b + bank + 1)
                    nc.scalar.mul(q[:, 2 * bank:2 * bank + 2].rearrange("p h t -> p (h t)"), qbank[:, bank, 0:2 * T],
                                  D ** -0.5).then_inc(q_ready, 1)
                if more:
                    stage_x(2 * b + 2, 0)
                    for head in range(HEADS):
                        weights(2 * b + 2, 0, head)
                for e, src in enumerate((turned, outT)):
                    act.wait_ge(k_turned, 2 * b + e + 1)
                    nc.scalar.copy(kT[:, :, TP * e:TP * e + TP], src[:, 0:4 * TP].rearrange("p (n t) -> p n t", n=4)) \
                        .then_inc(k_ready, 1)
                nc.scalar.copy(v[:], kv[:, 1]).then_inc(k_ready, 1)

            act.sem_inc(p_ready, 1)
            act.sem_inc(o_ready, 1)
            stage_x(0, 0)
            for head in range(HEADS):
                weights(0, 0, head)
            body(0, attending=False)
            with act.Fori(1, B - 1) as b:
                body(b)
            body(B - 1, more=False)
            for head in range(HEADS):
                attend(B - 1, head)

        @block.tensor
        def _(pe):
            def find(j, buf, first=False):
                pe.wait_ge(x_ready, j + 1)
                if not first:
                    pe.wait_ge(row_ready, HEADS * j)
                for p in range(2):
                    ins = nc.tensor.matmul(sims[0:TP, p, :], x[:, buf, :], wsim[:, p, :], start=True, stop=True)
                ins.then_inc(sims_ready, 1)

            def attend_scores(b, head):
                n = HEADS * b + head
                if head == 0:
                    pe.wait_ge(k_ready, 3 * b + 3)
                    pe.wait_ge(q_ready, 2 * b + 2)
                pe.wait_ge(lowered, n + 1)
                r = slice(D * (head % 2), D * (head % 2) + D)
                nc.tensor.matmul(score[0:TP, 0:TP], q[r, head // 2, 0:TP], kT[r, head // 2, 0:TP], start=True, stop=True)
                nc.tensor.matmul(score[0:TP, TP:SEEN], q[r, head // 2, TP:T], kT[r, head // 2, :], start=True,
                                 stop=True).then_inc(scored, 1)

            def attend_rest(b, head):
                n = HEADS * b + head
                pe.wait_ge(normed, 2 * n + 2)
                pe.wait_ge(p_ready, n + 1)
                probs = seen[:, head % 2]
                for i in range(3):
                    ins = nc.tensor.transpose(turned[0:TP, TP * i:TP * i + TP], probs[:, TP * i:TP * i + TP],
                                              g.ident[0:TP, 0:TP])
                ins.then_inc(p_turned, 1)
                pe.wait_ge(p_ready, n + 2)
                pe.wait_ge(o_ready, n + 1)
                nc.tensor.matmul(outT[0:D, 0:T], v[:, 0, head], pT[:, head % 2, 0:T], start=True, stop=False,
                                 skip_group_check=True)
                nc.tensor.matmul(outT[0:D, TP:T], v[:, 1, head], pT[:, head % 2, T:SEEN], start=False, stop=True,
                                 skip_group_check=True).then_inc(o_done, 1)
                pe.wait_ge(o_ready, n + 2)
                if head == 0:
                    pe.wait_ge(added, b + 1)
                for i in range(2):
                    ins = nc.tensor.matmul(out[0:TP, C * i:C * i + C], oT[:, head % 2, TP * i:TP * i + TP], wo[:, head],
                                           start=(head == 0 and i == 0), stop=(head == HEADS - 1),
                                           skip_group_check=True)
                if head == HEADS - 1:
                    ins.then_inc(out_ready, 1)

            def attend(b):
                for head in range(HEADS):
                    attend_scores(b, head)
                    if head:
                        attend_rest(b, head - 1)
                attend_rest(b, HEADS - 1)

            def body(b, attending=True, more=True):
                find(2 * b + 1, 1)
                if attending:
                    attend(b - 1)
                if attending:
                    pe.wait_ge(q_ready, 2 * b)
                for pair in range(PAIRS):
                    ins = nc.tensor.matmul(qbank[:, pair // 2, T * (pair % 2):T * (pair % 2) + T],
                                           wq[:, P * pair:P * pair + P], x[:].rearrange("c e t -> c (e t)"),
                                           start=True, stop=True)
                    if pair % 2:
                        ins.then_inc(q_done, 1)
                if more:
                    find(2 * b + 2, 0)
                for e, dst in enumerate((turned, outT)):
                    pe.wait_ge(weighed, 2 + HEADS * (2 * b + e + 1))
                    for pair in range(PAIRS):
                        ins = nc.tensor.transpose(dst[:, TP * pair:TP * pair + TP],
                                                  kv[:, 0, e, 2 * pair:2 * pair + 2, :].rearrange("p h d -> p (h d)"),
                                                  g.ident[0:TP, 0:TP])
                    ins.then_inc(k_turned, 1)

            pe.wait_ge(loads, 16 * 4)
            for n in range(2 * HEADS):
                ins = nc.tensor.matmul(sims[0:C, n // HEADS, KEYS * (n % HEADS):KEYS * (n % HEADS) + KEYS], wpkT[:, n],
                                       keysT[:, n], start=True, stop=True)
            ins.then_inc(folded, 1)
            pe.wait_ge(folded, 2)
            find(0, 0, first=True)
            body(0, attending=False)
            with pe.Fori(1, B - 1) as b:
                body(b)
            body(B - 1, more=False)
            attend(B - 1)


def rnn(nc, g, A):
    HID, KC, S = 256, 2, 11
    CHUNKS = T // S
    PARTS = 3
    with Stage(nc, "rc") as s:
        wi0, more0 = s.sb("wi0", [C + 1, HID]), s.sb("more0", [C + 1, HID])
        wh0, wi1, wh1 = (s.sb(n, [P, KC, HID]) for n in ("wh0", "wi1", "wh1"))
        bi1, more1 = s.sb("bi1", [1, HID]), s.sb("more1", [1, HID])
        fc, fc_b, ones = s.sb("fc", [P, KC, C]), s.sb("fc_b", [1, C]), s.sb("ones", [1, S * B])
        h0 = s.sb("h0", [P, 2, KC, S, B])
        h1 = s.sb("h1", [P, KC, B, T])
        w0, w1 = (s.sb(n, [P, PARTS, KC, HID], BF16) for n in ("w0", "w1"))
        w_rest = s.sb("w_rest", [P, KC, HID])
        a0, a1 = (s.sb(n, [P, 2, PARTS, KC, B], BF16) for n in ("a0", "a1"))
        rest0, rest1 = s.sb("rest0", [P, KC, B]), s.sb("rest1", [P, KC, B])
        sum0, sum1 = s.ps("sum0", [P, 2, BANK]), s.ps("sum1", [P, 2, BANK])
        final = s.ps("final", [TP, 4, BANK])
        loads, ready = s.sem("loads"), s.sem("ready")
        summed0, summed1, tanh0, tanh1, out_ready = (s.sem(n) for n in ("summed0", "summed1", "tanh0", "tanh1", "out_ready"))
        lead0, lead1, left0, left1 = (s.sem(n) for n in ("lead0", "lead1", "left0", "left1"))
        split0, split1, steps_w = s.sem("split0"), s.sem("split1"), s.sem("steps_w")
        block = s.block()
        x = g.xT[:].rearrange("c (b t) -> c t b", b=B)

        @block.sync
        def _(sp):
            for dst, name in ((wi0[0:C, :], "W_ih_0"), (wi0[C:C + 1, :], "b_ih_0"), (more0[C:C + 1, :], "b_hh_0"),
                              (wh0[:], "W_hh_0"), (wi1[:], "W_ih_1"), (wh1[:], "W_hh_1"), (bi1[:], "b_ih_1"),
                              (more1[:], "b_hh_1"), (fc[:], "fc_w"), (fc_b[:], "fc_b")):
                sp.dma_start(dst, A["L2_attn_" + name]).then_inc(loads, 16)

        @block.vector
        def _(dve):
            dve.wait_ge(loads, 16 * 10)
            nc.vector.memset(ones[:], 1.0).then_inc(ready, 1)
            nc.vector.tensor_tensor(wi0[C:C + 1, :], wi0[C:C + 1, :], more0[C:C + 1, :], ALU.add).then_inc(ready, 1)
            nc.vector.tensor_tensor(bi1[:], bi1[:], more1[:], ALU.add).then_inc(ready, 1)
            st = Steps(dve, steps_w)
            for w, parts in ((wh0, w0), (wh1, w1)):
                st.then(nc.vector.tensor_copy(parts[:, 0], w[:]))
                st.then(nc.vector.tensor_tensor(w_rest[:], w[:], parts[:, 0], ALU.subtract))
                st.then(nc.vector.tensor_copy(parts[:, 1], w_rest[:]))
                nc.vector.tensor_tensor(parts[:, 2], w_rest[:], parts[:, 1], ALU.subtract).then_inc(ready, 1)
                dve.wait_ge(ready, 4 if w is wh0 else 5)

            def split(h, parts, rest, n, tanh, lead, left, done, first=False):
                dve.wait_ge(tanh, n + 1)
                nc.vector.tensor_copy(parts[:, 0], h).then_inc(lead, 1)
                dve.wait_ge(lead, n + 1)
                nc.vector.tensor_tensor(parts[:, 1], h, parts[:, 0], ALU.subtract).then_inc(done, 1)
                if not first:
                    dve.wait_ge(done, 2 * n)
                nc.vector.tensor_tensor(rest[:], h, parts[:, 0], ALU.subtract).then_inc(left, 1)
                dve.wait_ge(left, n + 1)
                nc.vector.tensor_tensor(parts[:, 2], rest[:], parts[:, 1], ALU.subtract).then_inc(done, 1)

            def turn(c, buf, has0=True, has1=True, start0=False, start1=False):
                for t in range(S):
                    if has0:
                        split(h0[:, buf, :, t], a0[:, (S * buf + t) % 2], rest0, S * c + t, tanh0, lead0,
                              left0, split0, start0 and t == 0)
                    if has1:
                        n = S * (c - 1) + t
                        split(h1[:, :, :, bass.ds(n, 1)].rearrange("p m b o -> p m (b o)"),
                              a1[:, (S * (1 - buf) + t) % 2], rest1, n, tanh1, lead1, left1, split1,
                              start1 and t == 0)

            turn(0, 0, has1=False, start0=True)
            turn(1, 1, start1=True)
            with dve.Fori(1, CHUNKS // 2) as i:
                turn(2 * i, 0)
                turn(2 * i + 1, 1)
            turn(CHUNKS, 0, has0=False)
            for q in range(4):
                dve.wait_ge(out_ready, q + 1)
                part = g.h[:, 8 * q:8 * q + 8, :]
                nc.vector.tensor_tensor(part, part, final[:, q, :].rearrange("p (j c) -> p j c", j=8), ALU.add)

        @block.tensor
        def _(pe):
            def columns(bank, m, t=None):
                cols = bank[:, S * B * m:S * B * m + S * B]
                return cols if t is None else cols[:, B * t:B * t + B]

            def input0(c, buf):
                for m in range(KC):
                    ins = nc.tensor.matmul(columns(sum0[:, buf], m), wi0[:, P * m:P * m + P], x[:, bass.ds(S * c, S), :],
                                           start=(m == 0), stop=False, skip_group_check=True)
                return ins

            def input1(c, buf):
                pe.wait_ge(tanh0, S * c + S)
                for m in range(KC):
                    nc.tensor.matmul(columns(sum1[:, buf], m), bi1[:, P * m:P * m + P], ones[:], start=(m == 0),
                                     stop=False, skip_group_check=True)
                    for k in range(KC):
                        ins = nc.tensor.matmul(columns(sum1[:, buf], m), wi1[:, k, P * m:P * m + P],
                                               h0[:, buf, k].rearrange("p s b -> p (s b)"), start=False, stop=False,
                                               skip_group_check=True)
                return ins

            def step(bank, w, t, parts, n, lead, split):
                pe.wait_ge(lead, n)
                for part in range(PARTS):
                    if part:
                        pe.wait_ge(split, 2 * n - 2 + part)
                    for m in range(KC):
                        for k in range(KC):
                            for w_part in range(PARTS - part):
                                ins = nc.tensor.matmul(columns(bank, m, t), w[:, w_part, k, P * m:P * m + P],
                                                       parts[:, part, k], start=False, stop=(part == PARTS - 1),
                                                       skip_group_check=True)
                return ins

            def turn(c, buf, has0=True, has1=True, start0=False, start1=False, more=True):
                for t in range(S):
                    if has0 and not (start0 and t == 0):
                        step(sum0[:, buf], w0, t, a0[:, (S * buf + t + 1) % 2], S * c + t, lead0,
                             split0).then_inc(summed0, 1)
                    if has1:
                        if t == 0:
                            ins = input1(c - 1, 1 - buf)
                            if start1:
                                ins.then_inc(summed1, 1)
                        if not (start1 and t == 0):
                            step(sum1[:, 1 - buf], w1, t, a1[:, (S * (1 - buf) + t + 1) % 2], S * (c - 1) + t,
                                 lead1, split1).then_inc(summed1, 1)
                    if t == S // 2 and has0 and more:
                        input0(c + 1, 1 - buf)

            pe.wait_ge(ready, 5)
            input0(0, 0).then_inc(summed0, 1)
            turn(0, 0, has1=False, start0=True)
            turn(1, 1, start1=True)
            with pe.Fori(1, CHUNKS // 2 - 1) as i:
                turn(2 * i, 0)
                turn(2 * i + 1, 1)
            turn(CHUNKS - 2, 0)
            turn(CHUNKS - 1, 1, more=False)
            turn(CHUNKS, 0, has0=False)
            pe.wait_ge(tanh1, T)
            for j in range(NT):
                out = final[:, j // 8, C * (j % 8):C * (j % 8) + C]
                nc.tensor.matmul(out, ones[:, 0:TP], fc_b[:], start=True, stop=False)
                for k in range(KC):
                    ins = nc.tensor.matmul(out, h1[:, k, j // 2, TP * (j % 2):TP * (j % 2) + TP], fc[:, k],
                                           start=False, stop=(k == KC - 1))
                if j % 8 == 7:
                    ins.then_inc(out_ready, 1)

        @block.scalar
        def _(act):
            def turn(c, buf, has0=True, has1=True):
                for t in range(S):
                    cols = slice(B * t, B * t + B)
                    if has0:
                        act.wait_ge(summed0, S * c + t + 1)
                        total = sum0[:, buf, 0:KC * S * B].rearrange("p (m n) -> p m n", m=KC)[:, :, cols]
                        nc.scalar.activation(h0[:, buf, :, t], total, ACT.Tanh).then_inc(tanh0, 1)
                    if has1:
                        act.wait_ge(summed1, S * (c - 1) + t + 1)
                        total = sum1[:, 1 - buf, 0:KC * S * B].rearrange("p (m n) -> p m n", m=KC)[:, :, cols]
                        nc.scalar.activation(h1[:, :, :, bass.ds(S * (c - 1) + t, 1)]
                                             .rearrange("p m b o -> p m (b o)"), total, ACT.Tanh).then_inc(tanh1, 1)

            turn(0, 0, has1=False)
            turn(1, 1)
            with act.Fori(1, CHUNKS // 2) as i:
                turn(2 * i, 0)
                turn(2 * i + 1, 1)
            turn(CHUNKS, 0, has0=False)


def experts(nc, g, A):
    E, HID = 8, 128
    with Stage(nc, "ex") as s:
        gate = s.sb("gate", [TP, NT, E])
        w1, b1, w2 = s.sb("w1", [P, E * HID]), s.sb("b1", [P, E]), s.sb("w2", [HID, E, C])
        route(nc, g, "er", A["L2_ffn_Wg"], (A["L2_ffn_bg"], A["L2_ffn_bias"]), gate, E)
        run_experts(nc, g, "ee", gate, w1, b1, w2, A["L2_ffn_b2"], E, 1, ACT.Relu,
                    ((w1[0:C, :], A["L2_ffn_W1"]), (w1[C:P, :], A["L2_ffn_W1"]), (b1[:], A["L2_ffn_b1"]),
                     (w2[:], A["L2_ffn_W2"])))


def sigmoid_attention(nc, g, A):
    HEADS, F = 8, C
    SCALE = float(F) ** 0.5
    LO, HI = slice(0, C), slice(C, P)
    with Stage(nc, "sa") as s:
        wqT, wvT = (s.sb(n, [F, HEADS, 2, C]) for n in ("wqT", "wvT"))
        wkT, wo = s.sb("wkT", [F, HEADS, C]), s.sb("wo", [F, HEADS, C])
        w_rest = s.sb("w_rest", [C, HEADS * C])
        wq11, wq22, wq31 = (s.sb(n, [P, HEADS, 2, C], BF16) for n in ("wq11", "wq22", "wq31"))
        wv11, wv22, wv31 = (s.sb(n, [P, HEADS * C], BF16) for n in ("wv11", "wv22", "wv31"))
        x12, x13 = s.sb("x12", [P, N], BF16), s.sb("x13", [P, N], BF16)
        x_rest, q_rest = s.sb("x_rest", [P, GC]), s.sb("q_rest", [C, T])
        q11, q22, q31 = (s.sb(n, [P, 2, T], BF16) for n in ("q11", "q22", "q31"))
        v, probs = s.sb("v", [TP, 2, 2, HEADS * C]), s.sb("probs", [TP, 2, 2, T])
        v_banks, q_banks = s.ps("v_banks", [TP, 2, BANK]), s.ps("q_banks", [P, 2, BANK])
        score, out = s.ps("score", [TP, 2, BANK]), s.ps("out", [TP, BANK])
        loads, folded, folded_out, steps_w = s.sem("loads"), s.sem("folded"), s.sem("folded_out"), s.sem("steps_w")
        led, left, split, held = s.sem("led"), s.sem("left"), s.sem("split"), s.sem("held")
        q_done, q_led, q_left, q_split = s.sem("q_done"), s.sem("q_led"), s.sem("q_left"), s.sem("q_split")
        v_done, v_ready, scored, squashed = s.sem("v_done"), s.sem("v_ready"), s.sem("scored"), s.sem("squashed")
        weighted, added = s.sem("weighted"), s.sem("added")
        block = s.block()

        @block.sync
        def _(sp):
            for dst, name in ((wqT[:, :, 0], "Wq"), (wqT[:, :, 1], "Wq"), (wvT[:, :, 0], "Wv"), (wvT[:, :, 1], "Wv"),
                              (wkT[:], "Wk"), (wo[:], "Wo")):
                sp.dma_start(dst, A["L3_attn_" + name]).then_inc(loads, 16)

        @block.tensor
        def _(pe):
            pe.wait_ge(loads, 16 * 6)
            for n, (a, b) in enumerate(((wqT, wkT), (wvT, wo))):
                for head in range(HEADS):
                    ins = nc.tensor.matmul(q_banks[:, n, C * head:C * head + C],
                                           a[:, head].rearrange("f e c -> f (e c)"), b[:, head], start=True, stop=True)
                ins.then_inc(folded, 1)

            def project_v(b):
                pe.wait_ge(v_ready, b + 1)
                for half in range(2):
                    for i, (w, x) in enumerate(((wv11, x12), (wv22, x12), (wv31, x13))):
                        ins = nc.tensor.matmul(v_banks[:, half, :], x[:, bass.ds(T * b + TP * half, TP)], w[:],
                                               start=(i == 0), stop=(i == 2))
                ins.then_inc(v_done, 1)

            def project_q(b, head):
                for i, (w, x) in enumerate(((wq11, x12), (wq22, x12), (wq31, x13))):
                    ins = nc.tensor.matmul(q_banks[:, head % 2, 0:T], w[:, head].rearrange("c e o -> c (e o)"),
                                           x[:, bass.ds(T * b, T)], start=(i == 0), stop=(i == 2))
                ins.then_inc(q_done, 1)

            def scores(b, head):
                u = HEADS * b + head
                pe.wait_ge(q_split, 3 * u + 3)
                pe.wait_ge(squashed, u + 1)
                for half in range(2):
                    for i, (q, x) in enumerate(((q11, x12), (q22, x12), (q31, x13))):
                        ins = nc.tensor.matmul(score[:, head % 2, T * half:T * half + T],
                                               x[:, bass.ds(T * b + TP * half, TP)], q[:, head % 2, :],
                                               start=(i == 0), stop=(i == 2))
                ins.then_inc(scored, 1)

            def weigh(b, buf, head):
                if head == 0:
                    pe.wait_ge(v_ready, b + 2)
                    pe.wait_ge(added, b + 1)
                pe.wait_ge(squashed, HEADS * b + head + 3)
                for tile in range(2):
                    for u in range(2):
                        ins = nc.tensor.matmul(out[:, C * tile:C * tile + C],
                                               probs[:, head % 2, u, TP * tile:TP * tile + TP],
                                               v[:, buf, u, C * head:C * head + C],
                                               start=(head == 0 and tile == 0 and u == 0),
                                               stop=(head == HEADS - 1 and u == 1), skip_group_check=True)
                ins.then_inc(weighted, 1)

            def turn(i, first=False, last=False):
                for e in range(2):
                    b = 2 * i + e
                    for head in range(HEADS):
                        scores(b, head)
                        if e == 1 and head == 2 and not last:
                            pe.wait_ge(split, 3 * i + 6)
                        if head < HEADS - 2:
                            project_q(b, head + 2)
                        elif not (last and e == 1):
                            project_q(b + 1, head + 2 - HEADS)
                        if head == 2 and not (last and e == 1):
                            project_v(b + 1)
                        if head:
                            weigh(b, e, head - 1)
                        elif not (first and e == 0):
                            weigh(b - 1, 1 - e, HEADS - 1)

            pe.wait_ge(folded_out, 2)
            pe.wait_ge(split, 3)
            project_q(0, 0)
            project_q(0, 1)
            project_v(0)
            turn(0, first=True)
            with pe.Fori(1, B // 2 - 1) as i:
                turn(i)
            turn(B // 2 - 1, last=True)
            weigh(B - 1, 1, HEADS - 1)

        @block.gpsimd
        def _(pool):
            split_tokens(g, nc.gpsimd, 0, x12, x13, x_rest, led, left, split, first=True)
            with pool.Fori(1, NG) as n:
                split_tokens(g, nc.gpsimd, n, x12, x13, x_rest, led, left, split, held=held)

        @block.scalar
        def _(act):
            act.sem_inc(squashed, 2)

            def lead(b, head):
                act.wait_ge(q_done, HEADS * b + head + 1)
                nc.scalar.copy(q11[:, head % 2], q_banks[:, head % 2, 0:T]).then_inc(q_led, 1)

            def squash(b, head):
                act.wait_ge(scored, HEADS * b + head + 1)
                act.wait_ge(weighted, HEADS * b + head + 1)
                nc.scalar.activation(probs[:, head % 2].rearrange("p u t -> p (u t)"), score[:, head % 2, 0:2 * T],
                                     ACT.Sigmoid, scale=SCALE).then_inc(squashed, 1)

            def sequence(b, last=False):
                for head in range(HEADS):
                    squash(b, head)
                    if head < HEADS - 2:
                        lead(b, head + 2)
                    elif not last:
                        lead(b + 1, head + 2 - HEADS)

            lead(0, 0)
            lead(0, 1)
            with act.Fori(0, B // 2 - 1) as i:
                for e in range(2):
                    sequence(2 * i + e)
            sequence(B - 2)
            sequence(B - 1, last=True)

        @block.vector
        def _(dve):
            st = Steps(dve, steps_w)
            for n, (w11, w22, w31) in enumerate(((wq11[:, :, 0], wq22[:, :, 0], wq31[:, :, 0]), (wv11, wv22, wv31))):
                dve.wait_ge(folded, n + 1)
                if n == 0:
                    shape = "p (h c) -> p h c"
                    bank, rest = q_banks[:, 0, :].rearrange(shape, c=C), w_rest[:].rearrange(shape, c=C)
                else:
                    bank, rest = q_banks[:, 1, :], w_rest
                st.then(nc.vector.tensor_copy(w11[:], bank))
                st.done(nc.vector.tensor_tensor(w22[:], bank, w11[:], ALU.subtract))
                st.done(nc.vector.tensor_tensor(rest[:], bank[LO], w11[LO], ALU.subtract))
                st.then(nc.vector.tensor_copy(w31[HI], w11[HI]))
                st.then(nc.vector.tensor_tensor(w31[LO], rest[:], w22[LO], ALU.subtract))
                if n == 0:
                    for w in (wq11, wq22, wq31):
                        st.then(nc.vector.tensor_copy(w[:, :, 1], w[:, :, 0]))
                dve.sem_inc(folded_out, 1)
            dve.sem_inc(v_ready, 1)
            dve.sem_inc(added, 1)
            dve.sem_inc(weighted, 2)

            def split_q(b, head, first=False):
                u, buf = HEADS * b + head, head % 2
                q = q_banks[:, buf, 0:T]
                dve.wait_ge(q_led, u + 1)
                if not first:
                    dve.wait_ge(q_split, 3 * u)
                nc.vector.tensor_tensor(q_rest[:], q[LO], q11[LO, buf], ALU.subtract).then_inc(q_left, 1)
                nc.vector.tensor_tensor(q22[:, buf], q, q11[:, buf], ALU.subtract).then_inc(q_split, 1)
                nc.vector.tensor_copy(q31[HI, buf], q11[HI, buf]).then_inc(q_split, 1)
                dve.wait_ge(q_left, u + 1)
                dve.wait_ge(q_split, 3 * u + 2)
                nc.vector.tensor_tensor(q31[LO, buf], q_rest[:], q22[LO, buf], ALU.subtract).then_inc(q_split, 1)

            def take_v(b, buf):
                dve.wait_ge(v_done, b + 1)
                nc.vector.tensor_copy(v[:, buf], v_banks[:]).then_inc(v_ready, 1)

            def add(b):
                dve.wait_ge(weighted, HEADS * b + HEADS + 2)
                part = g.h[:, bass.ds(2 * b, 2), :]
                nc.vector.scalar_tensor_tensor(out=part, in0=out[:, 0:2 * C].rearrange("p (j c) -> p j c", j=2),
                                               scalar=0.0, in1=part, op0=ALU.max, op1=ALU.add).then_inc(added, 1)

            def turn(i, first=False, last=False):
                for e in range(2):
                    b = 2 * i + e
                    for head in range(HEADS):
                        if head < HEADS - 2:
                            split_q(b, head + 2)
                        elif not (last and e == 1):
                            split_q(b + 1, head + 2 - HEADS)
                        if head == 1 and not (first and e == 0):
                            add(b - 1)
                        if head == 3 and not (last and e == 1):
                            take_v(b + 1, 1 - e)

            split_q(0, 0, first=True)
            split_q(0, 1)
            take_v(0, 0)
            turn(0, first=True)
            with dve.Fori(1, B // 2 - 1) as i:
                turn(i)
            turn(B // 2 - 1, last=True)
            add(B - 1)


def routed_experts(nc, g, A):
    E, HID = 8, 256
    with Stage(nc, "re") as s:
        gate = s.sb("gate", [TP, NT, E])
        w1, w2 = s.sb("w1", [P, E * HID]), s.sb("w2", [P, 2 * E, C])
        b1 = s.sb("b1", [P, 2 * E])
        xn = s.sb("xn", [TP, NT, C])
        normalise(nc, g, "rn", kept=xn)
        route(nc, g, "rr", A["L3_ffn_Wr"], (A["L3_ffn_br"],), gate, E)
        normalise(nc, g, "rm", src=xn)
        with Stage(nc, "rf") as f:
            plain, given = f.sb("plain", [P, E, HID]), f.sb("given", [P, 2 * E])
            gain, shift = f.sb("gain", [P, E]), f.sb("shift", [C, E])
            bias = f.ps("bias", [P, 2 * E])
            loads, shifted = f.sem("loads"), f.sem("shifted")
            block = f.block()

            @block.sync
            def _(sp):
                for dst, name in ((plain[0:C], "W1"), (plain[C:P], "W1"), (gain[0:C, :], "ln_g"), (gain[C:P, :], "ln_g"),
                                  (shift[:], "ln_b"), (given[:], "b1")):
                    sp.dma_start(dst, A["L3_ffn_" + name]).then_inc(loads, 16)

            @block.tensor
            def _(pe):
                pe.wait_ge(loads, 16 * 6)
                for k in range(2 * E):
                    ins = nc.tensor.matmul(bias[:, k:k + 1], plain[0:C, k // 2, P * (k % 2):P * (k % 2) + P],
                                           shift[:, k // 2:k // 2 + 1], start=True, stop=True)
                ins.then_inc(shifted, 1)

            @block.vector
            def _(dve):
                dve.wait_ge(loads, 16 * 6)
                for e in range(E):
                    nc.vector.tensor_scalar(w1[:, HID * e:HID * e + HID], plain[:, e], gain[:, e:e + 1], None, ALU.mult)
                dve.wait_ge(shifted, 1)
                nc.vector.tensor_tensor(b1[:], bias[:], given[:], ALU.add)

        run_experts(nc, g, "ru", gate, w1, b1, w2, A["L3_ffn_b2"], E, 2, ACT.Gelu, ((w2[:], A["L3_ffn_W2"]),))


def constants(nc, g, A):
    with Stage(nc, "co") as s:
        cleared, filled = s.sem("cleared"), s.sem("filled")
        block = s.block()

        @block.gpsimd
        def _(pool):
            nc.gpsimd.memset(g.ident[:], 0.0).then_inc(cleared, 1)
            pool.wait_ge(cleared, 1)
            nc.gpsimd.affine_select(out=g.ident[:], in_=g.ident[:], compare_op=ALU.not_equal, fill=1.0,
                                    base=0, pattern=[[-1, P]], channel_multiplier=1)

        @block.vector
        def _(dve):
            nc.vector.memset(g.xT[C:C + 1, :], 1.0)


def store(nc, g, out):
    with Stage(nc, "st") as s:
        stored = s.sem("stored")
        block = s.block()

        @block.sync
        def _(sp):
            sp.dma_start(out.rearrange("b (t p) c -> p (b t) c", p=TP), g.h[:]).then_inc(stored, 16)
            sp.wait_ge(stored, 16)


class Held:

    def __init__(self, nc, ctx):
        self.h = ctx.enter_context(nc.sbuf_tensor("h", [TP, NT, C], F32))
        self.xT = ctx.enter_context(nc.sbuf_tensor("xT", [C + 1, N], F32))
        self.src_table = nc.dram_tensor("src_table", (N, 20), F32).ap()
        self.dst_table = nc.dram_tensor("dst_table", (NT * P, 8), F32).ap()
        self.ident = ctx.enter_context(nc.sbuf_tensor("ident", [P, P], F32))


def layouts(I):
    import numpy as np
    x = np.asarray(I["x"])
    out = {k: np.asarray(v) for k, v in I.items() if k != "x"}
    out["xT"] = x.reshape(2, B // 2, T_IN, C).transpose(0, 3, 1, 2).reshape(P, B // 2, T_IN)
    for k in ("L0_attn_in_proj_w", "L0_attn_x_proj_w", "L0_attn_x_proj_w_b", "L0_attn_dt_proj_w",
              "L0_attn_dt_proj_w_b", "L0_attn_out_proj_w"):
        out[k] = np.ascontiguousarray(out[k].T)
    for k in ("Wq", "Wk", "Wv"):
        out["L3_attn_" + k] = out["L3_attn_" + k].reshape(C, C, 8).transpose(1, 2, 0)
    out["L3_attn_Wo"] = out["L3_attn_Wo"].reshape(C, 8, C)
    for k in ("L0_ffn", "L2_ffn", "L3_ffn"):
        e, _, hid = out[k + "_W1"].shape
        out[k + "_W1"] = out[k + "_W1"].transpose(1, 0, 2).reshape(C, e * hid)
        out[k + "_W2"] = out[k + "_W2"].reshape(e * hid // P, P, C).transpose(1, 0, 2)
        out[k + "_b1"] = out[k + "_b1"].reshape(e * hid // P, P).T
        out[k + "_b2"] = out[k + "_b2"].reshape(1, e * C)
    out["L3_ffn_W1"] = out["L3_ffn_W1"].reshape(C, 8, 256)
    out["L3_ffn_ln_g"], out["L3_ffn_ln_b"] = out["L3_ffn_ln_g"].T, out["L3_ffn_ln_b"].T
    for k in ("W_ih_0", "W_hh_0", "W_ih_1", "W_hh_1", "fc_w"):
        w = out["L2_attn_" + k].T
        out["L2_attn_" + k] = w if k == "W_ih_0" else w.reshape(2, P, w.shape[1]).transpose(1, 0, 2)
    for k in ("b_ih_0", "b_hh_0", "b_ih_1", "b_hh_1", "fc_b"):
        out["L2_attn_" + k] = out["L2_attn_" + k].reshape(1, -1)
    fold = np.zeros((16, 24), np.float32)
    fold[:, 0:16] = np.eye(16, dtype=np.float32)
    for head in range(4):
        fold[4 * head:4 * head + 4, 16 + head] = out["L0_ffn_att_src"][head]
        fold[4 * head:4 * head + 4, 20 + head] = out["L0_ffn_att_dst"][head]
    out["fold"] = fold
    out["L1_ffn_Wq_pk"] = out["L1_ffn_Wq_pk"].reshape(C, 16, 32).transpose(2, 1, 0)
    out["L1_ffn_pk_keys"] = out["L1_ffn_pk_keys"].transpose(3, 0, 2, 1).reshape(32, 16, 64)
    out["L1_ffn_Wo"] = out["L1_ffn_Wo"].reshape(8, C, C).transpose(1, 0, 2)
    out["memory"] = np.concatenate([out.pop("L1_ffn_keys_table"), out.pop("L1_ffn_values_table")], axis=1)
    after = np.zeros(TP, np.float32)
    out["time_curve"] = np.concatenate([out["L1_attn_time_w"], after])
    out["time_steps"] = np.concatenate([np.ones(2 * TP, np.float32), after])
    return out


def recycle(nc, start):
    nc.clear_and_free_semaphores(nc.allocated_since(start))
    nc.all_engine_barrier()


def audio_tower(nc, A, out):
    with ExitStack() as ctx:
        g = Held(nc, ctx)
        start = nc.snapshot_sems()
        constants(nc, g, A)
        pool_windows(nc, g, A)
        stages = (mamba, graph_experts, rwkv, memory_attention, rnn, experts, sigmoid_attention)
        for n, stage in enumerate(stages):
            normalise(nc, g, f"n{n}")
            stage(nc, g, A)
            if n % 2:
                recycle(nc, start)
        recycle(nc, start)
        routed_experts(nc, g, A)
        store(nc, g, out)


def kernel(**inputs):
    import numpy as np
    import concourse.bacc as bacc
    from concourse.bass_utils import run_bass_kernel_spmd

    nc = bacc.Bacc("TRN2", target_bir_lowering=False, num_devices=1)
    arrays, A = {}, {}
    for name, a in layouts(inputs).items():
        a = np.ascontiguousarray(a)
        arrays[f"in_{name}"] = a
        A[name] = nc.dram_tensor(f"in_{name}", a.shape, mybir.dt.from_np(a.dtype), kind="ExternalInput").ap()
    out = nc.dram_tensor("out", (B, T, C), F32, kind="ExternalOutput").ap()
    audio_tower(nc, A, out)
    return run_bass_kernel_spmd(nc, [arrays], core_ids=[0]).results[0]["out"]
```

```python
from contextlib import ExitStack

import concourse.bass as bass
from concourse import mybir

F32 = mybir.dt.float32
BF16 = mybir.dt.bfloat16
I32 = mybir.dt.int32
U32 = mybir.dt.uint32
ALU = mybir.AluOpType
ACT = mybir.ActivationFunctionType
AX = mybir.AxisListType
RMAX = bass.bass_isa.ReduceOp.max

P = 128
B = 16
T_IN = 250
WIN = 9
T = T_IN - WIN + 1
C = 64
N = B * T
TP = T // 2
NT = N // TP
GT = 4
NG = NT // GT
GC = GT * TP
BANK = 512
EPS = 1e-5


class Stage:

    def __init__(self, nc, name):
        self.nc, self.name, self.ctx = nc, name, ExitStack()

    def __enter__(self):
        self.ctx.__enter__()
        return self

    def __exit__(self, *e):
        return self.ctx.__exit__(*e)

    def sb(self, name, shape, dt=F32):
        return self.ctx.enter_context(self.nc.sbuf_tensor(f"{self.name}_{name}", shape, dt))

    def ps(self, name, shape, dt=F32):
        return self.ctx.enter_context(self.nc.psum_tensor(f"{self.name}_{name}", shape, dt))

    def sem(self, name):
        return self.nc.alloc_semaphore(f"{self.name}_{name}")

    def block(self):
        return self.ctx.enter_context(self.nc.Block())


class Steps:

    def __init__(self, eng, sem, base=0):
        self.eng, self.sem, self.base, self.n = eng, sem, base, 0

    def done(self, ins):
        self.n += 1
        ins.then_inc(self.sem, 1)

    def then(self, ins):
        self.done(ins)
        self.eng.wait_ge(self.sem, self.base + self.n)


def bc(ap, shape):
    return ap.to_broadcast(shape)


def pool_windows(nc, g, A):
    HB = B // 2
    COLS = HB * T
    with Stage(nc, "pw") as s:
        wq, wk, vv = (s.sb(n, [P, P]) for n in ("wq", "wk", "vv"))
        bias, vcol = s.sb("bias", [P, 1]), s.sb("vcol", [P, 1])
        xT = s.sb("xT", [P, HB, T_IN])
        q, k = s.sb("q", [P, HB, T_IN]), s.sb("k", [P, HB, T_IN])
        score = s.sb("score", [P, WIN, HB, T])
        work = s.sb("work", [P, 2, HB, T])
        top, den, num = (s.sb(n, [P, HB, T]) for n in ("top", "den", "num"))
        proj = s.ps("proj", [P, 8, BANK])
        loads, projected, copied = s.sem("loads"), s.sem("projected"), s.sem("copied")
        summed, squashed, scored, kept = s.sem("summed"), s.sem("squashed"), s.sem("scored"), s.sem("kept")
        shifted, raised, done, steps_v = s.sem("shifted"), s.sem("raised"), s.sem("done"), s.sem("steps_v")
        totalled = s.sem("totalled")
        turned, steps_z, v_ready = s.sem("turned"), s.sem("steps_z"), s.sem("v_ready")
        block = s.block()

        @block.sync
        def _(sp):
            sp.wait_ge(steps_z, 3)
            sp.dma_start(xT[:], A["xT"]).then_inc(loads, 16)
            for half in range(2):
                r = slice(C * half, C * half + C)
                sp.dma_start(wq[r, r], A["L0_tok_W_qry"]).then_inc(loads, 16)
                sp.dma_start(wk[r, r], A["L0_tok_W_key"]).then_inc(loads, 16)
                sp.dma_start(vcol[r, :], A["L0_tok_v"].unsqueeze(1)).then_inc(loads, 16)
                sp.dma_start(bias[r, :], A["L0_tok_b"].unsqueeze(1)).then_inc(loads, 16)

        @block.tensor
        def _(pe):
            pe.wait_ge(loads, 16 * 9)
            for n, w in enumerate((wq, wk)):
                for c in range(4):
                    nc.tensor.matmul(proj[:, 4 * n + c, 0:2 * T_IN], w[:], xT[:, 2 * c:2 * c + 2, :],
                                     start=True, stop=True).then_inc(projected, 1)
            pe.wait_ge(v_ready, 2)
            for w in range(WIN):
                pe.wait_ge(squashed, w + 1)
                if w < 2:
                    pe.wait_ge(copied, w + 1)
                else:
                    pe.wait_ge(kept, w - 1)
                for c in range(4):
                    ins = nc.tensor.matmul(proj[:, 4 * (w % 2) + c, 0:2 * T], vv[:],
                                           work[:, w % 2, 2 * c:2 * c + 2, :], start=True, stop=True)
                ins.then_inc(scored, 1)
            pe.wait_ge(done, 1)
            pe.wait_ge(kept, WIN)
            for t in range(HB * 2):
                b, half = divmod(t, 2)
                ins = nc.tensor.transpose(proj[0:TP, t // 4, P * (t % 4):P * (t % 4) + P],
                                          num[:, b, TP * half:TP * half + TP], g.ident[:])
                if t % 4 == 3:
                    ins.then_inc(turned, 1)

        @block.scalar
        def _(act):
            for n, dst in enumerate((q, k)):
                act.wait_ge(projected, 4 * n + 4)
                nc.scalar.copy(dst[:].rearrange("p (c b) t -> p c (b t)", c=4),
                               proj[:, 4 * n:4 * n + 4, 0:2 * T_IN]).then_inc(copied, 1)
            for w in range(-1, WIN):
                if w + 1 < WIN:
                    buf = (w + 1) % 2
                    act.wait_ge(summed, w + 2)
                    nc.scalar.activation(work[:, buf], work[:, buf], ACT.Tanh, bias=bias[:]).then_inc(squashed, 1)
                if w < 0:
                    continue
                act.wait_ge(scored, w + 1)
                nc.scalar.copy(score[:, w].rearrange("p (c b) t -> p c (b t)", c=4),
                               proj[:, 4 * (w % 2):4 * (w % 2) + 4, 0:2 * T]).then_inc(kept, 1)
            for w in range(WIN):
                act.wait_ge(shifted, w + 1)
                nc.scalar.activation(score[:, w], score[:, w], ACT.Exp).then_inc(raised, 1)
            for bank in range(4):
                act.wait_ge(turned, bank + 1)
                for half in range(2):
                    dst = g.h[:, 32 // 2 * half + 4 * bank:32 // 2 * half + 4 * bank + 4, :]
                    src = proj[0:TP, bank, :].rearrange("p (t h c) -> p t h c", t=4, h=2)[:, :, half, :]
                    nc.scalar.copy(dst, src)

        @block.vector
        def _(dve):
            st = Steps(dve, steps_v)
            for z in (wq, wk, vv):
                nc.vector.memset(z[:], 0.0).then_inc(steps_z, 1)
            dve.wait_ge(loads, 16 * 9)
            dve.wait_ge(steps_z, 3)
            for half in range(2):
                r = slice(C * half, C * half + C)
                nc.vector.tensor_copy(vv[r, r], bc(vcol[r, :], [C, C])).then_inc(v_ready, 1)
            dve.wait_ge(copied, 2)
            for w in range(WIN + 2):
                if w < WIN:
                    if w >= 2:
                        dve.wait_ge(scored, w - 1)
                    nc.vector.tensor_tensor(work[:, w % 2], q[:, :, WIN // 2:WIN // 2 + T], k[:, :, w:w + T],
                                            ALU.add).then_inc(summed, 1)
                if w >= 3:
                    dve.wait_ge(kept, w - 1)
                    st.then(nc.vector.tensor_tensor(top[:], score[:, 0] if w == 3 else top[:], score[:, w - 2], ALU.max))
            for w in range(WIN):
                nc.vector.tensor_tensor(score[:, w], score[:, w], top[:], ALU.subtract).then_inc(shifted, 1)
            dve.wait_ge(raised, 1)
            st.then(nc.vector.tensor_tensor(num[:], score[:, 0], xT[:, :, 0:T], ALU.mult))
            for w in range(1, WIN):
                dve.wait_ge(raised, w + 1)
                st.then(nc.vector.tensor_tensor(work[:, 0], score[:, w], xT[:, :, w:w + T], ALU.mult))
                st.then(nc.vector.tensor_tensor(num[:], num[:], work[:, 0], ALU.add))
            dve.wait_ge(totalled, WIN - 1)
            st.then(nc.vector.reciprocal(den[:], den[:]))
            nc.vector.tensor_tensor(num[:], num[:], den[:], ALU.mult).then_inc(done, 1)

        @block.gpsimd
        def _(pool):
            for w in range(1, WIN):
                pool.wait_ge(raised, w + 1)
                if w > 1:
                    pool.wait_ge(totalled, w - 1)
                nc.gpsimd.tensor_tensor(den[:], score[:, 0] if w == 1 else den[:], score[:, w],
                                        ALU.add).then_inc(totalled, 1)


def normalise(nc, g, name, src=None, kept=None, fetch=None):
    HALF = NT // 2
    with Stage(nc, name) as s:
        src = g.h if src is None else src
        xc = s.sb("xc", [TP, NT, C]) if kept is None else kept
        sq = s.sb("sq", [TP, NT, C])
        mean, var = s.sb("mean", [TP, NT]), s.sb("var", [TP, NT])
        banks = s.ps("banks", [C, 8, BANK])
        steps, var_ready, root_ready = s.sem("steps"), s.sem("var_ready"), s.sem("root_ready")
        centred, squared, ready, turned = s.sem("centred"), s.sem("squared"), s.sem("ready"), s.sem("turned")
        block = s.block()
        halves = [slice(HALF * i, HALF * i + HALF) for i in range(2)]
        wide = [TP, HALF, C]

        if fetch:
            @block.sync
            def _(sp):
                fetch(sp)

        @block.vector
        def _(dve):
            st = Steps(dve, steps)
            for i, t in enumerate(halves):
                st.then(nc.vector.tensor_reduce(mean[:, t], src[:, t], AX.X, ALU.add))
                st.then(nc.vector.tensor_scalar(mean[:, t], mean[:, t], 1.0 / C, None, ALU.mult))
                nc.vector.tensor_tensor(xc[:, t], src[:, t], bc(mean[:, t].unsqueeze(2), wide),
                                        ALU.subtract).then_inc(centred, 1)
            dve.wait_ge(centred, 2)
            for i, t in enumerate(halves):
                dve.wait_ge(squared, i + 1)
                st.then(nc.vector.tensor_reduce(var[:, t], sq[:, t], AX.X, ALU.add))
                nc.vector.tensor_scalar(var[:, t], var[:, t], 1.0 / C, EPS, ALU.mult, ALU.add).then_inc(var_ready, 1)
            for i, t in enumerate(halves):
                dve.wait_ge(root_ready, i + 1)
                st.then(nc.vector.reciprocal(mean[:, t], var[:, t]))
                nc.vector.tensor_tensor(xc[:, t], xc[:, t], bc(mean[:, t].unsqueeze(2), wide),
                                        ALU.mult).then_inc(ready, 1)
            for n in range(1, NG, 2):
                dve.wait_ge(turned, n + 1)
                nc.vector.tensor_copy(g.xT[0:C, GC * n:GC * n + GC], banks[:, n, 0:GC])

        @block.scalar
        def _(act):
            for i, t in enumerate(halves):
                act.wait_ge(centred, i + 1)
                nc.scalar.activation(sq[:, t], xc[:, t], ACT.Square).then_inc(squared, 1)
            for i, t in enumerate(halves):
                act.wait_ge(var_ready, i + 1)
                nc.scalar.activation(var[:, t], var[:, t], ACT.Sqrt).then_inc(root_ready, 1)
            for n in range(0, NG, 2):
                act.wait_ge(turned, n + 1)
                nc.scalar.copy(g.xT[0:C, GC * n:GC * n + GC], banks[:, n, 0:GC])

        @block.tensor
        def _(pe):
            for j in range(NT):
                if j % HALF == 0:
                    pe.wait_ge(ready, j // HALF + 1)
                ins = nc.tensor.transpose(banks[:, j // GT, TP * (j % GT):TP * (j % GT) + TP], xc[:, j, :],
                                          g.ident[0:TP, 0:TP])
                if j % GT == GT - 1:
                    ins.then_inc(turned, 1)


def choose_two(nc, s, dve, act_in, act_out, st, logits, gate, experts):
    shape = [TP, NT, experts]
    order, eq = s.sb("order", [TP, experts]), s.sb("eq", shape)
    first, second, left = s.sb("first", shape), s.sb("second", shape), s.sb("left", shape)
    best, at, diff = s.sb("two", [TP, 2, NT]), s.sb("at", [TP, NT]), s.sb("diff", [TP, NT])
    share = s.sb("share", [TP, 2, NT])

    def wide(x):
        return bc(x.unsqueeze(2), shape)

    def dve_part():
        for e in range(experts):
            st.done(nc.vector.memset(order[:, e:e + 1], float(experts - e)))
        for n, (src, chosen) in enumerate(((logits, first), (left, second))):
            st.then(nc.vector.tensor_reduce(best[:, n], src[:], AX.X, ALU.max))
            st.then(nc.vector.tensor_tensor(eq[:], src[:], wide(best[:, n]), ALU.is_equal))
            st.then(nc.vector.tensor_tensor(eq[:], eq[:], bc(order[:].unsqueeze(1), shape), ALU.mult))
            st.then(nc.vector.tensor_reduce(at[:], eq[:], AX.X, ALU.max))
            st.then(nc.vector.tensor_tensor(chosen[:], eq[:], wide(at[:]), ALU.is_equal))
            if n == 0:
                st.then(nc.vector.scalar_tensor_tensor(out=left[:], in0=first[:], scalar=-3e38, in1=logits[:],
                                                       op0=ALU.mult, op1=ALU.add))
        nc.vector.tensor_tensor(diff[:], best[:, 1], best[:, 0], ALU.subtract).then_inc(act_in, 1)
        dve.wait_ge(act_out, 1)
        st.then(nc.vector.tensor_scalar(share[:, 0], diff[:], 1.0, None, ALU.add))
        st.then(nc.vector.reciprocal(share[:, 0], share[:, 0]))
        st.then(nc.vector.tensor_tensor(share[:, 1], share[:, 0], diff[:], ALU.mult))
        st.done(nc.vector.tensor_tensor(first[:], first[:], wide(share[:, 0]), ALU.mult))
        st.then(nc.vector.tensor_tensor(second[:], second[:], wide(share[:, 1]), ALU.mult))
        st.then(nc.vector.tensor_tensor(gate[:], first[:], second[:], ALU.add))

    return dve_part, diff


def route(nc, g, name, loads, count, wg, more, gate, experts):
    with Stage(nc, name) as s:
        logits = s.sb("logits", [TP, NT, experts])
        bank = s.ps("bank", [TP, BANK])
        steps = s.sem("steps")
        w_ready, logits_ready = s.sem("w_ready"), s.sem("logits_ready")
        diff_ready, exp_ready = s.sem("diff_ready"), s.sem("exp_ready")
        st = Steps(nc.vector, steps)
        dve_part, diff = choose_two(nc, s, nc.vector, diff_ready, exp_ready, st, logits, gate, experts)
        block = s.block()

        @block.tensor
        def _(pe):
            pe.wait_ge(loads, 16 * count)
            pe.wait_ge(w_ready, 1)
            for j in range(NT):
                ins = nc.tensor.matmul(bank[:, experts * j:experts * j + experts], g.xT[:, TP * j:TP * j + TP], wg[:],
                                       start=True, stop=True)
            ins.then_inc(logits_ready, 1)

        @block.scalar
        def _(act):
            act.wait_ge(diff_ready, 1)
            nc.scalar.activation(diff[:], diff[:], ACT.Exp).then_inc(exp_ready, 1)

        @block.vector
        def _(dve):
            dve.wait_ge(loads, 16 * count)
            if more is not None:
                nc.vector.tensor_tensor(wg[C:C + 1, :], wg[C:C + 1, :], more[C:C + 1, :], ALU.add).then_inc(w_ready, 1)
            else:
                dve.sem_inc(w_ready, 1)
            dve.wait_ge(logits_ready, 1)
            st.then(nc.vector.tensor_copy(logits[:].rearrange("p j e -> p (j e)"), bank[:, 0:NT * experts]))
            dve_part()


def split_tokens(g, eng, n, x12, x13, x_rest, led, left, split, first=False, held=None):
    lo, hi, cols = slice(0, C), slice(C, P), bass.ds(GC * n, GC)
    x = g.xT[lo, cols]
    eng.tensor_copy(x12[lo, cols], x).then_inc(led, 1)
    eng.wait_ge(led, n + 1)
    if not first:
        eng.wait_ge(split, 3 * n)
    if held:
        eng.sem_inc(held, 1)
    eng.tensor_tensor(x_rest[hi, :], x, x12[lo, cols], ALU.subtract).then_inc(left, 1)
    eng.tensor_tensor(x12[hi, cols], x, x12[lo, cols], ALU.subtract).then_inc(split, 1)
    eng.tensor_copy(x13[lo, cols], x12[lo, cols]).then_inc(split, 1)
    eng.wait_ge(left, n + 1)
    eng.wait_ge(split, 3 * n + 2)
    if held:
        eng.sem_inc(held, 1)
    eng.tensor_tensor(x13[hi, cols], x_rest[hi, :], x12[hi, cols], ALU.subtract).then_inc(split, 1)


def split_bias(nc, pool, st, pick, bias, rest, mid, parts, ready):
    st.then(nc.gpsimd.memset(pick[:], 0.0))
    for row in (0, 32, 64):
        st.then(nc.gpsimd.memset(pick[row:row + 1, :], 1.0))
    st.then(nc.gpsimd.tensor_copy(parts[:], bias[:]))
    st.then(nc.gpsimd.tensor_tensor(rest[:], bias[:], parts[:], ALU.subtract))
    st.then(nc.gpsimd.tensor_copy(mid[:], rest[:]))
    st.then(nc.gpsimd.tensor_copy(parts[32:64, :], mid[32:64, :]))
    nc.gpsimd.tensor_tensor(parts[64:96, :], rest[64:96, :], mid[64:96, :], ALU.subtract).then_inc(ready, 1)


def run_experts(nc, g, name, gate, w1, b1, w2, b2, experts, chunks, func):
    K = experts * chunks
    W = experts * C
    with Stage(nc, name) as s:
        pick, b2_parts, b2_mid = (s.sb(n, [96, w], BF16) for n, w in (("pick", TP), ("b2_parts", W), ("b2_mid", W)))
        b2_rest = s.sb("b2_rest", [96, W])
        w11, w22, w31 = (s.sb(n, [P, K * P], BF16) for n in ("w11", "w22", "w31"))
        w_rest, x_rest = s.sb("w_rest", [C, K * P]), s.sb("x_rest", [P, GC])
        x12, x13 = s.sb("x12", [P, N], BF16), s.sb("x13", [P, N], BF16)
        hidden = s.sb("hidden", [P, 4, GC])
        gated, summed = s.sb("gated", [TP, GT, experts, C]), s.sb("summed", [TP, GT, C])
        up = s.ps("up", [P, 4, BANK])
        down = s.ps("down", [TP, GT, BANK])
        ready, raised, squashed = (s.sem(n) for n in ("ready", "raised", "squashed"))
        used, taken, reduced, added = (s.sem(n) for n in ("used", "taken", "reduced", "added"))
        steps_w, led, left, split = (s.sem(n) for n in ("steps_w", "led", "left", "split"))
        b2_steps, b2_ready, w_led = s.sem("b2_steps"), s.sem("b2_ready"), s.sem("w_led")
        lo, hi = slice(0, C), slice(C, P)
        block = s.block()

        @block.gpsimd
        def _(pool):
            split_bias(nc, pool, Steps(pool, b2_steps), pick, b2, b2_rest, b2_mid, b2_parts, b2_ready)

        @block.tensor
        def _(pe):
            pe.wait_ge(b2_ready, 1)
            pe.wait_ge(ready, 1)
            with pe.Fori(0, NG) as n:
                pe.wait_ge(split, 3 * n + 3)
                for k in range(K + 1):
                    if k < K:
                        if k >= 4:
                            pe.wait_ge(squashed, K * n + k - 3)
                        for i, (w, x) in enumerate(((w11, x12), (w22, x12), (w31, x13))):
                            ins = nc.tensor.matmul(up[:, k % 4, 0:GC], w[:, P * k:P * k + P], x[:, bass.ds(GC * n, GC)],
                                                   start=(i == 0), stop=(i == 2))
                        ins.then_inc(raised, 1)
                    if k == 1:
                        for t in range(GT):
                            pe.wait_ge(taken, GT * n + t + 1)
                            nc.tensor.matmul(down[:, t, 0:W], pick[:], b2_parts[:], start=True, stop=False,
                                             skip_group_check=True)
                    if k:
                        c = k - 1
                        e = c // chunks
                        pe.wait_ge(squashed, K * n + c + 1)
                        for t in range(GT):
                            ins = nc.tensor.matmul(down[:, t, C * e:C * e + C], hidden[:, c % 4, TP * t:TP * t + TP],
                                                   w2[:, c, :], start=False, stop=(c == K - 1), skip_group_check=True)
                        ins.then_inc(used, 1)

        @block.scalar
        def _(act):
            nc.scalar.copy(w11[:], w1[:]).then_inc(w_led, 1)
            nc.scalar.copy(w31[hi, :], w1[hi, :]).then_inc(w_led, 1)
            with act.Fori(0, NG) as n:
                for k in range(K):
                    act.wait_ge(raised, K * n + k + 1)
                    if k >= 4:
                        act.wait_ge(used, K * n + k - 3)
                    nc.scalar.activation(hidden[:, k % 4], up[:, k % 4, 0:GC], func,
                                         bias=b1[:, k:k + 1]).then_inc(squashed, 1)

        @block.vector
        def _(dve):
            dve.sem_inc(taken, GT)
            split_tokens(g, nc.vector, 0, x12, x13, x_rest, led, left, split, first=True)
            st = Steps(dve, steps_w)
            dve.wait_ge(w_led, 2)
            st.done(nc.vector.tensor_tensor(w_rest[:], w1[lo, :], w11[lo, :], ALU.subtract))
            st.then(nc.vector.tensor_tensor(w22[:], w1[:], w11[:], ALU.subtract))
            nc.vector.tensor_tensor(w31[lo, :], w_rest[:], w22[lo, :], ALU.subtract).then_inc(ready, 1)

            def add_group(n):
                dve.wait_ge(used, K * n + K)
                for t in range(GT):
                    nc.vector.tensor_tensor(gated[:, t], down[:, t, 0:W].rearrange("p (e c) -> p e c", c=C),
                                            bc(gate[:, bass.ds(GT * n + t, 1), :].rearrange("p t e -> p (t e)")
                                               .unsqueeze(2), [TP, experts, C]), ALU.mult).then_inc(taken, 1)
                dve.wait_ge(taken, GT * n + 2 * GT)
                nc.vector.tensor_reduce(summed[:], gated[:].rearrange("p t e c -> p t c e"), AX.X,
                                        ALU.add).then_inc(reduced, 1)
                dve.wait_ge(reduced, n + 1)
                part = g.h[:, bass.ds(GT * n, GT), :]
                nc.vector.tensor_tensor(part, part, summed[:], ALU.add).then_inc(added, 1)
                dve.wait_ge(added, n + 1)

            with dve.Fori(0, NG - 1) as n:
                split_tokens(g, nc.vector, n + 1, x12, x13, x_rest, led, left, split)
                add_group(n)
            add_group(NG - 1)




def mamba(nc, g, A):
    DI, DS, DR, DC = 128, 16, 16, 4
    PAD = DC - 1
    HB = B // 2
    HN = HB * T
    QC = 2 * T
    with Stage(nc, "ma") as s:
        w_in, w_out = s.sb("w_in", [C, 2 * DI]), s.sb("w_out", [DI, C])
        w_dt, w_bc = s.sb("w_dt", [DI, 2, DR]), s.sb("w_bc", [DI, 2, 6 * DS])
        w_delta = s.sb("w_delta", [DR, 2, DI])
        conv_w, conv_b = s.sb("conv_w", [DI, 2, DC]), s.sb("conv_b", [DI, 2])
        delta_b, skip, a_log = s.sb("delta_b", [DI, 2]), s.sb("skip", [DI, 2]), s.sb("a_log", [DI, 2, DS])
        loads = s.sem("loads")
        LOADS = 16 * (2 + 2 * 10)

        def fetch(sp):
            names = ("", "_b")
            sp.dma_start(w_in[:], A["L0_attn_in_proj_w"]).then_inc(loads, 16)
            sp.dma_start(w_out[:], A["L0_attn_out_proj_w"]).then_inc(loads, 16)
            for d, n in enumerate(names):
                sp.dma_start(w_dt[:, d], A["L0_attn_x_proj_w" + n][:, 0:DR]).then_inc(loads, 16)
                for q in range(3):
                    sp.dma_start(w_bc[:, d, 2 * DS * q:2 * DS * q + 2 * DS],
                                 A["L0_attn_x_proj_w" + n][:, DR:DR + 2 * DS]).then_inc(loads, 16)
                sp.dma_start(w_delta[:, d], A["L0_attn_dt_proj_w" + n]).then_inc(loads, 16)
                sp.dma_start(conv_w[:, d], A["L0_attn_conv_w" + n]).then_inc(loads, 16)
                sp.dma_start(conv_b[:, d:d + 1], A["L0_attn_conv_b" + n].unsqueeze(1)).then_inc(loads, 16)
                sp.dma_start(delta_b[:, d:d + 1], A["L0_attn_dt_proj_b" + n].unsqueeze(1)).then_inc(loads, 16)
                sp.dma_start(skip[:, d:d + 1], A["L0_attn_D" + n].unsqueeze(1)).then_inc(loads, 16)
                sp.dma_start(a_log[:, d], A["L0_attn_A" + n + "_log"]).then_inc(loads, 16)

        normalise(nc, g, "man", fetch=fetch)
        pick = s.sb("pick", [96, 2 * DS, P], BF16)
        xpad = s.sb("xpad", [DI, B, T + 2 * PAD])
        gate, y = s.sb("gate", [DI, B, T]), s.sb("y", [DI, B, T])
        u, delta, du = s.sb("u", [DI, B, T]), s.sb("delta", [DI, B, T]), s.sb("du", [DI, B, T])
        dt = s.sb("dt", [DR, N])
        acc = s.sb("acc", [DI, B, T])
        bc_parts = s.sb("bc_parts", [96, N], BF16)
        low = s.sb("low", [96, HN], BF16)
        decay, state = s.sb("decay", [DI, 2, HB, T]), s.sb("state", [DI, 2, HB, T])
        small = state[:].rearrange("p k b t -> p (k b) t")
        lost = decay[:].rearrange("p k b t -> p (k b) t")
        rest = decay[0:96, 0].rearrange("p b t -> p (b t)")
        banks = s.ps("banks", [P, 8, BANK])
        cleared, picked = s.sem("cleared"), s.sem("picked")
        projected, evacuated, relued, split = s.sem("projected"), s.sem("evacuated"), s.sem("relued"), s.sem("split")
        convolved, u_ready, ln_ready, steps_v = s.sem("convolved"), s.sem("u_ready"), s.sem("ln_ready"), s.sem("steps_v")
        steps_a = s.sem("steps_a")
        b_ready, c_ready, decay_ready, driven = s.sem("b_ready"), s.sem("c_ready"), s.sem("decay_ready"), s.sem("driven")
        scanned, weighted, added, y_ready = s.sem("scanned"), s.sem("weighted"), s.sem("added"), s.sem("y_ready")
        out_ready, du_ready, acc_ready = s.sem("out_ready"), s.sem("du_ready"), s.sem("acc_ready")
        acc_used = s.sem("acc_used")
        restarted, e_ready = s.sem("restarted"), s.sem("e_ready")
        block = s.block()

        @block.tensor
        def _(pe):
            pe.wait_ge(loads, LOADS)
            for m in range(2):
                for c in range(8):
                    if m:
                        pe.wait_ge(evacuated, c + 1)
                    nc.tensor.matmul(banks[:, c, 0:QC], w_in[:, DI * m:DI * m + DI], g.xT[0:C, QC * c:QC * c + QC],
                                     start=True, stop=True).then_inc(projected, 1)
            pe.wait_ge(picked, 4)
            for d in range(2):
                done = 16 + 24 * d
                pe.wait_ge(u_ready, d + 1)
                if d:
                    pe.wait_ge(weighted, 1 + 32 * d)
                for c in range(8):
                    pe.wait_ge(evacuated, done if c == 0 else done - 8 + c + 1)
                    nc.tensor.matmul(banks[0:DR, c, 0:QC], w_dt[:, d], u[:, 2 * c:2 * c + 2, :],
                                     start=True, stop=True).then_inc(projected, 1)
                for c in range(8):
                    pe.wait_ge(evacuated, done + c + 1)
                    nc.tensor.matmul(banks[:, c, 0:QC], w_delta[:, d], dt[:, QC * c:QC * c + QC],
                                     start=True, stop=True).then_inc(projected, 1)
                for c in range(8):
                    pe.wait_ge(evacuated, done + 8 + c + 1)
                    nc.tensor.matmul(banks[0:96, c, 0:QC], w_bc[:, d], u[:, 2 * c:2 * c + 2, :],
                                     start=True, stop=True).then_inc(projected, 1)
                pe.wait_ge(split, 2 * d + 2)
                for half in range(2):
                    with pe.Fori(0, DS) as n:
                        k = (2 * d + half) * DS + n
                        for row, free, ready in ((0, driven, b_ready), (DS, weighted, c_ready)):
                            pe.wait_ge(free, k + 1)
                            for c in range(4):
                                ins = nc.tensor.matmul(banks[:, (4 if row else 0) + c, 0:QC], pick[:, row + n, :],
                                                       bc_parts[:, HN * half + QC * c:HN * half + QC * c + QC],
                                                       start=True, stop=True)
                            ins.then_inc(ready, 1)
            for j in range(NT):
                if j % 8 == 0:
                    pe.wait_ge(y_ready, j // 8 + 1)
                ins = nc.tensor.matmul(banks[0:TP, j // 8, C * (j % 8):C * (j % 8) + C],
                                       y[:, j // 2, TP * (j % 2):TP * (j % 2) + TP], w_out[:], start=True, stop=True)
                if j % 8 == 7:
                    ins.then_inc(out_ready, 1)

        @block.scalar
        def _(act):
            st = Steps(act, steps_a)
            act.wait_ge(loads, LOADS)
            st.done(nc.scalar.activation(a_log[:], a_log[:], ACT.Exp))
            act.wait_ge(cleared, 2)
            for c in range(8):
                act.wait_ge(projected, c + 1)
                nc.scalar.copy(xpad[:, 2 * c:2 * c + 2, PAD:PAD + T],
                               banks[:, c, 0:QC].rearrange("p (b t) -> p b t", b=2)).then_inc(evacuated, 1)
            for c in range(8):
                act.wait_ge(projected, 8 + c + 1)
                nc.scalar.activation(gate[:, 2 * c:2 * c + 2, :].rearrange("p b t -> p (b t)"), banks[:, c, 0:QC],
                                     ACT.Silu).then_inc(evacuated, 1)
            act.wait_ge(steps_a, 1)
            st.then(nc.scalar.mul(a_log[:], a_log[:], -1.0))
            for d in range(2):
                done = 16 + 24 * d
                act.wait_ge(convolved, d + 1)
                nc.scalar.activation(u[:], u[:], ACT.Silu, bias=conv_b[:, d:d + 1]).then_inc(u_ready, 1)
                for c in range(8):
                    act.wait_ge(projected, done + c + 1)
                    nc.scalar.copy(dt[:, QC * c:QC * c + QC], banks[0:DR, c, 0:QC]).then_inc(evacuated, 1)
                flat = delta[:].rearrange("p b t -> p (b t)")
                for c in range(8):
                    act.wait_ge(projected, done + 8 + c + 1)
                    nc.scalar.activation(flat[:, QC * c:QC * c + QC], banks[:, c, 0:QC], ACT.Identity,
                                         bias=delta_b[:, d:d + 1]).then_inc(evacuated, 1)
                for c in range(8):
                    act.wait_ge(projected, done + 16 + c + 1)
                    nc.scalar.copy(bc_parts[:, QC * c:QC * c + QC], banks[0:96, c, 0:QC]).then_inc(evacuated, 1)
                act.wait_ge(relued, d + 1)
                st.then(nc.scalar.activation(delta[:], delta[:], ACT.Abs))
                nc.scalar.activation(small, delta[:], ACT.Exp, scale=-1.0).then_inc(e_ready, 1)
                act.wait_ge(e_ready, d + 1)
                nc.scalar.activation(delta[:], small, ACT.Ln, bias=1.0).then_inc(ln_ready, 1)
                act.wait_ge(du_ready, d + 1)
                for half in range(2):
                    with act.Fori(0, DS // 2) as n2:
                        for b in range(2):
                            k = (2 * d + half) * DS + 2 * n2 + b
                            act.wait_ge(scanned, k + 1)
                            nc.scalar.activation(decay[:, b], delta[:, HB * half:HB * half + HB, :], ACT.Exp,
                                                 scale=a_log[:, d, bass.ds(2 * n2 + b, 1)]).then_inc(decay_ready, 1)

        @block.gpsimd
        def _(pool):
            nc.gpsimd.memset(pick[:], 0.0).then_inc(picked, 1)
            for q in range(3):
                pool.wait_ge(picked, q + 1)
                nc.gpsimd.affine_select(out=pick[:], in_=pick[:], compare_op=ALU.not_equal, fill=1.0,
                                        base=-2 * DS * q, pattern=[[-1, 2 * DS], [0, P]],
                                        channel_multiplier=1).then_inc(picked, 1)
            for d in range(2):
                if d:
                    pool.wait_ge(acc_used, 1)
                nc.gpsimd.memset(acc[:], 0.0).then_inc(acc_ready, 1)
                pool.wait_ge(acc_ready, d + 1)
                for half in range(2):
                    part = acc[:, HB * half:HB * half + HB, :]
                    with pool.Fori(0, DS // 2) as n2:
                        for b in range(2):
                            k = (2 * d + half) * DS + 2 * n2 + b
                            pool.wait_ge(weighted, k + 2)
                            pool.wait_ge(added, k + 2)
                            nc.gpsimd.tensor_tensor(part, part, state[:, b], ALU.add).then_inc(added, 1)

        @block.vector
        def _(dve):
            st = Steps(dve, steps_v)
            dve.sem_inc(driven, 1)
            dve.sem_inc(weighted, 1)
            dve.sem_inc(scanned, 2)
            dve.sem_inc(added, 2)
            nc.vector.memset(xpad[:, :, 0:PAD], 0.0).then_inc(cleared, 1)
            nc.vector.memset(xpad[:, :, PAD + T:], 0.0).then_inc(cleared, 1)
            for d in range(2):
                done = 16 + 24 * d
                dve.wait_ge(evacuated, 16)
                for i in range(DC):
                    x_i = xpad[:, :, i:i + T] if d == 0 else xpad[:, :, 2 * PAD - i:2 * PAD - i + T][:, :, ::-1]
                    w_i = conv_w[:, d, i:i + 1]
                    if i == 0:
                        st.then(nc.vector.tensor_scalar(u[:], x_i, w_i, None, ALU.mult))
                    elif i < DC - 1:
                        st.then(nc.vector.scalar_tensor_tensor(out=u[:], in0=x_i, scalar=w_i, in1=u[:],
                                                               op0=ALU.mult, op1=ALU.add))
                    else:
                        nc.vector.scalar_tensor_tensor(out=u[:], in0=x_i, scalar=w_i, in1=u[:], op0=ALU.mult,
                                                       op1=ALU.add).then_inc(convolved, 1)
                if d:
                    dve.wait_ge(added, 32 * d + 2)
                    nc.vector.tensor_tensor(y[:], y[:], acc[:], ALU.add).then_inc(acc_used, 1)
                    dve.wait_ge(acc_used, 1)
                dve.wait_ge(evacuated, done + 16)
                nc.vector.tensor_scalar(du[:], delta[:], 0.0, None, ALU.max).then_inc(relued, 1)
                for half in range(2):
                    dve.wait_ge(evacuated, done + 16 + 4 * half + 4)
                    cols = slice(HN * half, HN * half + HN)
                    if half or d:
                        dve.wait_ge(split, 2 * d + half)
                    rest4 = rest.rearrange("p (c n) -> p c n", c=4)
                    mine = bc_parts[:, cols].rearrange("p (c n) -> p c n", c=4)
                    st.then(nc.vector.tensor_tensor(rest4, banks[0:96, 4 * half:4 * half + 4, 0:QC], mine, ALU.subtract))
                    st.done(nc.vector.tensor_copy(bc_parts[32:64, cols], rest[32:64, :]))
                    st.then(nc.vector.tensor_copy(low[64:96, :], rest[64:96, :]))
                    nc.vector.tensor_tensor(bc_parts[64:96, cols], rest[64:96, :], low[64:96, :],
                                            ALU.subtract).then_inc(split, 1)
                dve.wait_ge(e_ready, d + 1)
                dve.wait_ge(split, 2 * d + 2)
                st.then(nc.vector.tensor_scalar(lost, small, 1.0, -1.0, ALU.add, ALU.add))
                st.then(nc.vector.tensor_tensor(lost, small, lost, ALU.subtract))
                dve.wait_ge(relued, d + 1)
                st.then(nc.vector.tensor_tensor(du[:], du[:], lost, ALU.add))
                dve.wait_ge(ln_ready, d + 1)
                st.then(nc.vector.tensor_tensor(delta[:], delta[:], du[:], ALU.add))
                nc.vector.tensor_tensor(du[:], delta[:], u[:], ALU.mult).then_inc(du_ready, 1)
                dve.wait_ge(du_ready, d + 1)
                for half in range(2):
                    part = du[:, HB * half:HB * half + HB, :].rearrange("p (c b) t -> p c (b t)", b=2)
                    with dve.Fori(0, DS // 2) as n2:
                        for b in range(2):
                            k = (2 * d + half) * DS + 2 * n2 + b
                            now = state[:, b].rearrange("p b t -> p (b t)")
                            now4 = state[:, b].rearrange("p (c b) t -> p c (b t)", b=2)
                            past = decay[:, b].rearrange("p b t -> p (b t)")
                            dve.wait_ge(b_ready, k + 1)
                            dve.wait_ge(added, k + 1)
                            nc.vector.tensor_tensor(now4, banks[:, 0:4, 0:QC], part, ALU.mult).then_inc(driven, 1)
                            dve.wait_ge(decay_ready, k + 1)
                            nc.vector.memset(decay[:, b, :, 0:1], 0.0).then_inc(restarted, 1)
                            dve.wait_ge(driven, k + 2)
                            dve.wait_ge(restarted, k + 1)
                            nc.vector.tensor_tensor_scan(now, past, now, 0.0, ALU.mult, ALU.add).then_inc(scanned, 1)
                            dve.wait_ge(scanned, k + 3)
                            dve.wait_ge(c_ready, k + 1)
                            nc.vector.tensor_tensor(now4, banks[:, 4:8, 0:QC], now4, ALU.mult).then_inc(weighted, 1)
                if d == 0:
                    st.then(nc.vector.tensor_scalar(y[:], u[:], skip[:, 0:1], None, ALU.mult))
                else:
                    dve.wait_ge(added, 32 * (d + 1) + 2)
                    for q in range(4):
                        part = slice(B // 4 * q, B // 4 * q + B // 4)
                        st.then(nc.vector.scalar_tensor_tensor(out=acc[:, part], in0=u[:, part], scalar=skip[:, 1:2],
                                                               in1=acc[:, part], op0=ALU.mult, op1=ALU.add))
                        st.then(nc.vector.tensor_tensor(y[:, part], y[:, part], acc[:, part, ::-1], ALU.add))
                        nc.vector.tensor_tensor(y[:, part], y[:, part], gate[:, part], ALU.mult).then_inc(y_ready, 1)
            for q in range(4):
                dve.wait_ge(out_ready, q + 1)
                part = g.h[:, 8 * q:8 * q + 8, :]
                nc.vector.tensor_tensor(part, part, banks[0:TP, q, :].rearrange("p (j c) -> p j c", j=8), ALU.add)


PARTS = 8


def graph_experts(nc, g, A):
    E, HEADS, TOPS = 4, 4, 16
    EDGES = 262144
    COLS = EDGES // P
    F = HEADS * E
    V = F + HEADS
    G = 8
    HIGH = 60.0
    ROUND = 12582912.0
    with Stage(nc, "ge") as s:
        w1, b1, w2 = s.sb("w1", [P, E * P]), s.sb("b1", [P, E]), s.sb("w2", [P, E, C])
        b2, gate = s.sb("b2", [96, E * C]), s.sb("gate", [TP, NT, E])
        nodes, own = s.sb("nodes", [TP, NT, F + 2 * HEADS]), s.sb("own", [TP, NT, V])
        keys = s.sb("keys", [P, COLS])
        last = s.sb("last", [TP, V])
        dst_rows = s.sb("dst_rows", [P, NT, 2 * HEADS])
        turns = s.sb("turns", [P, 2], I32)
        last_keys = s.sb("last_keys", [P, COLS])
        with Stage(nc, "gt") as t:
            wg, fold = t.sb("wg", [C, F]), t.sb("fold", [F, F + 2 * HEADS])
            src_i, dst_i = t.sb("src_i", [P, COLS], I32), t.sb("dst_i", [P, COLS], I32)
            loads, edges = t.sem("loads"), t.sem("edges")

            def fetch(sp):
                sp.dma_start(wg[:], A["L0_ffn_W_gat"]).then_inc(loads, 16)
                sp.dma_start(fold[:], A["fold"]).then_inc(loads, 16)
                for n, dst in ((1, dst_i), (0, src_i)):
                    sp.dma_start(dst[:], A["L0_ffn_edge_index"][n].rearrange("(p n) -> p n", p=P)).then_inc(edges, 16)
                for dst, name in ((w1[0:C, :], "W1"), (w1[C:P, :], "W1"), (b1[:], "b1"), (w2[:], "W2")):
                    sp.dma_start(dst, A["L0_ffn_" + name]).then_inc(loads, 16)
                sp.dma_start(b2[:], A["L0_ffn_b2"].to_broadcast([96, E * C])).then_inc(loads, 16)

            normalise(nc, g, "gn", fetch=fetch)
            make_tables(nc, g, t, wg, fold, src_i, dst_i, loads, edges, nodes, own, keys, turns, last, dst_rows,
                        last_keys, E, HEADS, F, V, COLS, HIGH, ROUND)
        with Stage(nc, "gc") as t:
            count_last(nc, t, nodes, own, last, dst_rows, last_keys, turns, E, HEADS, F, V, COLS)
        with Stage(nc, "gw") as t:
            walk_edges(nc, g, A, t, own, keys, turns, gate, E, HEADS, F, V, G)
        run_experts(nc, g, "gx", gate, w1, b1, w2, b2, E, 1, ACT.Gelu)


def make_tables(nc, g, s, wg, fold, src_i, dst_i, loads, edges, nodes, own, keys, turns, last, dst_rows, last_keys, E,
                HEADS, F, V, COLS, HIGH, ROUND):
    hT = s.sb("hT", [F, N])
    leaky = s.sb("leaky", [TP, NT, HEADS])
    bound, top, topmost = s.sb("bound", [TP, NT, HEADS]), s.sb("top", [P, HEADS]), s.sb("topmost", [P, HEADS])
    src, dst, tile, from_last = (s.sb(n, [P, COLS]) for n in ("src", "dst", "tile", "from_last"))
    in_part = s.sb("in_part", [P, PARTS])
    count, most = s.sb("count", [P, 2]), s.sb("most", [P, 2])
    banks = s.ps("banks", [P, 8, BANK])
    projected, hT_ready, folded = (s.sem(n) for n in ("projected", "hT_ready", "folded"))
    nodes_ready, top_ready, reduced, steps_v = (s.sem(n) for n in ("nodes_ready", "top_ready", "reduced", "steps_v"))
    own_in, own_out, rows_ready, stored, steps_p = (s.sem(n) for n in ("own_in", "own_out", "rows_ready", "stored", "steps_p"))
    count_ready = s.sem("count_ready")
    block = s.block()

    @block.sync
    def _(sp):
        sp.wait_ge(rows_ready, 1)
        sp.dma_start(g.src_table.rearrange("(j p) v -> p j v", p=TP), nodes[:, :, 0:V]).then_inc(stored, 16)
        sp.dma_start(g.dst_table.rearrange("(j p) v -> p j v", p=P), dst_rows[:]).then_inc(stored, 16)
        sp.wait_ge(stored, 32)
        sp.dma_start(last[:], g.src_table[N - 1:N, :].to_broadcast([TP, V])).then_inc(stored, 16)
        sp.wait_ge(stored, 48)

    @block.tensor
    def _(pe):
        pe.wait_ge(loads, 16 * 7)
        for c in range(NG):
            nc.tensor.matmul(banks[0:F, c, 0:GC], wg[:], g.xT[0:C, GC * c:GC * c + GC], start=True,
                             stop=True).then_inc(projected, 1)
        pe.wait_ge(hT_ready, NG)
        W = F + 2 * HEADS
        for j in range(NT):
            ins = nc.tensor.matmul(banks[0:TP, j // 16, W * (j % 16):W * (j % 16) + W], hT[:, TP * j:TP * j + TP],
                                   fold[:], start=True, stop=True)
        ins.then_inc(folded, 1)

    @block.scalar
    def _(act):
        for c in range(NG):
            act.wait_ge(projected, c + 1)
            nc.scalar.copy(hT[:, GC * c:GC * c + GC], banks[0:F, c, 0:GC]).then_inc(hT_ready, 1)
        act.wait_ge(folded, 1)
        nc.scalar.copy(nodes[:].rearrange("p (q j) w -> p q (j w)", q=2),
                       banks[0:TP, 0:2, 0:16 * (F + 2 * HEADS)]).then_inc(nodes_ready, 1)
        act.wait_ge(own_in, 1)
        nc.scalar.activation(own[:, :, F:V], own[:, :, F:V], ACT.Exp).then_inc(own_out, 1)

    @block.gpsimd
    def _(pool):
        pool.wait_ge(count_ready, 1)
        nc.gpsimd.partition_all_reduce(most[:], count[:], P, RMAX).then_inc(reduced, 1)
        pool.wait_ge(top_ready, 1)
        pool.wait_ge(reduced, 1)
        nc.gpsimd.partition_all_reduce(topmost[:], top[:], P, RMAX).then_inc(reduced, 1)

    @block.vector
    def _(dve):
        st = Steps(dve, steps_v)
        src_score, dst_score = nodes[:, :, F:V], nodes[:, :, V:V + HEADS]
        st.done(nc.vector.memset(dst_rows[:], 0.0))
        st.then(nc.vector.memset(top[:], -3e38))
        dve.wait_ge(edges, 32)
        st.done(nc.vector.tensor_copy(src[:], src_i[:]))
        st.then(nc.vector.tensor_copy(dst[:], dst_i[:]))
        st.then(nc.vector.tensor_scalar(tile[:], dst[:], float(TP // 2), 1.0 / TP, ALU.subtract, ALU.mult))
        st.then(nc.vector.tensor_scalar(tile[:], tile[:], ROUND, None, ALU.add))
        st.then(nc.vector.tensor_scalar(tile[:], tile[:], ROUND, None, ALU.subtract))
        st.done(nc.vector.scalar_tensor_tensor(out=keys[:], in0=tile[:], scalar=float(P - TP), in1=dst[:], op0=ALU.mult,
                                               op1=ALU.add))
        st.then(nc.vector.tensor_scalar(from_last[:], src[:], float(N - 1), None, ALU.is_ge))
        st.then(nc.vector.tensor_scalar(dst[:], dst[:], float(N), None, ALU.is_lt))
        st.then(nc.vector.tensor_tensor(from_last[:], from_last[:], dst[:], ALU.mult))
        st.then(nc.vector.tensor_tensor(dst[:], dst[:], from_last[:], ALU.subtract))
        st.then(nc.vector.scalar_tensor_tensor(out=last_keys[:], in0=keys[:], scalar=1.0, in1=from_last[:], op0=ALU.add,
                                               op1=ALU.mult))
        st.then(nc.vector.tensor_scalar(last_keys[:], last_keys[:], -1.0, None, ALU.add))
        st.then(nc.vector.tensor_reduce(in_part[:], from_last[:].rearrange("p (a n) -> p a n", a=PARTS), AX.X, ALU.add))
        st.done(nc.vector.tensor_reduce(count[:, 1:2], in_part[:], AX.X, ALU.max))
        st.then(nc.vector.tensor_scalar(src[:], src[:], float(N - 1), 1.0, ALU.min, ALU.add))
        st.then(nc.vector.scalar_tensor_tensor(out=keys[:], in0=keys[:], scalar=4096.0, in1=src[:], op0=ALU.mult, op1=ALU.add))
        st.done(nc.vector.tensor_reduce(count[:, 0:1], dst[:], AX.X, ALU.add))
        st.then(nc.vector.tensor_tensor(keys[:], keys[:], dst[:], ALU.mult))
        st.then(nc.vector.tensor_scalar(keys[:], keys[:], -1.0, None, ALU.add))
        dve.sem_inc(count_ready, 1)
        dve.wait_ge(nodes_ready, 1)
        nc.vector.tensor_reduce(top[0:TP, :], src_score.rearrange("p j h -> p h j"), AX.X, ALU.max).then_inc(top_ready, 1)
        st.done(nc.vector.tensor_copy(dst_rows[0:TP, :, 0:HEADS], dst_score))
        st.then(nc.vector.tensor_tensor(leaky[:], src_score, dst_score, ALU.add))
        st.then(nc.vector.scalar_tensor_tensor(out=leaky[:], in0=leaky[:], scalar=0.2, in1=leaky[:], op0=ALU.mult, op1=ALU.max))
        dve.wait_ge(reduced, 2)
        st.then(nc.vector.tensor_tensor(bound[:], dst_score, bc(topmost[0:TP, :].unsqueeze(1), [TP, NT, HEADS]), ALU.add))
        st.then(nc.vector.scalar_tensor_tensor(out=bound[:], in0=bound[:], scalar=0.2, in1=bound[:], op0=ALU.mult, op1=ALU.max))
        st.then(nc.vector.scalar_tensor_tensor(out=dst_rows[0:TP, :, HEADS:], in0=bound[:], scalar=-HIGH, in1=leaky[:],
                                               op0=ALU.add, op1=ALU.max))
        nc.vector.tensor_tensor(own[:, :, F:V], leaky[:], dst_rows[0:TP, :, HEADS:], ALU.subtract).then_inc(own_in, 1)
        dve.sem_inc(rows_ready, 1)
        dve.wait_ge(own_out, 1)
        w = bc(own[:, :, F:V].unsqueeze(3), [TP, NT, HEADS, E])
        st.done(nc.vector.tensor_tensor(own[:, :, 0:F].rearrange("p j (h e) -> p j h e", h=HEADS),
                                        nodes[:, :, 0:F].rearrange("p j (h e) -> p j h e", h=HEADS), w, ALU.mult))
        for n, shift in enumerate((4, 3)):
            part = turns[:, n:n + 1]
            st.then(nc.vector.tensor_scalar(part, most[:, n:n + 1], 1.0, 2.0 ** shift - 1, ALU.max, ALU.add))
            st.then(nc.vector.tensor_scalar(part, part, shift, None, ALU.arith_shift_right))


def count_last(nc, s, nodes, own, last, dst_rows, last_keys, turns, E, HEADS, F, V, COLS):
    PART = COLS // PARTS
    G = 8 * PARTS
    ramp_i, ramp = s.sb("ramp_i", [P, P], I32), s.sb("ramp", [P, P])
    best, code, part_i = s.sb("best", [P, G]), s.sb("code", [P, G], I32), s.sb("part_i", [P, 2, G], I32)
    place = s.sb("place", [P, 2, G])
    row_hot, tile_hot = s.sb("row_hot", [P, G, TP], BF16), s.sb("tile_hot", [P, G, NT], BF16)
    number, weight, zeros = s.sb("number", [TP, NT]), s.sb("weight", [TP, NT, HEADS]), s.sb("zeros", [1, TP], BF16)
    message = s.sb("message", [TP, NT, F])
    sums = s.ps("sums", [TP, NT])
    ramp_ready, made, used, held = s.sem("ramp_ready"), s.sem("made"), s.sem("used"), s.sem("held")
    steps_v, steps_l, raw_ready, exp_ready = s.sem("steps_v"), s.sem("steps_l"), s.sem("raw_ready"), s.sem("exp_ready")
    block = s.block()

    def turns_of(eng):
        return eng.value_load(turns[0:1, 1:2], min_val=1, max_val=PART // 8)

    @block.gpsimd
    def _(pool):
        nc.gpsimd.iota(ramp_i[:], pattern=[[1, P]], base=0, channel_multiplier=0).then_inc(ramp_ready, 1)

    @block.tensor
    def _(pe):
        pe.wait_ge(ramp_ready, 2)
        nc.tensor.matmul(sums[:], zeros[:], zeros[:, 0:NT], start=True, stop=False, skip_group_check=True)
        with pe.Fori(0, turns_of(pe)) as n:
            for half in range(2):
                pe.wait_ge(made, 4 * n + 2 * half + 2)
                for k in range(G // 2 * half, G // 2 * half + G // 2):
                    ins = nc.tensor.matmul(sums[:], row_hot[:, k, :], tile_hot[:, k, :], start=False, stop=False,
                                           skip_group_check=True)
                ins.then_inc(used, 1)

    @block.scalar
    def _(act):
        act.wait_ge(raw_ready, 1)
        nc.scalar.activation(weight[:], weight[:], ACT.Exp).then_inc(exp_ready, 1)

    @block.vector
    def _(dve):
        st = Steps(dve, steps_v)
        dve.sem_inc(used, 2)
        st.then(nc.vector.memset(zeros[:], 0.0))
        dve.wait_ge(ramp_ready, 1)
        nc.vector.tensor_copy(ramp[:], ramp_i[:]).then_inc(ramp_ready, 1)
        dve.wait_ge(ramp_ready, 2)
        shape = [TP, NT, HEADS]
        st.then(nc.vector.tensor_tensor(weight[:], nodes[:, :, V:V + HEADS], bc(last[:, F:V].unsqueeze(1), shape), ALU.add))
        st.then(nc.vector.scalar_tensor_tensor(out=weight[:], in0=weight[:], scalar=0.2, in1=weight[:], op0=ALU.mult,
                                               op1=ALU.max))
        nc.vector.tensor_tensor(weight[:], weight[:], dst_rows[0:TP, :, HEADS:], ALU.subtract).then_inc(raw_ready, 1)
        count = turns_of(dve)
        STEPS = 2 * PARTS + 5
        with dve.Fori(0, count) as n:
            loop = Steps(dve, steps_l, STEPS * n)
            parts = [(best[:, 8 * a:8 * a + 8], last_keys[:, PART * a:PART * a + PART]) for a in range(PARTS)]
            for top, mine in parts:
                loop.done(nc.vector.max(out=top, in_=mine))
            dve.wait_ge(steps_l, loop.base + loop.n)
            dve.sem_inc(held, 1)
            for top, mine in parts:
                loop.done(nc.vector.match_replace(out=mine, in_to_replace=top, in_values=mine, imm_value=-1.0))
            loop.then(nc.vector.tensor_copy(code[:], best[:]))
            loop.done(nc.vector.tensor_scalar(part_i[:, 0], code[:], P - 1, None, ALU.bitwise_and))
            loop.then(nc.vector.tensor_scalar(part_i[:, 1], code[:], 7, None, ALU.arith_shift_right))
            loop.done(nc.vector.tensor_copy(place[:, 0], part_i[:, 0]))
            loop.then(nc.vector.tensor_copy(place[:, 1], part_i[:, 1]))
            assert loop.n == STEPS
            for half in range(2):
                dve.wait_ge(used, 2 * n + half + 1)
                k = slice(G // 2 * half, G // 2 * half + G // 2)
                for what, out, size in ((0, row_hot, TP), (1, tile_hot, NT)):
                    wide = [P, G // 2, size]
                    nc.vector.tensor_tensor(out[:, k], bc(ramp[:, 0:size].unsqueeze(1), wide),
                                            bc(place[:, what, k].unsqueeze(2), wide), ALU.is_equal).then_inc(made, 1)
            dve.wait_ge(made, 4 * n + 4)
            dve.sem_inc(held, 1)
        dve.wait_ge(used, 2 * count + 2)
        st.done(nc.vector.tensor_copy(number[:], sums[:]))
        dve.wait_ge(exp_ready, 1)
        dve.wait_ge(steps_v, st.n)
        st.then(nc.vector.tensor_tensor(weight[:], weight[:], bc(number[:].unsqueeze(2), shape), ALU.mult))
        st.done(nc.vector.tensor_tensor(own[:, :, F:V], own[:, :, F:V], weight[:], ALU.add))
        st.then(nc.vector.tensor_tensor(message[:].rearrange("p j (h e) -> p j h e", h=HEADS),
                                        bc(last[:, 0:F].rearrange("p (h e) -> p h e", h=HEADS).unsqueeze(1),
                                           shape + [E]), bc(weight[:].unsqueeze(3), shape + [E]), ALU.mult))
        st.then(nc.vector.tensor_tensor(own[:, :, 0:F], own[:, :, 0:F], message[:], ALU.add))


def walk_edges(nc, g, A, s, own, keys, turns, gate, E, HEADS, F, V, G):
    MOST = keys.shape[1] // (2 * G)
    best = s.sb("largest", [P, G])
    code = s.sb("code", [P, G], I32)
    src_at, dst_at = s.sb("src_at", [P, 2, G], I32), s.sb("dst_at", [P, 2, G], I32)
    part_i = s.sb("part_i", [P, 2, G], I32)
    tile, row = s.sb("tile", [P, 2, G]), s.sb("row", [P, 2, G])
    src_rows, dst_rows = s.sb("src_rows", [P, 2, G, V]), s.sb("dst_rows", [P, 2, G, 2 * HEADS])
    score = s.sb("score", [P, G, HEADS])
    value = s.sb("value", [P, G, V])
    row_hot, tile_hot = s.sb("row_hot", [P, 2, G, TP]), s.sb("tile_hot", [P, G, NT])
    spread = s.sb("spread", [P, 2, G, NT, V])
    ramp_i, ramp, zeros = s.sb("ramp_i", [P, P], I32), s.sb("ramp", [P, P]), s.sb("zeros", [1, BANK])
    total = s.sb("total", [TP, NT, V])
    gamma, beta, b_gat = (s.sb(n, [TP, F]) for n in ("gamma", "beta", "b_gat"))
    mean, var, sq = s.sb("mean", [TP, NT]), s.sb("var", [TP, NT]), s.sb("sq", [TP, NT, F])
    scores = s.sb("scores", [TP, NT, E])
    sums = s.ps("sums", [TP, 2, BANK])
    W = NT // 2 * V
    loads, consts, picked, steps_v = (s.sem(n) for n in ("loads", "consts", "picked", "steps_v"))
    gathered = [s.sem(f"gathered{b}") for b in range(2)]
    consumed, score_in, score_out = s.sem("consumed"), s.sem("score_in"), s.sem("score_out")
    spread_ready, summed, root_in, root_out = (s.sem(n) for n in ("spread_ready", "summed", "root_in", "root_out"))
    diff_ready, exp_ready = s.sem("diff_ready"), s.sem("exp_ready")
    steps_end, waited = s.sem("steps_end"), s.sem("waited")
    st_end = Steps(nc.vector, steps_end)
    dve_part, diff = choose_two(nc, s, nc.vector, diff_ready, exp_ready, st_end, scores, gate, E)
    block = s.block()

    def turns_of(eng):
        return eng.value_load(turns[0:1, 0:1], min_val=1, max_val=MOST)

    @block.sync
    def _(sp):
        for dst, name in ((gamma, "ln_gamma"), (beta, "ln_beta"), (b_gat, "b_gat")):
            sp.dma_start(dst[:], A["L0_ffn_" + name].unsqueeze(0).to_broadcast([TP, F])).then_inc(loads, 16)

    @block.gpsimd
    def _(pool):
        nc.gpsimd.iota(ramp_i[:], pattern=[[1, P]], base=0, channel_multiplier=0).then_inc(consts, 1)
        with pool.Fori(0, turns_of(pool)) as i:
            for b in range(2):
                pool.wait_ge(picked, 2 * i + b + 1)
                pool.wait_ge(consumed, 2 * i + b + 1)
                pool.sem_inc(waited, 1)
                for k in range(G):
                    for rows, at, table in ((src_rows, src_at, g.src_table), (dst_rows, dst_at, g.dst_table)):
                        nc.gpsimd.indirect_dma_start(
                            out=rows[:, b, k, :], out_offset=None, in_=table,
                            in_offset=bass.IndirectOffsetOnAxis(ap=at[:, b, k:k + 1], axis=0)).then_inc(gathered[b], 16)

    @block.scalar
    def _(act):
        with act.Fori(0, turns_of(act)) as i:
            for b in range(2):
                act.wait_ge(score_in, 2 * i + b + 1)
                nc.scalar.activation(value[:, :, F:V], score[:], ACT.Exp).then_inc(score_out, 1)
        act.wait_ge(root_in, 1)
        nc.scalar.activation(var[:], var[:], ACT.Sqrt).then_inc(root_out, 1)
        act.wait_ge(diff_ready, 1)
        nc.scalar.activation(diff[:], diff[:], ACT.Exp).then_inc(exp_ready, 1)

    @block.tensor
    def _(pe):
        pe.wait_ge(consts, 3)
        for q in range(2):
            nc.tensor.matmul(sums[:, q, 0:W], zeros[:, 0:TP], zeros[:, 0:W], start=True, stop=False,
                             skip_group_check=True)
        with pe.Fori(0, turns_of(pe)) as i:
            for b in range(2):
                pe.wait_ge(spread_ready, 2 * i + b + 1)
                for k in range(G):
                    for q in range(2):
                        half = spread[:, b, k, NT // 2 * q:NT // 2 * q + NT // 2, :].rearrange("p j v -> p (j v)")
                        ins = nc.tensor.matmul(sums[:, q, 0:W], row_hot[:, b, k, :], half, start=False, stop=False,
                                               skip_group_check=True)
                ins.then_inc(summed, 1)

    @block.vector
    def _(dve):
        st = Steps(dve, steps_v)
        dve.sem_inc(consumed, 2)
        dve.sem_inc(summed, 2)
        dve.wait_ge(consts, 1)
        nc.vector.memset(zeros[:], 0.0).then_inc(consts, 1)
        nc.vector.tensor_copy(ramp[:], ramp_i[:]).then_inc(consts, 1)
        dve.wait_ge(consts, 3)

        def pick(turn, b, st):
            dve.sem_inc(waited, 1)
            st.then(nc.vector.max(out=best[:], in_=keys[:]))
            dve.sem_inc(waited, 1)
            st.done(nc.vector.match_replace(out=keys[:], in_to_replace=best[:], in_values=keys[:], imm_value=-1.0))
            st.then(nc.vector.tensor_copy(code[:], best[:]))
            st.done(nc.vector.tensor_scalar(src_at[:, b], code[:], 4095, None, ALU.bitwise_and))
            st.done(nc.vector.tensor_scalar(dst_at[:, b], code[:], 12, None, ALU.arith_shift_right))
            st.then(nc.vector.tensor_scalar(part_i[:, 0], code[:], 19, None, ALU.arith_shift_right))
            st.done(nc.vector.tensor_copy(tile[:, b], part_i[:, 0]))
            st.then(nc.vector.tensor_scalar(part_i[:, 1], dst_at[:, b], P - 1, None, ALU.bitwise_and))
            st.done(nc.vector.tensor_copy(row[:, b], part_i[:, 1]))
            st.done(nc.vector.tensor_scalar(src_at[:, b], src_at[:, b], float(N - 1), None, ALU.min))
            st.then(nc.vector.tensor_scalar(dst_at[:, b], dst_at[:, b], 0.0, None, ALU.max))
            dve.sem_inc(picked, 1)

        def spread_out(turn, b, st):
            dve.wait_ge(gathered[b], 256 * (turn + 1))
            st.then(nc.vector.tensor_tensor(score[:], src_rows[:, b, :, F:V], dst_rows[:, b, :, 0:HEADS], ALU.add))
            st.then(nc.vector.scalar_tensor_tensor(out=score[:], in0=score[:], scalar=0.2, in1=score[:], op0=ALU.mult,
                                                   op1=ALU.max))
            nc.vector.tensor_tensor(score[:], score[:], dst_rows[:, b, :, HEADS:], ALU.subtract).then_inc(score_in, 1)
            dve.wait_ge(summed, 2 * turn + b + 1)
            st.done(nc.vector.tensor_tensor(row_hot[:, b], bc(ramp[:, 0:TP].unsqueeze(1), [P, G, TP]),
                                            bc(row[:, b].unsqueeze(2), [P, G, TP]), ALU.is_equal))
            st.done(nc.vector.tensor_tensor(tile_hot[:], bc(ramp[:, 0:NT].unsqueeze(1), [P, G, NT]),
                                            bc(tile[:, b].unsqueeze(2), [P, G, NT]), ALU.is_equal))
            dve.wait_ge(score_out, 2 * turn + b + 1)
            w = bc(value[:, :, F:V].unsqueeze(3), [P, G, HEADS, E])
            st.then(nc.vector.tensor_tensor(value[:, :, 0:F].rearrange("p k (h e) -> p k h e", h=HEADS),
                                            src_rows[:, b, :, 0:F].rearrange("p k (h e) -> p k h e", h=HEADS), w,
                                            ALU.mult))
            dve.sem_inc(consumed, 1)
            nc.vector.tensor_tensor(spread[:, b], bc(tile_hot[:].unsqueeze(3), [P, G, NT, V]),
                                    bc(value[:].unsqueeze(2), [P, G, NT, V]), ALU.mult).then_inc(spread_ready, 1)
            dve.wait_ge(spread_ready, 2 * turn + b + 1)

        pick(0, 0, st)
        first = st.n
        PICK, SPREAD = 11, 5
        count = turns_of(dve)
        with dve.Fori(0, count) as i:
            st = Steps(dve, steps_v, first + 2 * (PICK + SPREAD) * i)
            for b in range(2):
                pick(i, 1 - b, st)
                spread_out(i, b, st)
            assert st.n == 2 * (PICK + SPREAD)
        st = st_end
        dve.wait_ge(summed, 2 * count + 2)
        for q in range(2):
            part = slice(NT // 2 * q, NT // 2 * q + NT // 2)
            st.done(nc.vector.tensor_tensor(total[:, part], sums[:, q, 0:W].rearrange("p (j v) -> p j v", v=V),
                                            own[:, part], ALU.add))
        dve.wait_ge(steps_end, st.n)
        den = total[:, :, F:V]
        st.then(nc.vector.tensor_scalar(den, den, 1e-16, None, ALU.add))
        st.then(nc.vector.reciprocal(den, den))
        agg = total[:, :, 0:F]
        agg4 = agg.rearrange("p j (h e) -> p j h e", h=HEADS)
        wide = [TP, NT, F]
        st.then(nc.vector.tensor_tensor(agg4, agg4, bc(den.unsqueeze(3), [TP, NT, HEADS, E]), ALU.mult))
        dve.wait_ge(loads, 48)
        st.then(nc.vector.tensor_tensor(agg, agg, bc(b_gat[:].unsqueeze(1), wide), ALU.add))
        st.then(nc.vector.tensor_reduce(mean[:], agg, AX.X, ALU.add))
        st.then(nc.vector.tensor_scalar(mean[:], mean[:], 1.0 / F, None, ALU.mult))
        st.then(nc.vector.tensor_tensor(agg, agg, bc(mean[:].unsqueeze(2), wide), ALU.subtract))
        st.then(nc.vector.tensor_tensor(sq[:], agg, agg, ALU.mult))
        st.then(nc.vector.tensor_reduce(var[:], sq[:], AX.X, ALU.add))
        nc.vector.tensor_scalar(var[:], var[:], 1.0 / F, EPS, ALU.mult, ALU.add).then_inc(root_in, 1)
        dve.wait_ge(root_out, 1)
        st.then(nc.vector.reciprocal(mean[:], var[:]))
        st.then(nc.vector.tensor_tensor(agg, agg, bc(mean[:].unsqueeze(2), wide), ALU.mult))
        st.then(nc.vector.tensor_tensor(agg, agg, bc(gamma[:].unsqueeze(1), wide), ALU.mult))
        st.then(nc.vector.tensor_tensor(agg, agg, bc(beta[:].unsqueeze(1), wide), ALU.add))
        st.then(nc.vector.tensor_reduce(scores[:], agg.rearrange("p j (h e) -> p j e h", h=HEADS), AX.X, ALU.add))
        st.then(nc.vector.tensor_scalar(scores[:], scores[:], 1.0 / HEADS, None, ALU.mult))
        dve_part()


def rwkv(nc, g, A):
    with Stage(nc, "rw") as s:
        mix, rest = s.sb("mix", [C, 3]), s.sb("rest", [C, 3])
        w3, wo = s.sb("w3", [C, 3, C]), s.sb("wo", [C, C])
        windows = s.sb("windows", [TP, 2, 2, TP])
        loads = s.sem("loads")

        def fetch(sp):
            for n, m in enumerate("kvr"):
                sp.dma_start(mix[:, n:n + 1], A["L1_attn_time_mix_" + m].rearrange("a b c -> c (a b)")).then_inc(loads, 16)
                sp.dma_start(w3[:, n], A["L1_attn_W" + m]).then_inc(loads, 16)
            sp.dma_start(wo[:], A["L1_attn_Wo"]).then_inc(loads, 16)
            for far in range(2):
                for n, name in enumerate(("time_curve", "time_steps")):
                    curve = A[name]
                    window = bass.AP(tensor=curve.tensor, offset=curve.shape[0] - 2 * TP - TP * far,
                                     ap=[[1, TP], [1, TP]])
                    sp.dma_start(windows[:, n, far], window).then_inc(loads, 16)

        normalise(nc, g, "rwn", fetch=fetch)
        decay, steps = s.sb("decay", [TP, 2, TP]), s.sb("ones", [TP, 2, TP])
        mixed = s.sb("mixed", [C, 3, B, T])
        k, kv, r, z = (s.sb(n, [TP, NT, C]) for n in ("k", "kv", "r", "z"))
        inv = s.sb("inv", [TP, 4, BANK])
        zT = s.sb("zT", [C, N])
        banks = s.ps("banks", [P, 8, BANK])
        steps_v = s.sem("steps_v")
        mix_ready, projected, k_clipped, k_ready = s.sem("mix_ready"), s.sem("projected"), s.sem("k_clipped"), s.sem("k_ready")
        kv_ready, r_ready, summed, z_ready = s.sem("kv_ready"), s.sem("r_ready"), s.sem("summed"), s.sem("z_ready")
        turned, zT_ready, out_ready = s.sem("turned"), s.sem("zT_ready"), s.sem("out_ready")
        turned_round = s.sem("turned_round")
        block = s.block()
        x = g.xT[0:C, :].rearrange("c (b t) -> c b t", b=B)

        @block.vector
        def _(dve):
            st = Steps(dve, steps_v)
            dve.wait_ge(loads, 16 * 11)
            nc.vector.tensor_copy(decay[:], windows[:, 0, :, ::-1]).then_inc(turned_round, 1)
            nc.vector.tensor_copy(steps[:], windows[:, 1, :, ::-1]).then_inc(turned_round, 1)
            st.then(nc.vector.tensor_scalar(rest[:], mix[:], -1.0, 1.0, ALU.mult, ALU.add))
            for n in range(3):
                st.then(nc.vector.tensor_scalar(mixed[:, n], x, mix[:, n:n + 1], None, ALU.mult))
                nc.vector.scalar_tensor_tensor(out=mixed[:, n, :, 1:T], in0=x[:, :, 0:T - 1], scalar=rest[:, n:n + 1],
                                               in1=mixed[:, n, :, 1:T], op0=ALU.mult, op1=ALU.add).then_inc(mix_ready, 1)
            dve.wait_ge(projected, 4)
            nc.vector.tensor_scalar(k[:], banks[0:TP, 0:4, :].rearrange("p q (j c) -> p (q j) c", c=C), 30.0, -60.0,
                                    ALU.min, ALU.max).then_inc(k_clipped, 1)
            dve.wait_ge(projected, 8)
            dve.wait_ge(k_ready, 1)
            nc.vector.tensor_tensor(kv[:], banks[0:TP, 4:8, :].rearrange("p q (j c) -> p (q j) c", c=C), k[:],
                                    ALU.mult).then_inc(kv_ready, 1)
            dve.wait_ge(summed, 1)
            st.then(nc.vector.reciprocal(inv[:], banks[0:TP, 0:4, :]))
            dve.wait_ge(r_ready, 1)
            dve.wait_ge(summed, 2)
            for half in range(2):
                zh = z[:].rearrange("p (b t) c -> p t b c", t=2)[:, half]
                rh = r[:].rearrange("p (b t) c -> p t b c", t=2)[:, half]
                w = banks[0:TP, 4 + 2 * half:6 + 2 * half, :].rearrange("p q (b c) -> p (q b) c", c=C)
                i = inv[:, 2 * half:2 * half + 2, :].rearrange("p q (b c) -> p (q b) c", c=C)
                st.then(nc.vector.tensor_tensor(zh, w, rh, ALU.mult))
                nc.vector.tensor_tensor(zh, zh, i, ALU.mult).then_inc(z_ready, 1)
            for q in range(4):
                dve.wait_ge(out_ready, q + 1)
                part = g.h[:, 8 * q:8 * q + 8, :]
                nc.vector.tensor_tensor(part, part, banks[0:TP, q, :].rearrange("p (j c) -> p j c", j=8), ALU.add)

        @block.scalar
        def _(act):
            act.wait_ge(k_clipped, 1)
            nc.scalar.activation(k[:], k[:], ACT.Exp).then_inc(k_ready, 1)
            act.wait_ge(projected, 12)
            nc.scalar.activation(r[:], banks[0:TP, 0:4, :].rearrange("p q (j c) -> p (q j) c", c=C),
                                 ACT.Sigmoid).then_inc(r_ready, 1)
            for n in range(NG):
                act.wait_ge(turned, n + 1)
                nc.scalar.copy(zT[:, GC * n:GC * n + GC], banks[0:C, n, 0:GC]).then_inc(zT_ready, 1)

        @block.tensor
        def _(pe):
            pe.wait_ge(loads, 16 * 11)
            for n in range(3):
                pe.wait_ge(mix_ready, n + 1)
                if n == 2:
                    pe.wait_ge(k_clipped, 1)
                for j in range(NT):
                    ins = nc.tensor.matmul(banks[0:TP, 4 * (n % 2) + j // 8, C * (j % 8):C * (j % 8) + C],
                                           mixed[:, n, j // 2, TP * (j % 2):TP * (j % 2) + TP], w3[:, n],
                                           start=True, stop=True)
                    if j % 8 == 7:
                        ins.then_inc(projected, 1)
            pe.wait_ge(turned_round, 2)
            for src, tri, bank, waits in ((k, steps, 0, ((k_ready, 1), (r_ready, 1))), (kv, decay, 4, ((kv_ready, 1),))):
                for sem, value in waits:
                    pe.wait_ge(sem, value)
                halves = src[:].rearrange("p (b t) c -> p t b c", t=2)
                for half in range(2):
                    for q in range(2):
                        out = banks[0:TP, bank + 2 * half + q, :]
                        for u in range(half + 1):
                            ins = nc.tensor.matmul(out, tri[:, half - u], halves[:, u, 8 * q:8 * q + 8, :],
                                                   start=(u == 0), stop=(u == half))
                ins.then_inc(summed, 1)
            pe.wait_ge(z_ready, 2)
            for j in range(NT):
                ins = nc.tensor.transpose(banks[0:C, j // GT, TP * (j % GT):TP * (j % GT) + TP], z[:, j, :],
                                          g.ident[0:TP, 0:TP])
                if j % GT == GT - 1:
                    ins.then_inc(turned, 1)
            pe.wait_ge(zT_ready, NG)
            for j in range(NT):
                ins = nc.tensor.matmul(banks[0:TP, j // 8, C * (j % 8):C * (j % 8) + C], zT[:, TP * j:TP * j + TP],
                                       wo[:], start=True, stop=True)
                if j % 8 == 7:
                    ins.then_inc(out_ready, 1)


def memory_attention(nc, g, A):
    HEADS, D, KEYS, TOP = 8, C, 64, 16
    RUNS = [TOP // (r + 1) for r in range(TOP // 2)]
    CAND = sum(RUNS) + TOP // 2
    NUM_KV = KEYS * KEYS
    SEEN = TP + T
    PAIRS = HEADS // 2
    RING = 4
    BODY_STEPS = 552
    with Stage(nc, "me") as s:
        wpkT, keysT = s.sb("wpkT", [D // 2, 2 * HEADS, C]), s.sb("keysT", [D // 2, 2 * HEADS, KEYS])
        wq, wo = s.sb("wq", [C, HEADS * D]), s.sb("wo", [D, HEADS, C])
        loads = s.sem("loads")

        def fetch(sp):
            for dst, src in ((wpkT[:], A["L1_ffn_Wq_pk"]), (keysT[:], A["L1_ffn_pk_keys"]), (wq[:], A["L1_ffn_Wq"]),
                             (wo[:], A["L1_ffn_Wo"])):
                sp.dma_start(dst, src).then_inc(loads, 16)

        normalise(nc, g, "men", fetch=fetch)
        wsim = s.sb("wsim", [C, 2, HEADS * KEYS])
        ramp_i, ramp = s.sb("ramp_i", [TP, CAND], I32), s.sb("ramp", [TP, CAND])
        mask = s.sb("mask", [TP, SEEN])
        x = s.sb("x", [C, 2, TP])
        best = [s.sb(f"best{p}", [TP, 2, TOP]) for p in range(2)]
        place, left = s.sb("place", [TP, 2, TOP], U32), s.sb("left", [TP, KEYS])
        cand, cand_left = s.sb("cand", [TP, 2, CAND]), s.sb("cand_left", [TP, CAND])
        final, at, atf = s.sb("final", [TP, 2, HEADS, TOP]), s.sb("at", [TP, TOP], U32), s.sb("atf", [TP, TOP])
        hot, rowf = s.sb("hot", [TP, TOP, CAND]), s.sb("rowf", [TP, TOP])
        row = s.sb("row", [TP, 2, HEADS, TOP], I32)
        lowest, weight = s.sb("lowest", [TP, 2, HEADS]), s.sb("weight", [TP, 2, HEADS, TOP])
        total = s.sb("total", [TP, 2, HEADS])
        rows = s.sb("rows", [TP, RING, TOP, 2 * D])
        kv = s.sb("kv", [TP, 2, 2, HEADS, D])
        kT, v, q = s.sb("kT", [P, PAIRS, T]), s.sb("v", [TP, 2, HEADS, D]), s.sb("q", [P, PAIRS, T])
        seen, neg = s.sb("seen", [TP, 2, SEEN]), s.sb("neg", [TP, 2, 2])
        norm = s.sb("norm", [TP, 2, 2])
        pT, oT = s.sb("pT", [TP, 2, SEEN]), s.sb("oT", [D, 2, T])
        sims = s.ps("sims", [P, 2, BANK])
        qbank = s.ps("qbank", [P, 2, BANK])
        score, turned, outT, out = (s.ps(n, [P, BANK]) for n in ("score", "turned", "outT", "out"))

        folded, ramp_ready = s.sem("folded"), s.sem("ramp_ready")
        mask_zero, mask_ready = s.sem("mask_zero"), s.sem("mask_ready")
        x_ready, sims_ready, chosen, exp_ready = (s.sem(n) for n in ("x_ready", "sims_ready", "chosen", "exp_ready"))
        row_ready, waited = s.sem("row_ready"), s.sem("waited")
        gathered = [s.sem(f"gathered{b}") for b in range(RING)]
        weighed, steps_v, steps_l = s.sem("weighed"), s.sem("steps_v"), s.sem("steps_l")
        q_done, q_ready, k_turned, k_ready = (s.sem(n) for n in ("q_done", "q_ready", "k_turned", "k_ready"))
        scored, lowered, raised, inverted = (s.sem(n) for n in ("scored", "lowered", "raised", "inverted"))
        normed, p_turned, p_ready, o_done = (s.sem(n) for n in ("normed", "p_turned", "p_ready", "o_done"))
        o_ready, out_ready, added, waited_v = (s.sem(n) for n in ("o_ready", "out_ready", "added", "waited_v"))
        block = s.block()
        table = A["memory"]

        @block.gpsimd
        def _(pool):
            nc.gpsimd.iota(ramp_i[:], pattern=[[1, CAND]], base=0, channel_multiplier=0).then_inc(ramp_ready, 1)
            pool.wait_ge(mask_zero, 1)
            for n, start in enumerate((0, TP + TP)):
                part = mask[:, start:start + TP]
                nc.gpsimd.affine_select(out=part, in_=part, compare_op=ALU.is_ge, fill=-3e38, base=0,
                                        pattern=[[-1, TP]], channel_multiplier=1).then_inc(mask_ready, 1)
                pool.wait_ge(mask_ready, n + 1)
            with pool.Fori(0, B) as b:
                for e in range(2):
                    for head in range(HEADS):
                        unit = 2 * HEADS * b + HEADS * e + head
                        buf = head % RING
                        pool.wait_ge(row_ready, unit + 1)
                        pool.wait_ge(weighed, unit + 1)
                        pool.sem_inc(waited, 1)
                        for k in range(TOP):
                            nc.gpsimd.indirect_dma_start(
                                out=rows[:, buf, k, :], out_offset=None, in_=table,
                                in_offset=bass.IndirectOffsetOnAxis(ap=row[:, e, head, k:k + 1], axis=0)) \
                                .then_inc(gathered[buf], 16)

        @block.vector
        def _(dve):
            def tile_of(b, e):
                return 2 * b + e

            def choose(j, e, head, st):
                if head == 0:
                    dve.wait_ge(sims_ready, j + 1)
                for p in range(2):
                    mine = sims[0:TP, p, KEYS * head:KEYS * head + KEYS]
                    vals = best[p][:, 0]
                    dve.sem_inc(waited_v, 1)
                    st.then(nc.vector.max(out=vals[:, 0:8], in_=mine))
                    dve.sem_inc(waited_v, 1)
                    st.done(nc.vector.max_index(out=place[:, p, 0:8], in_max=vals[:, 0:8], in_values=mine))
                    st.then(nc.vector.match_replace(out=left[:], in_to_replace=vals[:, 0:8], in_values=mine,
                                                    imm_value=-3e38))
                    dve.sem_inc(waited_v, 1)
                    st.then(nc.vector.max(out=vals[:, 8:16], in_=left[:]))
                    dve.sem_inc(waited_v, 1)
                    st.then(nc.vector.max_index(out=place[:, p, 8:16], in_max=vals[:, 8:16], in_values=left[:]))
                st.done(nc.vector.tensor_scalar(best[0][:, 1], place[:, 0], float(NUM_KV * head), None, ALU.add))
                st.then(nc.vector.tensor_scalar(best[1][:, 1], place[:, 1], float(KEYS), None, ALU.mult))
                start = 0
                for r, n in enumerate(RUNS):
                    st.done(nc.vector.tensor_tensor(cand[:, :, start:start + n], best[1][:, :, 0:n],
                                                    bc(best[0][:, :, r:r + 1], [TP, 2, n]), ALU.add))
                    start += n
                st.then(nc.vector.tensor_tensor(cand[:, :, start:CAND], best[0][:, :, 8:16],
                                                bc(best[1][:, :, 0:1], [TP, 2, 8]), ALU.add))
                top = final[:, e, head]
                dve.sem_inc(waited_v, 1)
                st.then(nc.vector.max(out=top[:, 0:8], in_=cand[:, 0]))
                dve.sem_inc(waited_v, 1)
                st.done(nc.vector.max_index(out=at[:, 0:8], in_max=top[:, 0:8], in_values=cand[:, 0]))
                st.then(nc.vector.match_replace(out=cand_left[:], in_to_replace=top[:, 0:8], in_values=cand[:, 0],
                                                imm_value=-3e38))
                dve.sem_inc(waited_v, 1)
                st.then(nc.vector.max(out=top[:, 8:16], in_=cand_left[:]))
                dve.sem_inc(waited_v, 1)
                st.done(nc.vector.max_index(out=at[:, 8:16], in_max=top[:, 8:16], in_values=cand_left[:]))
                nc.vector.tensor_scalar(lowest[:, e, head:head + 1], top[:, 0:1], -1.0, None,
                                        ALU.mult).then_inc(chosen, 1)
                dve.wait_ge(st.sem, st.base + st.n)
                st.then(nc.vector.tensor_copy(atf[:], at[:]))
                st.then(nc.vector.tensor_tensor(hot[:], bc(ramp[:].unsqueeze(1), [TP, TOP, CAND]),
                                                bc(atf[:].unsqueeze(2), [TP, TOP, CAND]), ALU.is_equal))
                st.then(nc.vector.tensor_tensor(hot[:], hot[:], bc(cand[:, 1].unsqueeze(1), [TP, TOP, CAND]), ALU.mult))
                st.then(nc.vector.tensor_reduce(rowf[:], hot[:], AX.X, ALU.add))
                nc.vector.tensor_copy(row[:, e, head, :], rowf[:]).then_inc(row_ready, 1)

            def weigh(j, e, head, st, first):
                unit = HEADS * j + head
                buf = head % RING
                w = weight[:, e, head]
                dve.wait_ge(exp_ready, unit + 1)
                st.then(nc.vector.reciprocal(total[:, e, head:head + 1], total[:, e, head:head + 1]))
                st.then(nc.vector.tensor_scalar(w, w, total[:, e, head:head + 1], None, ALU.mult))
                dve.wait_ge(gathered[buf], 256 * (HEADS // RING * j + head // RING + 1))
                st.then(nc.vector.tensor_tensor(rows[:, buf], rows[:, buf], bc(w.unsqueeze(2), [TP, TOP, 2 * D]),
                                                ALU.mult))
                if head == 0 and e == 0 and not first:
                    dve.wait_ge(k_ready, 3 * now[0])
                nc.vector.tensor_reduce(kv[:, :, e, head, :], rows[:, buf].rearrange("p k (n d) -> p n d k", n=2),
                                        AX.X, ALU.add).then_inc(weighed, 1)
                dve.wait_ge(weighed, unit + 1 + RING)

            def invert(b, head, st):
                dve.wait_ge(raised, 2 * (HEADS * b + head) + 2)
                nc.vector.reciprocal(norm[:, head % 2], norm[:, head % 2]).then_inc(inverted, 1)

            def lower(b, head, st):
                dve.wait_ge(scored, HEADS * b + head + 1)
                mine = seen[:, head % 2]
                st.then(nc.vector.tensor_tensor(mine, score[0:TP, 0:SEEN], mask[:], ALU.add))
                st.done(nc.vector.tensor_reduce(neg[:, head % 2, 0:1], mine[:, 0:TP], AX.X, ALU.max))
                st.then(nc.vector.tensor_reduce(neg[:, head % 2, 1:2], mine[:, TP:SEEN], AX.X, ALU.max))
                nc.vector.tensor_scalar(neg[:, head % 2], neg[:, head % 2], -1.0, None, ALU.mult).then_inc(lowered, 1)

            def add_out(b):
                dve.wait_ge(out_ready, b + 1)
                part = g.h[:, bass.ds(2 * b, 2), :]
                nc.vector.tensor_tensor(part, part, out[0:TP, 0:2 * C].rearrange("p (j c) -> p j c", j=2),
                                        ALU.add).then_inc(added, 1)

            def body(b, attend=True, more=True, st=None):
                now[0] = b
                for e in range(2):
                    if attend and e == 1:
                        invert(b - 1, HEADS - 1, st)
                    for head in range(HEADS):
                        if e == 0 or more:
                            choose(tile_of(b, e) + 1, 1 - e, head, st)
                        weigh(tile_of(b, e), e, head, st, first=not attend)
                        if attend and e == 0:
                            if head:
                                invert(b - 1, head - 1, st)
                            lower(b - 1, head, st)
                    if attend and e == 1:
                        add_out(b - 1)

            now = [0]
            dve.wait_ge(folded, 1)
            nc.vector.tensor_copy(wsim[:], sims[0:C, :, :]).then_inc(folded, 1)
            nc.vector.memset(mask[:], 0.0).then_inc(mask_zero, 1)
            dve.sem_inc(weighed, RING)
            dve.sem_inc(lowered, 1)
            dve.sem_inc(added, 1)
            dve.wait_ge(ramp_ready, 1)
            st = Steps(dve, steps_v)
            st.then(nc.vector.tensor_copy(ramp[:], ramp_i[:]))
            dve.wait_ge(mask_ready, 2)
            for head in range(HEADS):
                choose(0, 0, head, st)
            body(0, attend=False, st=st)
            with dve.Fori(1, B - 1) as b:
                loop = Steps(dve, steps_l, BODY_STEPS * (b - 1))
                body(b, st=loop)
                assert loop.n == BODY_STEPS, loop.n
            body(B - 1, more=False, st=st)
            for head in range(HEADS):
                if head:
                    invert(B - 1, head - 1, st)
                lower(B - 1, head, st)
            invert(B - 1, HEADS - 1, st)
            add_out(B - 1)

        @block.scalar
        def _(act):
            def stage_x(j, buf):
                nc.scalar.copy(x[:, buf, :], g.xT[0:C, bass.ds(TP * j, TP)]).then_inc(x_ready, 1)

            def weights(j, e, head):
                act.wait_ge(chosen, HEADS * j + head + 1)
                nc.scalar.activation(weight[:, e, head], final[:, e, head], ACT.Exp, bias=lowest[:, e, head:head + 1],
                                     accum_out=total[:, e, head:head + 1]).then_inc(exp_ready, 1)

            def attend(b, head):
                n = HEADS * b + head
                act.wait_ge(lowered, n + 2)
                mine = seen[:, head % 2]
                for i, cols in enumerate((slice(0, TP), slice(TP, SEEN))):
                    nc.scalar.activation(mine[:, cols], mine[:, cols], ACT.Exp, bias=neg[:, head % 2, i:i + 1],
                                         accum_out=norm[:, head % 2, i:i + 1]).then_inc(raised, 1)
                act.wait_ge(inverted, n + 1)
                for i, cols in enumerate((slice(0, TP), slice(TP, SEEN))):
                    nc.scalar.activation(mine[:, cols], mine[:, cols], ACT.Copy,
                                         scale=norm[:, head % 2, i:i + 1]).then_inc(normed, 1)
                act.wait_ge(p_turned, n + 1)
                nc.scalar.copy(pT[:, head % 2], turned[0:TP, 0:SEEN]).then_inc(p_ready, 1)
                act.wait_ge(o_done, n + 1)
                nc.scalar.copy(oT[:, head % 2], outT[0:D, 0:T]).then_inc(o_ready, 1)

            def body(b, attending=True, more=True):
                stage_x(2 * b + 1, 1)
                for head in range(HEADS):
                    weights(2 * b + 1, 1, head)
                    if attending:
                        attend(b - 1, head)
                for bank in range(2):
                    act.wait_ge(q_done, 2 * b + bank + 1)
                    nc.scalar.mul(q[:, 2 * bank:2 * bank + 2].rearrange("p h t -> p (h t)"), qbank[:, bank, 0:2 * T],
                                  D ** -0.5).then_inc(q_ready, 1)
                if more:
                    stage_x(2 * b + 2, 0)
                    for head in range(HEADS):
                        weights(2 * b + 2, 0, head)
                for e, src in enumerate((turned, outT)):
                    act.wait_ge(k_turned, 2 * b + e + 1)
                    nc.scalar.copy(kT[:, :, TP * e:TP * e + TP], src[:, 0:4 * TP].rearrange("p (n t) -> p n t", n=4)) \
                        .then_inc(k_ready, 1)
                nc.scalar.copy(v[:], kv[:, 1]).then_inc(k_ready, 1)

            act.sem_inc(p_ready, 1)
            act.sem_inc(o_ready, 1)
            stage_x(0, 0)
            for head in range(HEADS):
                weights(0, 0, head)
            body(0, attending=False)
            with act.Fori(1, B - 1) as b:
                body(b)
            body(B - 1, more=False)
            for head in range(HEADS):
                attend(B - 1, head)

        @block.tensor
        def _(pe):
            def find(j, buf, first=False):
                pe.wait_ge(x_ready, j + 1)
                if not first:
                    pe.wait_ge(row_ready, HEADS * j)
                for p in range(2):
                    ins = nc.tensor.matmul(sims[0:TP, p, :], x[:, buf, :], wsim[:, p, :], start=True, stop=True)
                ins.then_inc(sims_ready, 1)

            def attend_scores(b, head):
                n = HEADS * b + head
                if head == 0:
                    pe.wait_ge(k_ready, 3 * b + 3)
                    pe.wait_ge(q_ready, 2 * b + 2)
                pe.wait_ge(lowered, n + 1)
                r = slice(D * (head % 2), D * (head % 2) + D)
                nc.tensor.matmul(score[0:TP, 0:TP], q[r, head // 2, 0:TP], kT[r, head // 2, 0:TP], start=True, stop=True)
                nc.tensor.matmul(score[0:TP, TP:SEEN], q[r, head // 2, TP:T], kT[r, head // 2, :], start=True,
                                 stop=True).then_inc(scored, 1)

            def attend_rest(b, head):
                n = HEADS * b + head
                pe.wait_ge(normed, 2 * n + 2)
                pe.wait_ge(p_ready, n + 1)
                probs = seen[:, head % 2]
                for i in range(3):
                    ins = nc.tensor.transpose(turned[0:TP, TP * i:TP * i + TP], probs[:, TP * i:TP * i + TP],
                                              g.ident[0:TP, 0:TP])
                ins.then_inc(p_turned, 1)
                pe.wait_ge(p_ready, n + 2)
                pe.wait_ge(o_ready, n + 1)
                nc.tensor.matmul(outT[0:D, 0:T], v[:, 0, head], pT[:, head % 2, 0:T], start=True, stop=False,
                                 skip_group_check=True)
                nc.tensor.matmul(outT[0:D, TP:T], v[:, 1, head], pT[:, head % 2, T:SEEN], start=False, stop=True,
                                 skip_group_check=True).then_inc(o_done, 1)
                pe.wait_ge(o_ready, n + 2)
                if head == 0:
                    pe.wait_ge(added, b + 1)
                for i in range(2):
                    ins = nc.tensor.matmul(out[0:TP, C * i:C * i + C], oT[:, head % 2, TP * i:TP * i + TP], wo[:, head],
                                           start=(head == 0 and i == 0), stop=(head == HEADS - 1),
                                           skip_group_check=True)
                if head == HEADS - 1:
                    ins.then_inc(out_ready, 1)

            def attend(b):
                for head in range(HEADS):
                    attend_scores(b, head)
                    if head:
                        attend_rest(b, head - 1)
                attend_rest(b, HEADS - 1)

            def body(b, attending=True, more=True):
                find(2 * b + 1, 1)
                if attending:
                    attend(b - 1)
                if attending:
                    pe.wait_ge(q_ready, 2 * b)
                for pair in range(PAIRS):
                    ins = nc.tensor.matmul(qbank[:, pair // 2, T * (pair % 2):T * (pair % 2) + T],
                                           wq[:, P * pair:P * pair + P], x[:].rearrange("c e t -> c (e t)"),
                                           start=True, stop=True)
                    if pair % 2:
                        ins.then_inc(q_done, 1)
                if more:
                    find(2 * b + 2, 0)
                for e, dst in enumerate((turned, outT)):
                    pe.wait_ge(weighed, RING + HEADS * (2 * b + e + 1))
                    for pair in range(PAIRS):
                        ins = nc.tensor.transpose(dst[:, TP * pair:TP * pair + TP],
                                                  kv[:, 0, e, 2 * pair:2 * pair + 2, :].rearrange("p h d -> p (h d)"),
                                                  g.ident[0:TP, 0:TP])
                    ins.then_inc(k_turned, 1)

            pe.wait_ge(loads, 16 * 4)
            for n in range(2 * HEADS):
                ins = nc.tensor.matmul(sims[0:C, n // HEADS, KEYS * (n % HEADS):KEYS * (n % HEADS) + KEYS], wpkT[:, n],
                                       keysT[:, n], start=True, stop=True)
            ins.then_inc(folded, 1)
            pe.wait_ge(folded, 2)
            find(0, 0, first=True)
            body(0, attending=False)
            with pe.Fori(1, B - 1) as b:
                body(b)
            body(B - 1, more=False)
            attend(B - 1)


def rnn(nc, g, A):
    HID, KC, S = 256, 2, 11
    CHUNKS = T // S
    PARTS = 3
    with Stage(nc, "rc") as s:
        wi0, more0 = s.sb("wi0", [C + 1, HID]), s.sb("more0", [C + 1, HID])
        wh0, wi1, wh1 = (s.sb(n, [P, KC, HID]) for n in ("wh0", "wi1", "wh1"))
        bi1, more1 = s.sb("bi1", [96, HID]), s.sb("more1", [96, HID])
        fc, fc_b = s.sb("fc", [P, KC, C]), s.sb("fc_b", [TP, C])
        loads = s.sem("loads")

        def fetch(sp):
            for dst, name in ((wi0[0:C, :], "W_ih_0"), (wi0[C:C + 1, :], "b_ih_0"), (more0[C:C + 1, :], "b_hh_0"),
                              (wh0[:], "W_hh_0"), (wi1[:], "W_ih_1"), (wh1[:], "W_hh_1"), (fc[:], "fc_w")):
                sp.dma_start(dst, A["L2_attn_" + name]).then_inc(loads, 16)
            for dst, name in ((bi1, "b_ih_1"), (more1, "b_hh_1"), (fc_b, "fc_b")):
                sp.dma_start(dst[:], A["L2_attn_" + name].to_broadcast(dst.shape)).then_inc(loads, 16)

        normalise(nc, g, "rcn", fetch=fetch)
        h0 = s.sb("h0", [P, 2, KC, S, B])
        h1 = s.sb("h1", [P, KC, B, T])
        w0, w1 = (s.sb(n, [P, PARTS, KC, HID], BF16) for n in ("w0", "w1"))
        w_rest = s.sb("w_rest", [P, KC, HID])
        pick = s.sb("pick", [96, S * B], BF16)
        bi1_rest = s.sb("bi1_rest", [96, HID])
        bi1_mid, bi1_parts = s.sb("bi1_mid", [96, HID], BF16), s.sb("bi1_parts", [96, HID], BF16)
        a0, a1 = (s.sb(n, [P, 2, PARTS, KC, B], BF16) for n in ("a0", "a1"))
        rest0, rest1 = s.sb("rest0", [P, KC, B]), s.sb("rest1", [P, KC, B])
        sum0, sum1 = s.ps("sum0", [P, 2, BANK]), s.ps("sum1", [P, 2, BANK])
        final = s.ps("final", [TP, 4, BANK])
        ready = s.sem("ready")
        summed0, summed1, tanh0, tanh1, out_ready = (s.sem(n) for n in ("summed0", "summed1", "tanh0", "tanh1", "out_ready"))
        lead0, lead1, left0, left1 = (s.sem(n) for n in ("lead0", "lead1", "left0", "left1"))
        biased, steps_p, bias_ready = s.sem("biased"), s.sem("steps_p"), s.sem("bias_ready")
        split0, split1, steps_w = s.sem("split0"), s.sem("split1"), s.sem("steps_w")
        block = s.block()
        x = g.xT[:].rearrange("c (b t) -> c t b", b=B)

        @block.vector
        def _(dve):
            dve.wait_ge(loads, 16 * 10)
            nc.vector.tensor_tensor(wi0[C:C + 1, :], wi0[C:C + 1, :], more0[C:C + 1, :], ALU.add).then_inc(ready, 1)
            st = Steps(dve, steps_w)
            for w, parts in ((wh0, w0), (wh1, w1)):
                st.then(nc.vector.tensor_copy(parts[:, 0], w[:]))
                st.then(nc.vector.tensor_tensor(w_rest[:], w[:], parts[:, 0], ALU.subtract))
                st.then(nc.vector.tensor_copy(parts[:, 1], w_rest[:]))
                nc.vector.tensor_tensor(parts[:, 2], w_rest[:], parts[:, 1], ALU.subtract).then_inc(ready, 1)
                dve.wait_ge(ready, 2 if w is wh0 else 3)

            def split(h, parts, rest, n, tanh, lead, left, done, first=False):
                dve.wait_ge(lead, n + 1)
                dve.wait_ge(tanh, n + 1)
                nc.vector.tensor_tensor(parts[:, 1], h, parts[:, 0], ALU.subtract).then_inc(done, 1)
                if not first:
                    dve.wait_ge(done, 2 * n)
                nc.vector.tensor_tensor(rest[:], h, parts[:, 0], ALU.subtract).then_inc(left, 1)
                dve.wait_ge(left, n + 1)
                nc.vector.tensor_tensor(parts[:, 2], rest[:], parts[:, 1], ALU.subtract).then_inc(done, 1)

            def turn(c, buf, has0=True, has1=True, start0=False, start1=False):
                for t in range(S):
                    if has0:
                        split(h0[:, buf, :, t], a0[:, (S * buf + t) % 2], rest0, S * c + t, tanh0, lead0,
                              left0, split0, start0 and t == 0)
                    if has1:
                        n = S * (c - 1) + t
                        split(h1[:, :, :, bass.ds(n, 1)].rearrange("p m b o -> p m (b o)"),
                              a1[:, (S * (1 - buf) + t) % 2], rest1, n, tanh1, lead1, left1, split1,
                              start1 and t == 0)

            turn(0, 0, has1=False, start0=True)
            turn(1, 1, start1=True)
            with dve.Fori(1, CHUNKS // 2) as i:
                turn(2 * i, 0)
                turn(2 * i + 1, 1)
            turn(CHUNKS, 0, has0=False)
            dve.wait_ge(biased, 1)
            for q in range(4):
                dve.wait_ge(out_ready, q + 1)
                part = g.h[:, 8 * q:8 * q + 8, :]
                nc.vector.tensor_tensor(part, part, final[:, q, :].rearrange("p (j c) -> p j c", j=8), ALU.add)

        @block.gpsimd
        def _(pool):
            pool.wait_ge(loads, 16 * 10)
            st = Steps(pool, steps_p)
            st.then(nc.gpsimd.tensor_tensor(bi1[:], bi1[:], more1[:], ALU.add))
            split_bias(nc, pool, st, pick, bi1, bi1_rest, bi1_mid, bi1_parts, bias_ready)
            pool.wait_ge(bias_ready, 1)
            nc.gpsimd.tensor_tensor(g.h[:], g.h[:], bc(fc_b[:].unsqueeze(1), [TP, NT, C]), ALU.add).then_inc(biased, 1)

        @block.tensor
        def _(pe):
            def columns(bank, m, t=None):
                cols = bank[:, S * B * m:S * B * m + S * B]
                return cols if t is None else cols[:, B * t:B * t + B]

            def input0(c, buf):
                for m in range(KC):
                    ins = nc.tensor.matmul(columns(sum0[:, buf], m), wi0[:, P * m:P * m + P], x[:, bass.ds(S * c, S), :],
                                           start=(m == 0), stop=False, skip_group_check=True)
                return ins

            def input1(c, buf):
                pe.wait_ge(tanh0, S * c + S)
                for m in range(KC):
                    nc.tensor.matmul(columns(sum1[:, buf], m), bi1_parts[:, P * m:P * m + P], pick[:], start=(m == 0),
                                     stop=False, skip_group_check=True)
                    for k in range(KC):
                        ins = nc.tensor.matmul(columns(sum1[:, buf], m), wi1[:, k, P * m:P * m + P],
                                               h0[:, buf, k].rearrange("p s b -> p (s b)"), start=False, stop=False,
                                               skip_group_check=True)
                return ins

            def step(bank, w, t, parts, n, lead, tanh, split):
                pe.wait_ge(lead, n)
                pe.wait_ge(tanh, n)
                for part in range(PARTS):
                    if part:
                        pe.wait_ge(split, 2 * n - 2 + part)
                    for m in range(KC):
                        for k in range(KC):
                            for w_part in range(PARTS - part):
                                ins = nc.tensor.matmul(columns(bank, m, t), w[:, w_part, k, P * m:P * m + P],
                                                       parts[:, part, k], start=False, stop=(part == PARTS - 1),
                                                       skip_group_check=True)
                return ins

            def turn(c, buf, has0=True, has1=True, start0=False, start1=False, more=True):
                for t in range(S):
                    if has0 and not (start0 and t == 0):
                        step(sum0[:, buf], w0, t, a0[:, (S * buf + t + 1) % 2], S * c + t, lead0, tanh0,
                             split0).then_inc(summed0, 1)
                    if has1:
                        if t == 0:
                            ins = input1(c - 1, 1 - buf)
                            if start1:
                                ins.then_inc(summed1, 1)
                        if not (start1 and t == 0):
                            step(sum1[:, 1 - buf], w1, t, a1[:, (S * (1 - buf) + t + 1) % 2], S * (c - 1) + t,
                                 lead1, tanh1, split1).then_inc(summed1, 1)
                    if t == S // 2 and has0 and more:
                        input0(c + 1, 1 - buf)

            pe.wait_ge(ready, 3)
            pe.wait_ge(bias_ready, 1)
            input0(0, 0).then_inc(summed0, 1)
            turn(0, 0, has1=False, start0=True)
            turn(1, 1, start1=True)
            with pe.Fori(1, CHUNKS // 2 - 1) as i:
                turn(2 * i, 0)
                turn(2 * i + 1, 1)
            turn(CHUNKS - 2, 0)
            turn(CHUNKS - 1, 1, more=False)
            turn(CHUNKS, 0, has0=False)
            pe.wait_ge(tanh1, T)
            for j in range(NT):
                out = final[:, j // 8, C * (j % 8):C * (j % 8) + C]
                for k in range(KC):
                    ins = nc.tensor.matmul(out, h1[:, k, j // 2, TP * (j % 2):TP * (j % 2) + TP], fc[:, k],
                                           start=(k == 0), stop=(k == KC - 1))
                if j % 8 == 7:
                    ins.then_inc(out_ready, 1)

        @block.scalar
        def _(act):
            def turn(c, buf, has0=True, has1=True):
                for t in range(S):
                    cols = slice(B * t, B * t + B)
                    if has0:
                        act.wait_ge(summed0, S * c + t + 1)
                        total = sum0[:, buf, 0:KC * S * B].rearrange("p (m n) -> p m n", m=KC)[:, :, cols]
                        nc.scalar.activation(a0[:, (S * buf + t) % 2, 0], total, ACT.Tanh).then_inc(lead0, 1)
                        nc.scalar.activation(h0[:, buf, :, t], total, ACT.Tanh).then_inc(tanh0, 1)
                    if has1:
                        act.wait_ge(summed1, S * (c - 1) + t + 1)
                        total = sum1[:, 1 - buf, 0:KC * S * B].rearrange("p (m n) -> p m n", m=KC)[:, :, cols]
                        nc.scalar.activation(a1[:, (S * (1 - buf) + t) % 2, 0], total, ACT.Tanh).then_inc(lead1, 1)
                        nc.scalar.activation(h1[:, :, :, bass.ds(S * (c - 1) + t, 1)]
                                             .rearrange("p m b o -> p m (b o)"), total, ACT.Tanh).then_inc(tanh1, 1)

            turn(0, 0, has1=False)
            turn(1, 1)
            with act.Fori(1, CHUNKS // 2) as i:
                turn(2 * i, 0)
                turn(2 * i + 1, 1)
            turn(CHUNKS, 0, has0=False)


def experts(nc, g, A):
    E, HID = 8, 128
    with Stage(nc, "ex") as s:
        w1, b1, w2 = s.sb("w1", [P, E * HID]), s.sb("b1", [P, E]), s.sb("w2", [HID, E, C])
        wg, more, b2 = s.sb("wg", [C + 1, E]), s.sb("more", [C + 1, E]), s.sb("b2", [96, E * C])
        loads = s.sem("loads")

        def fetch(sp):
            for dst, name in ((wg[0:C, :], "Wg"), (wg[C:C + 1, :], "bg"), (more[C:C + 1, :], "bias"),
                              (w1[0:C, :], "W1"), (w1[C:P, :], "W1"), (b1[:], "b1"), (w2[:], "W2")):
                sp.dma_start(dst, A["L2_ffn_" + name]).then_inc(loads, 16)
            sp.dma_start(b2[:], A["L2_ffn_b2"].to_broadcast([96, E * C])).then_inc(loads, 16)

        normalise(nc, g, "exn", fetch=fetch)
        gate = s.sb("gate", [TP, NT, E])
        route(nc, g, "er", loads, 8, wg, more, gate, E)
        run_experts(nc, g, "ee", gate, w1, b1, w2, b2, E, 1, ACT.Relu)


def sigmoid_attention(nc, g, A):
    HEADS, F = 8, C
    SCALE = float(F) ** 0.5
    LO, HI = slice(0, C), slice(C, P)
    with Stage(nc, "sa") as s:
        wqT, wvT = (s.sb(n, [F, HEADS, 2, C]) for n in ("wqT", "wvT"))
        wkT, wo = s.sb("wkT", [F, HEADS, C]), s.sb("wo", [F, HEADS, C])
        loads = s.sem("loads")

        def fetch(sp):
            for dst, name in ((wqT[:, :, 0], "Wq"), (wqT[:, :, 1], "Wq"), (wvT[:, :, 0], "Wv"), (wvT[:, :, 1], "Wv"),
                              (wkT[:], "Wk"), (wo[:], "Wo")):
                sp.dma_start(dst, A["L3_attn_" + name]).then_inc(loads, 16)

        normalise(nc, g, "san", fetch=fetch)
        w_rest = s.sb("w_rest", [C, HEADS * C])
        wq11, wq22, wq31 = (s.sb(n, [P, HEADS, 2, C], BF16) for n in ("wq11", "wq22", "wq31"))
        wv11, wv22, wv31 = (s.sb(n, [P, HEADS * C], BF16) for n in ("wv11", "wv22", "wv31"))
        x12, x13 = s.sb("x12", [P, N], BF16), s.sb("x13", [P, N], BF16)
        x_rest, q_rest = s.sb("x_rest", [P, GC]), s.sb("q_rest", [C, T])
        q11, q22, q31 = (s.sb(n, [P, 2, T], BF16) for n in ("q11", "q22", "q31"))
        v, probs = s.sb("v", [TP, 2, 2, HEADS * C]), s.sb("probs", [TP, 2, 2, T])
        v_banks, q_banks = s.ps("v_banks", [TP, 2, BANK]), s.ps("q_banks", [P, 2, BANK])
        score, out = s.ps("score", [TP, 2, BANK]), s.ps("out", [TP, BANK])
        folded, folded_out, steps_w = s.sem("folded"), s.sem("folded_out"), s.sem("steps_w")
        led, left, split, held = s.sem("led"), s.sem("left"), s.sem("split"), s.sem("held")
        q_done, q_led, q_left, q_split = s.sem("q_done"), s.sem("q_led"), s.sem("q_left"), s.sem("q_split")
        v_done, v_ready, scored, squashed = s.sem("v_done"), s.sem("v_ready"), s.sem("scored"), s.sem("squashed")
        weighted, added = s.sem("weighted"), s.sem("added")
        block = s.block()

        @block.tensor
        def _(pe):
            pe.wait_ge(loads, 16 * 6)
            for n, (a, b) in enumerate(((wqT, wkT), (wvT, wo))):
                for head in range(HEADS):
                    ins = nc.tensor.matmul(q_banks[:, n, C * head:C * head + C],
                                           a[:, head].rearrange("f e c -> f (e c)"), b[:, head], start=True, stop=True)
                ins.then_inc(folded, 1)

            def project_v(b):
                pe.wait_ge(v_ready, b + 1)
                for half in range(2):
                    for i, (w, x) in enumerate(((wv11, x12), (wv22, x12), (wv31, x13))):
                        ins = nc.tensor.matmul(v_banks[:, half, :], x[:, bass.ds(T * b + TP * half, TP)], w[:],
                                               start=(i == 0), stop=(i == 2))
                ins.then_inc(v_done, 1)

            def project_q(b, head):
                for i, (w, x) in enumerate(((wq11, x12), (wq22, x12), (wq31, x13))):
                    ins = nc.tensor.matmul(q_banks[:, head % 2, 0:T], w[:, head].rearrange("c e o -> c (e o)"),
                                           x[:, bass.ds(T * b, T)], start=(i == 0), stop=(i == 2))
                ins.then_inc(q_done, 1)

            def scores(b, head):
                u = HEADS * b + head
                pe.wait_ge(q_split, 3 * u + 3)
                pe.wait_ge(squashed, u + 1)
                for half in range(2):
                    for i, (q, x) in enumerate(((q11, x12), (q22, x12), (q31, x13))):
                        ins = nc.tensor.matmul(score[:, head % 2, T * half:T * half + T],
                                               x[:, bass.ds(T * b + TP * half, TP)], q[:, head % 2, :],
                                               start=(i == 0), stop=(i == 2))
                ins.then_inc(scored, 1)

            def weigh(b, buf, head):
                if head == 0:
                    pe.wait_ge(v_ready, b + 2)
                    pe.wait_ge(added, b + 1)
                pe.wait_ge(squashed, HEADS * b + head + 3)
                for tile in range(2):
                    for u in range(2):
                        ins = nc.tensor.matmul(out[:, C * tile:C * tile + C],
                                               probs[:, head % 2, u, TP * tile:TP * tile + TP],
                                               v[:, buf, u, C * head:C * head + C],
                                               start=(head == 0 and tile == 0 and u == 0),
                                               stop=(head == HEADS - 1 and u == 1), skip_group_check=True)
                ins.then_inc(weighted, 1)

            def turn(i, first=False, last=False):
                for e in range(2):
                    b = 2 * i + e
                    for head in range(HEADS):
                        scores(b, head)
                        if e == 1 and head == 2 and not last:
                            pe.wait_ge(split, 3 * i + 6)
                        if head < HEADS - 2:
                            project_q(b, head + 2)
                        elif not (last and e == 1):
                            project_q(b + 1, head + 2 - HEADS)
                        if head == 2 and not (last and e == 1):
                            project_v(b + 1)
                        if head:
                            weigh(b, e, head - 1)
                        elif not (first and e == 0):
                            weigh(b - 1, 1 - e, HEADS - 1)

            pe.wait_ge(folded_out, 2)
            pe.wait_ge(split, 3)
            project_q(0, 0)
            project_q(0, 1)
            project_v(0)
            turn(0, first=True)
            with pe.Fori(1, B // 2 - 1) as i:
                turn(i)
            turn(B // 2 - 1, last=True)
            weigh(B - 1, 1, HEADS - 1)

        @block.gpsimd
        def _(pool):
            split_tokens(g, nc.gpsimd, 0, x12, x13, x_rest, led, left, split, first=True)
            with pool.Fori(1, NG) as n:
                split_tokens(g, nc.gpsimd, n, x12, x13, x_rest, led, left, split, held=held)

        @block.scalar
        def _(act):
            act.sem_inc(squashed, 2)

            def lead(b, head):
                act.wait_ge(q_done, HEADS * b + head + 1)
                nc.scalar.copy(q11[:, head % 2], q_banks[:, head % 2, 0:T]).then_inc(q_led, 1)

            def squash(b, head):
                act.wait_ge(scored, HEADS * b + head + 1)
                act.wait_ge(weighted, HEADS * b + head + 1)
                nc.scalar.activation(probs[:, head % 2].rearrange("p u t -> p (u t)"), score[:, head % 2, 0:2 * T],
                                     ACT.Sigmoid, scale=SCALE).then_inc(squashed, 1)

            def sequence(b, last=False):
                for head in range(HEADS):
                    squash(b, head)
                    if head < HEADS - 2:
                        lead(b, head + 2)
                    elif not last:
                        lead(b + 1, head + 2 - HEADS)

            lead(0, 0)
            lead(0, 1)
            with act.Fori(0, B // 2 - 1) as i:
                for e in range(2):
                    sequence(2 * i + e)
            sequence(B - 2)
            sequence(B - 1, last=True)

        @block.vector
        def _(dve):
            st = Steps(dve, steps_w)
            for n, (w11, w22, w31) in enumerate(((wq11[:, :, 0], wq22[:, :, 0], wq31[:, :, 0]), (wv11, wv22, wv31))):
                dve.wait_ge(folded, n + 1)
                if n == 0:
                    shape = "p (h c) -> p h c"
                    bank, rest = q_banks[:, 0, :].rearrange(shape, c=C), w_rest[:].rearrange(shape, c=C)
                else:
                    bank, rest = q_banks[:, 1, :], w_rest
                st.then(nc.vector.tensor_copy(w11[:], bank))
                st.done(nc.vector.tensor_tensor(w22[:], bank, w11[:], ALU.subtract))
                st.done(nc.vector.tensor_tensor(rest[:], bank[LO], w11[LO], ALU.subtract))
                st.then(nc.vector.tensor_copy(w31[HI], w11[HI]))
                st.then(nc.vector.tensor_tensor(w31[LO], rest[:], w22[LO], ALU.subtract))
                if n == 0:
                    for w in (wq11, wq22, wq31):
                        st.then(nc.vector.tensor_copy(w[:, :, 1], w[:, :, 0]))
                dve.sem_inc(folded_out, 1)
            dve.sem_inc(v_ready, 1)
            dve.sem_inc(added, 1)
            dve.sem_inc(weighted, 2)

            def split_q(b, head, first=False):
                u, buf = HEADS * b + head, head % 2
                q = q_banks[:, buf, 0:T]
                dve.wait_ge(q_led, u + 1)
                if not first:
                    dve.wait_ge(q_split, 3 * u)
                nc.vector.tensor_tensor(q_rest[:], q[LO], q11[LO, buf], ALU.subtract).then_inc(q_left, 1)
                nc.vector.tensor_tensor(q22[:, buf], q, q11[:, buf], ALU.subtract).then_inc(q_split, 1)
                nc.vector.tensor_copy(q31[HI, buf], q11[HI, buf]).then_inc(q_split, 1)
                dve.wait_ge(q_left, u + 1)
                dve.wait_ge(q_split, 3 * u + 2)
                nc.vector.tensor_tensor(q31[LO, buf], q_rest[:], q22[LO, buf], ALU.subtract).then_inc(q_split, 1)

            def take_v(b, buf):
                dve.wait_ge(v_done, b + 1)
                nc.vector.tensor_copy(v[:, buf], v_banks[:]).then_inc(v_ready, 1)

            def add(b):
                dve.wait_ge(weighted, HEADS * b + HEADS + 2)
                part = g.h[:, bass.ds(2 * b, 2), :]
                nc.vector.scalar_tensor_tensor(out=part, in0=out[:, 0:2 * C].rearrange("p (j c) -> p j c", j=2),
                                               scalar=0.0, in1=part, op0=ALU.max, op1=ALU.add).then_inc(added, 1)

            def turn(i, first=False, last=False):
                for e in range(2):
                    b = 2 * i + e
                    for head in range(HEADS):
                        if head < HEADS - 2:
                            split_q(b, head + 2)
                        elif not (last and e == 1):
                            split_q(b + 1, head + 2 - HEADS)
                        if head == 1 and not (first and e == 0):
                            add(b - 1)
                        if head == 3 and not (last and e == 1):
                            take_v(b + 1, 1 - e)

            split_q(0, 0, first=True)
            split_q(0, 1)
            take_v(0, 0)
            turn(0, first=True)
            with dve.Fori(1, B // 2 - 1) as i:
                turn(i)
            turn(B // 2 - 1, last=True)
            add(B - 1)


def routed_experts(nc, g, A):
    E, HID = 8, 256
    with Stage(nc, "re") as s:
        w1, w2 = s.sb("w1", [P, E * HID]), s.sb("w2", [P, 2 * E, C])
        b1, b2 = s.sb("b1", [P, 2 * E]), s.sb("b2", [96, E * C])
        wg = s.sb("wg", [C + 1, E])
        plain, given = s.sb("plain", [P, E, HID]), s.sb("given", [P, 2 * E])
        gain, shift = s.sb("gain", [P, E]), s.sb("shift", [C, E])
        xn = s.sb("xn", [TP, NT, C])
        gate = s.sb("gate", [TP, NT, E])
        loads = s.sem("loads")

        def fetch(sp):
            for dst, name in ((wg[0:C, :], "Wr"), (wg[C:C + 1, :], "br"), (plain[0:C], "W1"), (plain[C:P], "W1"),
                              (gain[0:C, :], "ln_g"), (gain[C:P, :], "ln_g"), (shift[:], "ln_b"), (given[:], "b1"),
                              (w2[:], "W2")):
                sp.dma_start(dst, A["L3_ffn_" + name]).then_inc(loads, 16)
            sp.dma_start(b2[:], A["L3_ffn_b2"].to_broadcast([96, E * C])).then_inc(loads, 16)

        normalise(nc, g, "rn", kept=xn, fetch=fetch)
        route(nc, g, "rr", loads, 10, wg, None, gate, E)
        normalise(nc, g, "rm", src=xn)
        with Stage(nc, "rf") as f:
            bias = f.ps("bias", [P, 2 * E])
            shifted = f.sem("shifted")
            block = f.block()

            @block.tensor
            def _(pe):
                for k in range(2 * E):
                    ins = nc.tensor.matmul(bias[:, k:k + 1], plain[0:C, k // 2, P * (k % 2):P * (k % 2) + P],
                                           shift[:, k // 2:k // 2 + 1], start=True, stop=True)
                ins.then_inc(shifted, 1)

            @block.vector
            def _(dve):
                for e in range(E):
                    nc.vector.tensor_scalar(w1[:, HID * e:HID * e + HID], plain[:, e], gain[:, e:e + 1], None, ALU.mult)
                dve.wait_ge(shifted, 1)
                nc.vector.tensor_tensor(b1[:], bias[:], given[:], ALU.add)

        run_experts(nc, g, "ru", gate, w1, b1, w2, b2, E, 2, ACT.Gelu)


def constants(nc, g, A):
    with Stage(nc, "co") as s:
        cleared, filled = s.sem("cleared"), s.sem("filled")
        block = s.block()

        @block.gpsimd
        def _(pool):
            nc.gpsimd.memset(g.ident[:], 0.0).then_inc(cleared, 1)
            pool.wait_ge(cleared, 1)
            nc.gpsimd.affine_select(out=g.ident[:], in_=g.ident[:], compare_op=ALU.not_equal, fill=1.0,
                                    base=0, pattern=[[-1, P]], channel_multiplier=1)

        @block.vector
        def _(dve):
            nc.vector.memset(g.xT[C:C + 1, :], 1.0)


def store(nc, g, out):
    with Stage(nc, "st") as s:
        stored = s.sem("stored")
        block = s.block()

        @block.sync
        def _(sp):
            sp.dma_start(out.rearrange("b (t p) c -> p (b t) c", p=TP), g.h[:]).then_inc(stored, 16)
            sp.wait_ge(stored, 16)


class Held:

    def __init__(self, nc, ctx):
        self.h = ctx.enter_context(nc.sbuf_tensor("h", [TP, NT, C], F32))
        self.xT = ctx.enter_context(nc.sbuf_tensor("xT", [C + 1, N], F32))
        self.src_table = nc.dram_tensor("src_table", (N, 20), F32).ap()
        self.dst_table = nc.dram_tensor("dst_table", (NT * P, 8), F32).ap()
        self.ident = ctx.enter_context(nc.sbuf_tensor("ident", [P, P], F32))


def layouts(I):
    import numpy as np
    x = np.asarray(I["x"])
    out = {k: np.asarray(v) for k, v in I.items() if k != "x"}
    out["xT"] = x.reshape(2, B // 2, T_IN, C).transpose(0, 3, 1, 2).reshape(P, B // 2, T_IN)
    for k in ("L0_attn_in_proj_w", "L0_attn_x_proj_w", "L0_attn_x_proj_w_b", "L0_attn_dt_proj_w",
              "L0_attn_dt_proj_w_b", "L0_attn_out_proj_w"):
        out[k] = np.ascontiguousarray(out[k].T)
    for k in ("Wq", "Wk", "Wv"):
        out["L3_attn_" + k] = out["L3_attn_" + k].reshape(C, C, 8).transpose(1, 2, 0)
    out["L3_attn_Wo"] = out["L3_attn_Wo"].reshape(C, 8, C)
    for k in ("L0_ffn", "L2_ffn", "L3_ffn"):
        e, _, hid = out[k + "_W1"].shape
        out[k + "_W1"] = out[k + "_W1"].transpose(1, 0, 2).reshape(C, e * hid)
        out[k + "_W2"] = out[k + "_W2"].reshape(e * hid // P, P, C).transpose(1, 0, 2)
        out[k + "_b1"] = out[k + "_b1"].reshape(e * hid // P, P).T
        out[k + "_b2"] = out[k + "_b2"].reshape(1, e * C)
    out["L3_ffn_W1"] = out["L3_ffn_W1"].reshape(C, 8, 256)
    out["L3_ffn_ln_g"], out["L3_ffn_ln_b"] = out["L3_ffn_ln_g"].T, out["L3_ffn_ln_b"].T
    for k in ("W_ih_0", "W_hh_0", "W_ih_1", "W_hh_1", "fc_w"):
        w = out["L2_attn_" + k].T
        out["L2_attn_" + k] = w if k == "W_ih_0" else w.reshape(2, P, w.shape[1]).transpose(1, 0, 2)
    for k in ("b_ih_0", "b_hh_0", "b_ih_1", "b_hh_1", "fc_b"):
        out["L2_attn_" + k] = out["L2_attn_" + k].reshape(1, -1)
    fold = np.zeros((16, 24), np.float32)
    fold[:, 0:16] = np.eye(16, dtype=np.float32)
    for head in range(4):
        fold[4 * head:4 * head + 4, 16 + head] = out["L0_ffn_att_src"][head]
        fold[4 * head:4 * head + 4, 20 + head] = out["L0_ffn_att_dst"][head]
    out["fold"] = fold
    out["L1_ffn_Wq_pk"] = out["L1_ffn_Wq_pk"].reshape(C, 16, 32).transpose(2, 1, 0)
    out["L1_ffn_pk_keys"] = out["L1_ffn_pk_keys"].transpose(3, 0, 2, 1).reshape(32, 16, 64)
    out["L1_ffn_Wo"] = out["L1_ffn_Wo"].reshape(8, C, C).transpose(1, 0, 2)
    out["memory"] = np.concatenate([out.pop("L1_ffn_keys_table"), out.pop("L1_ffn_values_table")], axis=1)
    after = np.zeros(TP, np.float32)
    out["time_curve"] = np.concatenate([out["L1_attn_time_w"], after])
    out["time_steps"] = np.concatenate([np.ones(2 * TP, np.float32), after])
    return out


def recycle(nc, start):
    nc.clear_and_free_semaphores(nc.allocated_since(start))
    nc.all_engine_barrier()


def audio_tower(nc, A, out):
    with ExitStack() as ctx:
        g = Held(nc, ctx)
        start = nc.snapshot_sems()
        constants(nc, g, A)
        pool_windows(nc, g, A)
        stages = (mamba, graph_experts, rwkv, memory_attention, rnn, experts, sigmoid_attention)
        for n, stage in enumerate(stages):
            stage(nc, g, A)
            if n % 2:
                recycle(nc, start)
        recycle(nc, start)
        routed_experts(nc, g, A)
        store(nc, g, out)


def kernel(**inputs):
    import numpy as np
    import concourse.bacc as bacc
    from concourse.bass_utils import run_bass_kernel_spmd

    nc = bacc.Bacc("TRN2", target_bir_lowering=False, num_devices=1)
    arrays, A = {}, {}
    for name, a in layouts(inputs).items():
        a = np.ascontiguousarray(a)
        arrays[f"in_{name}"] = a
        A[name] = nc.dram_tensor(f"in_{name}", a.shape, mybir.dt.from_np(a.dtype), kind="ExternalInput").ap()
    out = nc.dram_tensor("out", (B, T, C), F32, kind="ExternalOutput").ap()
    audio_tower(nc, A, out)
    return run_bass_kernel_spmd(nc, [arrays], core_ids=[0]).results[0]["out"]
```
